# Optimizing a Trainium2 kernel written in Bass

```python
import numpy as np
import jax
import jax.numpy as jnp

def _softmax(x, axis=-1):
    return jax.nn.softmax(x, axis=axis)

def _gelu(x):
    return jax.nn.gelu(x, approximate=True)

def _silu(x):
    return jax.nn.silu(x)

def _sigmoid(x):
    return jax.nn.sigmoid(x)

def _layernorm(x, axis=-1, eps=1e-05):
    m = jnp.mean(x, axis=axis, keepdims=True)
    v = jnp.var(x, axis=axis, keepdims=True)
    return (x - m) / jnp.sqrt(v + eps)

def _scatter_add(tgt, idx, src, axis=0):
    return tgt.at[idx].add(src)

def _segment_sum(src, seg, n):
    return jax.ops.segment_sum(src, seg, n)
kernel_name = 'mk_decoder_preln_d2_seqx_r4_6285e4'

def setup_inputs(seed: int=0):
    np.random.seed(seed)
    _w = jnp.asarray

    def _rec_inputs():
        import jax
        import jax.numpy as jnp
        _rk = jax.random.key(seed)
        x = -0.0002928 + 1 * jax.random.normal(jax.random.fold_in(_rk, 1), (2, 512, 256), jnp.float32)
        _lenS = 512 - jax.random.randint(jax.random.fold_in(_rk, 7), (2,), 0, max(1, 512 // 4) + 1, jnp.int32)
        _lenS2 = 1024 - jax.random.randint(jax.random.fold_in(_rk, 8), (2,), 0, max(1, 1024 // 4) + 1, jnp.int32)
        _ctx_512P = jax.random.normal(jax.random.fold_in(_rk, 11), (2, 16, 128), jnp.float32)
        _ctx_512c = jax.random.dirichlet(jax.random.fold_in(_rk, 511), 0.3 * jnp.ones((16,), jnp.float32), (2, 1024))
        _ctx_512t = jnp.einsum('bsk,bkd->bsd', _ctx_512c, _ctx_512P)
        _ctx_512t = _ctx_512t * jax.lax.rsqrt(jnp.mean(jnp.square(_ctx_512t)) + 1e-12) * 0.953939
        ctx_512 = 0.00222621 + 0.99962 * (_ctx_512t + 0.3 * jax.random.normal(jax.random.fold_in(_rk, 611), (2, 1024, 128), jnp.float32))
        return (x, ctx_512)
    x, ctx_512 = _rec_inputs()

    def _L0_attn_setup():
        import jax, jax.numpy as jnp
        import numpy as np
        B, N, D, H, DH, M = (4, 1024, 256, 16, 64, 64)
        EPS = 0.0001

        def softmax_kernel(data, P, is_query):
            dn = data.shape[-1] ** (-0.25)
            ratio = P.shape[0] ** (-0.5)
            dd = jnp.einsum('bhnd,md->bhnm', dn * data, P)
            diag = (jnp.sum(data * data, axis=-1) * 0.5 * dn * dn)[..., None]
            if is_query:
                mx = jnp.max(dd, axis=-1, keepdims=True)
            else:
                mx = jnp.max(dd)
            return ratio * (jnp.exp(dd - diag - mx) + EPS)
        key = jax.random.key(seed)
        ks = jax.random.split(key, 6)
        s = 1.0 / np.sqrt(D).astype(np.float32)
        x = jax.random.normal(ks[0], (B, N, D), jnp.float32)
        Wq = jax.random.normal(ks[1], (D, H * DH), jnp.float32) * s
        Wk = jax.random.normal(ks[2], (D, H * DH), jnp.float32) * s
        Wv = jax.random.normal(ks[3], (D, H * DH), jnp.float32) * s
        Wo = jax.random.normal(ks[4], (H * DH, D), jnp.float32) * s
        bo = jnp.zeros((D,), jnp.float32)
        P = jax.random.normal(ks[5], (M, DH), jnp.float32)
        return {'x': x, 'Wq': Wq, 'Wk': Wk, 'Wv': Wv, 'Wo': Wo, 'bo': bo, 'P': P}
    _L0_attn_all = _L0_attn_setup()
    _L0_attn_in = {k: v for k, v in _L0_attn_all.items() if k in ('Wq', 'Wk', 'Wv', 'Wo', 'bo', 'P')}
    del _L0_attn_all

    def _L0_xattn_setup():
        import jax, jax.numpy as jnp
        import numpy as np
        B, T, TC, C, CC, H = (2, 512, 128, 256, 128, 16)
        D = C // H

        def _heads(t):
            b, l, _ = t.shape
            return t.reshape(b, l, H, D).transpose(0, 2, 1, 3)
        key = jax.random.key(seed)
        ks = jax.random.split(key, 18)
        w = lambda k, i, o: jax.random.normal(k, (i, o), jnp.float32) / np.sqrt(i).astype(np.float32)
        return {'x': jax.random.normal(ks[0], (B, T, C), jnp.float32), 'cross_input': jax.random.normal(ks[1], (B, TC, CC), jnp.float32), 'Wk': w(ks[2], C, C), 'bk': jnp.zeros((C,), jnp.float32), 'Wq': w(ks[3], C, C), 'bq': jnp.zeros((C,), jnp.float32), 'Wv': w(ks[4], C, C), 'bv': jnp.zeros((C,), jnp.float32), 'Wck': w(ks[5], CC, C), 'bck': jnp.zeros((C,), jnp.float32), 'Wcq': w(ks[6], C, C), 'bcq': jnp.zeros((C,), jnp.float32), 'Wcv': w(ks[7], CC, C), 'bcv': jnp.zeros((C,), jnp.float32), 'Wp': w(ks[8], C, C), 'bp': jnp.zeros((C,), jnp.float32)}
    _L0_xattn_all = _L0_xattn_setup()
    _L0_xattn_in = {k: v for k, v in _L0_xattn_all.items() if k in ('Wk', 'bk', 'Wq', 'bq', 'Wv', 'bv', 'Wck', 'bck', 'Wcq', 'bcq', 'Wcv', 'bcv', 'Wp', 'bp')}
    del _L0_xattn_all

    def _L0_ffn_setup():
        import jax, jax.numpy as jnp
        import numpy as np
        import math
        E = 8
        K = 2
        CF = 1.2
        D = 256
        H = 1024
        key = jax.random.key(seed)
        k0, k1, k2, k3 = jax.random.split(key, 4)
        B, T = (8, 512)
        x_btd = jax.random.normal(k0, (B, T, D), jnp.float32)
        Wr = jax.random.normal(k1, (D, E), jnp.float32) / np.sqrt(D)
        br = jnp.zeros((E,), jnp.float32)
        W1 = jax.random.normal(k2, (E, D, H), jnp.float32) / np.sqrt(D)
        b1 = jnp.zeros((E, H), jnp.float32)
        W2 = jax.random.normal(k3, (E, H, D), jnp.float32) / np.sqrt(H)
        b2 = jnp.zeros((E, D), jnp.float32)
        return dict(x_btd=x_btd, Wr=Wr, br=br, W1=W1, b1=b1, W2=W2, b2=b2)
    _L0_ffn_all = _L0_ffn_setup()
    _L0_ffn_in = {k: v for k, v in _L0_ffn_all.items() if k in ('Wr', 'br', 'W1', 'b1', 'W2', 'b2')}
    del _L0_ffn_all

    def _L1_attn_setup():
        import jax, jax.numpy as jnp
        import numpy as np
        LN_EPS = 1e-05

        def _layernorm(x):
            mu = jnp.mean(x, axis=-1, keepdims=True)
            var = jnp.var(x, axis=-1, keepdims=True)
            return (x - mu) * jax.lax.rsqrt(var + LN_EPS)
        key = jax.random.key(seed)
        k1, k2, k3 = jax.random.split(key, 3)
        B, L, D = (2, 1024, 256)
        x = jax.random.normal(k1, (B, L, D), dtype=jnp.float32)
        W_qkv = jax.random.normal(k2, (3 * D, D), dtype=jnp.float32) * 0.02
        W_o = jax.random.normal(k3, (D, D), dtype=jnp.float32) * 0.02
        log_gamma = jnp.zeros((16,), dtype=jnp.float32)
        return {'x': x, 'W_qkv': W_qkv, 'W_o': W_o, 'log_gamma': log_gamma}
    _L1_attn_all = _L1_attn_setup()
    _L1_attn_in = {k: v for k, v in _L1_attn_all.items() if k in ('W_qkv', 'W_o', 'log_gamma')}
    del _L1_attn_all

    def _L1_xattn_setup():
        import jax, jax.numpy as jnp
        import numpy as np
        H, D, C1, C2, S, M, B, W = (16, 32, 256, 128, 512, 128, 2, 4)

        def _ln(x, g, b):
            m = jnp.mean(x, -1, keepdims=True)
            v = jnp.var(x, -1, keepdims=True)
            return (x - m) * jax.lax.rsqrt(v + 1e-05) * g + b

        def _mha(x, y, wq, wk, wv, li1_w, li1_b, lnx_g, lnx_b, lny_g, lny_b, ln3_g, ln3_b, li2_w, li2_b, li3_w, li3_b, causal):
            xn = _ln(x, lnx_g, lnx_b)
            yn = _ln(y, lny_g, lny_b)
            q = jnp.einsum('bsc,hcd->bhsd', xn, wq)
            k = jnp.einsum('btc,hcd->bhtd', yn, wk)
            v = jnp.einsum('btc,hcd->bhtd', yn, wv)
            a = jax.nn.softmax(jnp.einsum('bhsd,bhtd->bhst', q, k) * D ** (-0.5), axis=-1)
            if causal:
                s, t = (a.shape[-2], a.shape[-1])
                mask = (jnp.arange(t)[None, :] > jnp.arange(s)[:, None]).astype(a.dtype)
                a = a * mask
            o = jnp.einsum('bhst,bhtd->bhsd', a, v)
            o = o.transpose(0, 2, 1, 3).reshape(x.shape[0], x.shape[1], H * D)
            x_out = x + o @ li1_w + li1_b
            h = jax.nn.gelu(_ln(x_out, ln3_g, ln3_b) @ li2_w + li2_b, approximate=False)
            return x_out + h @ li3_w + li3_b
        key = jax.random.key(seed)
        ks = iter(jax.random.split(key, 64))

        def w(shape, scale=0.02):
            return jax.random.normal(next(ks), shape, jnp.float32) * scale
        inp = {'xx': jax.random.normal(next(ks), (B, S, C1), jnp.float32), 'ee': jax.random.normal(next(ks), (B, M, C2), jnp.float32), 'ln1_g': jnp.ones(C1, jnp.float32), 'ln1_b': jnp.zeros(C1, jnp.float32), 'ln2_g': jnp.ones(C1, jnp.float32), 'ln2_b': jnp.zeros(C1, jnp.float32)}
        for pfx, cy in (('a1', C1), ('a2', C2)):
            inp[pfx + '_wq'] = w((H, C1, D))
            inp[pfx + '_wk'] = w((H, cy, D))
            inp[pfx + '_wv'] = w((H, cy, D))
            inp[pfx + '_li1_w'] = w((H * D, C1))
            inp[pfx + '_li1_b'] = jnp.zeros(C1, jnp.float32)
            inp[pfx + '_lnx_g'] = jnp.ones(C1, jnp.float32)
            inp[pfx + '_lnx_b'] = jnp.zeros(C1, jnp.float32)
            inp[pfx + '_lny_g'] = jnp.ones(cy, jnp.float32)
            inp[pfx + '_lny_b'] = jnp.zeros(cy, jnp.float32)
            inp[pfx + '_ln3_g'] = jnp.ones(C1, jnp.float32)
            inp[pfx + '_ln3_b'] = jnp.zeros(C1, jnp.float32)
            inp[pfx + '_li2_w'] = w((C1, C1 * W))
            inp[pfx + '_li2_b'] = jnp.zeros(C1 * W, jnp.float32)
            inp[pfx + '_li3_w'] = w((C1 * W, C1))
            inp[pfx + '_li3_b'] = jnp.zeros(C1, jnp.float32)
        inp['training'] = 0
        return inp
    _L1_xattn_all = _L1_xattn_setup()
    _L1_xattn_in = {k: v for k, v in _L1_xattn_all.items() if k in ('ln1_g', 'ln1_b', 'ln2_g', 'ln2_b', 'a1_wq', 'a1_wk', 'a1_wv', 'a1_li1_w', 'a1_li1_b', 'a1_lnx_g', 'a1_lnx_b', 'a1_lny_g', 'a1_lny_b', 'a1_ln3_g', 'a1_ln3_b', 'a1_li2_w', 'a1_li2_b', 'a1_li3_w', 'a1_li3_b', 'a2_wq', 'a2_wk', 'a2_wv', 'a2_li1_w', 'a2_li1_b', 'a2_lnx_g', 'a2_lnx_b', 'a2_lny_g', 'a2_lny_b', 'a2_ln3_g', 'a2_ln3_b', 'a2_li2_w', 'a2_li2_b', 'a2_li3_w', 'a2_li3_b')}
    del _L1_xattn_all

    def _L1_ffn_setup():
        import jax, jax.numpy as jnp
        import numpy as np
        B, S, D = (2, 512, 256)
        E = 4
        H = 4 * D
        key = jax.random.key(seed)
        k_x, k_r, k_wv, k_wp = jax.random.split(key, 4)
        x = jax.random.normal(k_x, (B, S, D), dtype=jnp.float32)
        w_router = jax.random.normal(k_r, (D, E), dtype=jnp.float32) * 0.02
        w_v = jax.random.normal(k_wv, (E, D, 2 * H), dtype=jnp.float32) * 0.02
        w_proj = jax.random.normal(k_wp, (E, H, D), dtype=jnp.float32) * 0.02
        return {'x': x, 'w_router': w_router, 'w_v': w_v, 'w_proj': w_proj}
    _L1_ffn_all = _L1_ffn_setup()
    _L1_ffn_in = {k: v for k, v in _L1_ffn_all.items() if k in ('w_router', 'w_v', 'w_proj')}
    del _L1_ffn_all
    return {'x': x, 'ctx_512': ctx_512, 'L0_attn_Wq': _L0_attn_in['Wq'], 'L0_attn_Wk': _L0_attn_in['Wk'], 'L0_attn_Wv': _L0_attn_in['Wv'], 'L0_attn_Wo': _L0_attn_in['Wo'], 'L0_attn_bo': _L0_attn_in['bo'], 'L0_attn_P': _L0_attn_in['P'], 'L0_xattn_Wk': _L0_xattn_in['Wk'], 'L0_xattn_bk': _L0_xattn_in['bk'], 'L0_xattn_Wq': _L0_xattn_in['Wq'], 'L0_xattn_bq': _L0_xattn_in['bq'], 'L0_xattn_Wv': _L0_xattn_in['Wv'], 'L0_xattn_bv': _L0_xattn_in['bv'], 'L0_xattn_Wck': _L0_xattn_in['Wck'], 'L0_xattn_bck': _L0_xattn_in['bck'], 'L0_xattn_Wcq': _L0_xattn_in['Wcq'], 'L0_xattn_bcq': _L0_xattn_in['bcq'], 'L0_xattn_Wcv': _L0_xattn_in['Wcv'], 'L0_xattn_bcv': _L0_xattn_in['bcv'], 'L0_xattn_Wp': _L0_xattn_in['Wp'], 'L0_xattn_bp': _L0_xattn_in['bp'], 'L0_ffn_Wr': _L0_ffn_in['Wr'], 'L0_ffn_br': _L0_ffn_in['br'], 'L0_ffn_W1': _L0_ffn_in['W1'], 'L0_ffn_b1': _L0_ffn_in['b1'], 'L0_ffn_W2': _L0_ffn_in['W2'], 'L0_ffn_b2': _L0_ffn_in['b2'], 'L1_attn_W_qkv': _L1_attn_in['W_qkv'], 'L1_attn_W_o': _L1_attn_in['W_o'], 'L1_attn_log_gamma': _L1_attn_in['log_gamma'], 'L1_xattn_ln1_g': _L1_xattn_in['ln1_g'], 'L1_xattn_ln1_b': _L1_xattn_in['ln1_b'], 'L1_xattn_ln2_g': _L1_xattn_in['ln2_g'], 'L1_xattn_ln2_b': _L1_xattn_in['ln2_b'], 'L1_xattn_a1_wq': _L1_xattn_in['a1_wq'], 'L1_xattn_a1_wk': _L1_xattn_in['a1_wk'], 'L1_xattn_a1_wv': _L1_xattn_in['a1_wv'], 'L1_xattn_a1_li1_w': _L1_xattn_in['a1_li1_w'], 'L1_xattn_a1_li1_b': _L1_xattn_in['a1_li1_b'], 'L1_xattn_a1_lnx_g': _L1_xattn_in['a1_lnx_g'], 'L1_xattn_a1_lnx_b': _L1_xattn_in['a1_lnx_b'], 'L1_xattn_a1_lny_g': _L1_xattn_in['a1_lny_g'], 'L1_xattn_a1_lny_b': _L1_xattn_in['a1_lny_b'], 'L1_xattn_a1_ln3_g': _L1_xattn_in['a1_ln3_g'], 'L1_xattn_a1_ln3_b': _L1_xattn_in['a1_ln3_b'], 'L1_xattn_a1_li2_w': _L1_xattn_in['a1_li2_w'], 'L1_xattn_a1_li2_b': _L1_xattn_in['a1_li2_b'], 'L1_xattn_a1_li3_w': _L1_xattn_in['a1_li3_w'], 'L1_xattn_a1_li3_b': _L1_xattn_in['a1_li3_b'], 'L1_xattn_a2_wq': _L1_xattn_in['a2_wq'], 'L1_xattn_a2_wk': _L1_xattn_in['a2_wk'], 'L1_xattn_a2_wv': _L1_xattn_in['a2_wv'], 'L1_xattn_a2_li1_w': _L1_xattn_in['a2_li1_w'], 'L1_xattn_a2_li1_b': _L1_xattn_in['a2_li1_b'], 'L1_xattn_a2_lnx_g': _L1_xattn_in['a2_lnx_g'], 'L1_xattn_a2_lnx_b': _L1_xattn_in['a2_lnx_b'], 'L1_xattn_a2_lny_g': _L1_xattn_in['a2_lny_g'], 'L1_xattn_a2_lny_b': _L1_xattn_in['a2_lny_b'], 'L1_xattn_a2_ln3_g': _L1_xattn_in['a2_ln3_g'], 'L1_xattn_a2_ln3_b': _L1_xattn_in['a2_ln3_b'], 'L1_xattn_a2_li2_w': _L1_xattn_in['a2_li2_w'], 'L1_xattn_a2_li2_b': _L1_xattn_in['a2_li2_b'], 'L1_xattn_a2_li3_w': _L1_xattn_in['a2_li3_w'], 'L1_xattn_a2_li3_b': _L1_xattn_in['a2_li3_b'], 'L1_ffn_w_router': _L1_ffn_in['w_router'], 'L1_ffn_w_v': _L1_ffn_in['w_v'], 'L1_ffn_w_proj': _L1_ffn_in['w_proj']}

def reference(x, ctx_512, L0_attn_Wq, L0_attn_Wk, L0_attn_Wv, L0_attn_Wo, L0_attn_bo, L0_attn_P, L0_xattn_Wk, L0_xattn_bk, L0_xattn_Wq, L0_xattn_bq, L0_xattn_Wv, L0_xattn_bv, L0_xattn_Wck, L0_xattn_bck, L0_xattn_Wcq, L0_xattn_bcq, L0_xattn_Wcv, L0_xattn_bcv, L0_xattn_Wp, L0_xattn_bp, L0_ffn_Wr, L0_ffn_br, L0_ffn_W1, L0_ffn_b1, L0_ffn_W2, L0_ffn_b2, L1_attn_W_qkv, L1_attn_W_o, L1_attn_log_gamma, L1_xattn_ln1_g, L1_xattn_ln1_b, L1_xattn_ln2_g, L1_xattn_ln2_b, L1_xattn_a1_wq, L1_xattn_a1_wk, L1_xattn_a1_wv, L1_xattn_a1_li1_w, L1_xattn_a1_li1_b, L1_xattn_a1_lnx_g, L1_xattn_a1_lnx_b, L1_xattn_a1_lny_g, L1_xattn_a1_lny_b, L1_xattn_a1_ln3_g, L1_xattn_a1_ln3_b, L1_xattn_a1_li2_w, L1_xattn_a1_li2_b, L1_xattn_a1_li3_w, L1_xattn_a1_li3_b, L1_xattn_a2_wq, L1_xattn_a2_wk, L1_xattn_a2_wv, L1_xattn_a2_li1_w, L1_xattn_a2_li1_b, L1_xattn_a2_lnx_g, L1_xattn_a2_lnx_b, L1_xattn_a2_lny_g, L1_xattn_a2_lny_b, L1_xattn_a2_ln3_g, L1_xattn_a2_ln3_b, L1_xattn_a2_li2_w, L1_xattn_a2_li2_b, L1_xattn_a2_li3_w, L1_xattn_a2_li3_b, L1_ffn_w_router, L1_ffn_w_v, L1_ffn_w_proj):
    import jax
    import jax.numpy as jnp

    def _L0_attn_ref(x, Wq, Wk, Wv, Wo, bo, P):
        import jax, jax.numpy as jnp
        import numpy as np
        B, N, D, H, DH, M = (4, 1024, 256, 16, 64, 64)
        EPS = 0.0001

        def softmax_kernel(data, P, is_query):
            dn = data.shape[-1] ** (-0.25)
            ratio = P.shape[0] ** (-0.5)
            dd = jnp.einsum('bhnd,md->bhnm', dn * data, P)
            diag = (jnp.sum(data * data, axis=-1) * 0.5 * dn * dn)[..., None]
            if is_query:
                mx = jnp.max(dd, axis=-1, keepdims=True)
            else:
                mx = jnp.max(dd)
            return ratio * (jnp.exp(dd - diag - mx) + EPS)
        b, n, _ = x.shape

        def proj(W):
            return (x @ W).reshape(b, n, H, DH).transpose(0, 2, 1, 3)
        q, k, v = (proj(Wq), proj(Wk), proj(Wv))
        qp = softmax_kernel(q, P, is_query=True)
        kp = softmax_kernel(k, P, is_query=False)
        k_cumsum = kp.sum(axis=-2)
        D_inv = 1.0 / jnp.einsum('bhnm,bhm->bhn', qp, k_cumsum)
        ctx = jnp.einsum('bhnm,bhne->bhme', kp, v)
        out = jnp.einsum('bhme,bhnm,bhn->bhne', ctx, qp, D_inv)
        out = out.transpose(0, 2, 1, 3).reshape(b, n, H * DH)
        return out @ Wo + bo

    def _L0_xattn_ref(x, cross_input, Wk, bk, Wq, bq, Wv, bv, Wck, bck, Wcq, bcq, Wcv, bcv, Wp, bp):
        import jax, jax.numpy as jnp
        import numpy as np
        B, T, TC, C, CC, H = (2, 512, 128, 256, 128, 16)
        D = C // H

        def _heads(t):
            b, l, _ = t.shape
            return t.reshape(b, l, H, D).transpose(0, 2, 1, 3)
        scale = np.float32(1.0 / np.sqrt(D))
        q = _heads(x @ Wq + bq)
        k = _heads(x @ Wk + bk)
        v = _heads(x @ Wv + bv)
        att = jnp.einsum('bhqd,bhkd->bhqk', q, k) * scale
        causal = jnp.tril(jnp.ones((T, T), bool))
        att = jnp.where(causal[None, None], att, -jnp.inf)
        y = jnp.einsum('bhqk,bhkd->bhqd', jax.nn.softmax(att, axis=-1), v)
        qc = _heads(x @ Wcq + bcq)
        kc = _heads(cross_input @ Wck + bck)
        vc = _heads(cross_input @ Wcv + bcv)
        attc = jnp.einsum('bhqd,bhkd->bhqk', qc, kc) * scale
        y = y + jnp.einsum('bhqk,bhkd->bhqd', jax.nn.softmax(attc, axis=-1), vc)
        y = y.transpose(0, 2, 1, 3).reshape(x.shape[0], T, C)
        return y @ Wp + bp

    def _L0_ffn_ref(x_btd, Wr, br, W1, b1, W2, b2):
        import jax, jax.numpy as jnp
        import numpy as np
        import math
        E = 8
        K = 2
        CF = 1.2
        D = 256
        H = 1024
        B, T, Dm = x_btd.shape
        N = B * T
        x = x_btd.reshape(N, Dm)
        cap = int(math.ceil(CF * N / E))
        probs = jax.nn.softmax(x @ Wr + br, axis=-1)
        gates, ids = jax.lax.top_k(probs, K)
        flat_ids = ids.reshape(-1)
        flat_g = gates.reshape(-1)
        M = N * K
        order = jnp.lexsort((-flat_g, flat_ids))
        s_ids = flat_ids[order]
        s_tok = (order // K).astype(jnp.int32)
        s_g = flat_g[order]
        counts = jnp.bincount(flat_ids, length=E)
        starts = jnp.concatenate([jnp.zeros((1,), counts.dtype), jnp.cumsum(counts)[:-1]])
        rank = jnp.arange(M) - starts[s_ids]
        valid = rank < cap
        pos = jnp.where(valid, s_ids * cap + rank, E * cap)
        disp_tok = jnp.zeros((E * cap + 1,), jnp.int32).at[pos].set(s_tok)[:E * cap]
        disp_g = jnp.zeros((E * cap + 1,), x.dtype).at[pos].set(s_g)[:E * cap]
        xg = x[disp_tok].reshape(E, cap, Dm)
        h = jax.nn.silu(jnp.einsum('ecd,edh->ech', xg, W1) + b1[:, None, :])
        out = jnp.einsum('ech,ehd->ecd', h, W2) + b2[:, None, :]
        gated = out * disp_g.reshape(E, cap, 1)
        y = jnp.zeros((N, Dm), x.dtype).at[disp_tok].add(gated.reshape(E * cap, Dm))
        return y.reshape(B, T, Dm)

    def _L1_attn_ref(x, W_qkv, W_o, log_gamma):
        import jax, jax.numpy as jnp
        import numpy as np
        LN_EPS = 1e-05

        def _layernorm(x):
            mu = jnp.mean(x, axis=-1, keepdims=True)
            var = jnp.var(x, axis=-1, keepdims=True)
            return (x - mu) * jax.lax.rsqrt(var + LN_EPS)
        B, L, D = x.shape
        H = log_gamma.shape[0]
        dk = D // H
        qkv = (x @ W_qkv.T).reshape(B, L, 3, H, dk)
        q, k, v = (qkv[:, :, 0], qkv[:, :, 1], qkv[:, :, 2])
        k = _layernorm(k)
        gamma = jax.nn.sigmoid(log_gamma).reshape(1, H, 1, 1)
        qT = jnp.transpose(q, (1, 0, 2, 3))
        kT = jnp.transpose(k, (1, 0, 2, 3))
        vT = jnp.transpose(v, (1, 0, 2, 3))

        def step(S, qkv_t):
            q_t, k_t, v_t = qkv_t
            S = gamma * S + v_t[..., :, None] * k_t[..., None, :]
            y_t = jnp.einsum('bhde,bhe->bhd', S, q_t)
            return (S, y_t)
        S0 = jnp.zeros((B, H, dk, dk), dtype=x.dtype)
        _, ys = jax.lax.scan(step, S0, (qT, kT, vT))
        y = jnp.transpose(ys, (1, 0, 2, 3)).reshape(B, L, D)
        return y @ W_o.T

    def _L1_xattn_ref(xx, ee, ln1_g, ln1_b, ln2_g, ln2_b, a1_wq, a1_wk, a1_wv, a1_li1_w, a1_li1_b, a1_lnx_g, a1_lnx_b, a1_lny_g, a1_lny_b, a1_ln3_g, a1_ln3_b, a1_li2_w, a1_li2_b, a1_li3_w, a1_li3_b, a2_wq, a2_wk, a2_wv, a2_li1_w, a2_li1_b, a2_lnx_g, a2_lnx_b, a2_lny_g, a2_lny_b, a2_ln3_g, a2_ln3_b, a2_li2_w, a2_li2_b, a2_li3_w, a2_li3_b, training):
        import jax, jax.numpy as jnp
        import numpy as np
        H, D, C1, C2, S, M, B, W = (16, 32, 256, 128, 512, 128, 2, 4)

        def _ln(x, g, b):
            m = jnp.mean(x, -1, keepdims=True)
            v = jnp.var(x, -1, keepdims=True)
            return (x - m) * jax.lax.rsqrt(v + 1e-05) * g + b

        def _mha(x, y, wq, wk, wv, li1_w, li1_b, lnx_g, lnx_b, lny_g, lny_b, ln3_g, ln3_b, li2_w, li2_b, li3_w, li3_b, causal):
            xn = _ln(x, lnx_g, lnx_b)
            yn = _ln(y, lny_g, lny_b)
            q = jnp.einsum('bsc,hcd->bhsd', xn, wq)
            k = jnp.einsum('btc,hcd->bhtd', yn, wk)
            v = jnp.einsum('btc,hcd->bhtd', yn, wv)
            a = jax.nn.softmax(jnp.einsum('bhsd,bhtd->bhst', q, k) * D ** (-0.5), axis=-1)
            if causal:
                s, t = (a.shape[-2], a.shape[-1])
                mask = (jnp.arange(t)[None, :] > jnp.arange(s)[:, None]).astype(a.dtype)
                a = a * mask
            o = jnp.einsum('bhst,bhtd->bhsd', a, v)
            o = o.transpose(0, 2, 1, 3).reshape(x.shape[0], x.shape[1], H * D)
            x_out = x + o @ li1_w + li1_b
            h = jax.nn.gelu(_ln(x_out, ln3_g, ln3_b) @ li2_w + li2_b, approximate=False)
            return x_out + h @ li3_w + li3_b
        x = _ln(xx, ln1_g, ln1_b)
        x = x + _mha(x, x, a1_wq, a1_wk, a1_wv, a1_li1_w, a1_li1_b, a1_lnx_g, a1_lnx_b, a1_lny_g, a1_lny_b, a1_ln3_g, a1_ln3_b, a1_li2_w, a1_li2_b, a1_li3_w, a1_li3_b, causal=True)
        x = _ln(x, ln2_g, ln2_b)
        return x + _mha(x, ee, a2_wq, a2_wk, a2_wv, a2_li1_w, a2_li1_b, a2_lnx_g, a2_lnx_b, a2_lny_g, a2_lny_b, a2_ln3_g, a2_ln3_b, a2_li2_w, a2_li2_b, a2_li3_w, a2_li3_b, causal=False)

    def _L1_ffn_ref(x, w_router, w_v, w_proj):
        import jax, jax.numpy as jnp
        import numpy as np
        B, S, D = (2, 512, 256)
        E = 4
        H = 4 * D
        logits = jnp.einsum('bsd,de->bse', x, w_router)
        probs = jax.nn.softmax(logits, axis=-1)
        expert_idx = jnp.argmax(probs, axis=-1)
        gv = jnp.einsum('bsd,edh->ebsh', x, w_v)
        gate_raw, value = jnp.split(gv, 2, axis=-1)
        h = gate_raw * jax.nn.sigmoid(gate_raw) * value
        y = jnp.einsum('ebsh,ehd->ebsd', h, w_proj)
        onehot = jax.nn.one_hot(expert_idx, w_v.shape[0], dtype=x.dtype)
        return jnp.einsum('bse,ebsd->bsd', onehot, y)
    x = x + _L0_attn_ref(_layernorm(x, axis=-1), L0_attn_Wq, L0_attn_Wk, L0_attn_Wv, L0_attn_Wo, L0_attn_bo, L0_attn_P)
    x = x + _L0_xattn_ref(_layernorm(x, axis=-1), ctx_512, L0_xattn_Wk, L0_xattn_bk, L0_xattn_Wq, L0_xattn_bq, L0_xattn_Wv, L0_xattn_bv, L0_xattn_Wck, L0_xattn_bck, L0_xattn_Wcq, L0_xattn_bcq, L0_xattn_Wcv, L0_xattn_bcv, L0_xattn_Wp, L0_xattn_bp)
    x = x + _L0_ffn_ref(_layernorm(x, axis=-1), L0_ffn_Wr, L0_ffn_br, L0_ffn_W1, L0_ffn_b1, L0_ffn_W2, L0_ffn_b2)
    x = x + _L1_attn_ref(_layernorm(x, axis=-1), L1_attn_W_qkv, L1_attn_W_o, L1_attn_log_gamma)
    x = x + _L1_xattn_ref(_layernorm(x, axis=-1), ctx_512, L1_xattn_ln1_g, L1_xattn_ln1_b, L1_xattn_ln2_g, L1_xattn_ln2_b, L1_xattn_a1_wq, L1_xattn_a1_wk, L1_xattn_a1_wv, L1_xattn_a1_li1_w, L1_xattn_a1_li1_b, L1_xattn_a1_lnx_g, L1_xattn_a1_lnx_b, L1_xattn_a1_lny_g, L1_xattn_a1_lny_b, L1_xattn_a1_ln3_g, L1_xattn_a1_ln3_b, L1_xattn_a1_li2_w, L1_xattn_a1_li2_b, L1_xattn_a1_li3_w, L1_xattn_a1_li3_b, L1_xattn_a2_wq, L1_xattn_a2_wk, L1_xattn_a2_wv, L1_xattn_a2_li1_w, L1_xattn_a2_li1_b, L1_xattn_a2_lnx_g, L1_xattn_a2_lnx_b, L1_xattn_a2_lny_g, L1_xattn_a2_lny_b, L1_xattn_a2_ln3_g, L1_xattn_a2_ln3_b, L1_xattn_a2_li2_w, L1_xattn_a2_li2_b, L1_xattn_a2_li3_w, L1_xattn_a2_li3_b, 0)
    x = x + _L1_ffn_ref(_layernorm(x, axis=-1), L1_ffn_w_router, L1_ffn_w_v, L1_ffn_w_proj)
    return x

_drawn_inputs = setup_inputs


def setup_inputs(seed=0):
    import zlib

    import numpy as np

    out = dict(_drawn_inputs(seed))
    spreads = {'L0_attn_bo': (0.0, 0.1),
     'L0_xattn_bk': (0.0, 2.0),
     'L0_xattn_bq': (0.0, 0.366),
     'L0_xattn_bv': (0.0, 0.1),
     'L0_xattn_bck': (0.0, 2.0),
     'L0_xattn_bcq': (0.0, 0.1),
     'L0_xattn_bcv': (0.0, 0.1),
     'L0_xattn_bp': (0.0, 0.1),
     'L0_ffn_br': (0.0, 0.1),
     'L0_ffn_b1': (0.0, 0.395),
     'L0_ffn_b2': (0.0, 0.1),
     'L1_attn_log_gamma': (0.0, 0.8),
     'L1_xattn_ln1_g': (1.0, 0.2),
     'L1_xattn_ln1_b': (0.0, 0.1),
     'L1_xattn_ln2_g': (1.0, 0.2),
     'L1_xattn_ln2_b': (0.0, 0.1),
     'L1_xattn_a1_li1_b': (0.0, 0.287),
     'L1_xattn_a1_lnx_g': (1.0, 0.6),
     'L1_xattn_a1_lnx_b': (0.0, 0.8),
     'L1_xattn_a1_lny_g': (1.0, 0.6),
     'L1_xattn_a1_lny_b': (0.0, 0.8),
     'L1_xattn_a1_ln3_g': (1.0, 0.6),
     'L1_xattn_a1_ln3_b': (0.0, 0.8),
     'L1_xattn_a1_li2_b': (0.0, 0.732),
     'L1_xattn_a1_li3_b': (0.0, 0.27),
     'L1_xattn_a2_li1_b': (0.0, 0.269),
     'L1_xattn_a2_lnx_g': (1.0, 0.6),
     'L1_xattn_a2_lnx_b': (0.0, 0.8),
     'L1_xattn_a2_lny_g': (1.0, 0.6),
     'L1_xattn_a2_lny_b': (0.0, 0.8),
     'L1_xattn_a2_ln3_g': (1.0, 0.6),
     'L1_xattn_a2_ln3_b': (0.0, 0.8),
     'L1_xattn_a2_li2_b': (0.0, 0.724),
     'L1_xattn_a2_li3_b': (0.0, 0.269)}
    factors = {'L0_attn_Wq': 23.472,
     'L0_attn_Wk': 3.653,
     'L1_xattn_a1_wq': 8.0,
     'L1_xattn_a1_wk': 8.0,
     'L1_xattn_a1_wv': 4.714,
     'L1_xattn_a1_li1_w': 4.317,
     'L1_xattn_a2_wq': 8.0,
     'L1_xattn_a2_wk': 8.0,
     'L1_xattn_a2_wv': 3.568,
     'L1_xattn_a2_li1_w': 3.459,
     'L1_ffn_w_router': 6.277,
     'L1_ffn_w_v': 5.512,
     'L1_ffn_w_proj': 5.52,
     'L0_attn_P': 8.0}
    for name, (base, spread) in spreads.items():
        noise = np.random.default_rng([zlib.crc32(name.encode()), seed]).standard_normal(out[name].shape)
        drawn = base * np.exp(spread * noise) if base else spread * noise
        out[name] = jnp.asarray(drawn.astype(out[name].dtype))
    for name, factor in factors.items():
        out[name] = (out[name] * factor).astype(out[name].dtype)
    return out
```

```python
from contextlib import ExitStack

import numpy as np

import concourse.bass as bass
from concourse import mybir

F32 = mybir.dt.float32
BF16 = mybir.dt.bfloat16
U32 = mybir.dt.uint32
ALU = mybir.AluOpType
ACT = mybir.ActivationFunctionType
AX = mybir.AxisListType

P = 128
B, S, D = 2, 512, 256
T = B * S
NC = T // P
SC = S // P
FC = D // P
MEM, CW = 1024, 128
TM = B * MEM
MC = TM // P
H = 16
LN_EPS = 1e-5
PH, PM = 64, 64
PAIRS = H * PH // P
DN = PH ** -0.25
KEPS = 1e-4
E0, HID = 8, 1024
CAP = -(-12 * T // (10 * E0))
E1 = 4
HC = HID // P
NEG = -1e30
BANK = 512


class Lane:

    def __init__(self, name, sem):
        self.name, self.sem, self.count, self.items, self.seen = name, sem, 0, [], {}

    def wait(self, *tickets):
        for t in tickets:
            if t is None:
                continue
            if isinstance(t, list):
                self.wait(*t)
                continue
            sem, value = t
            if self.seen.get(id(sem), 0) < value:
                self.seen[id(sem)] = value
                self.items.append(lambda e, s=sem, v=value: e.wait_ge(s, v))

    def do(self, make, *tickets, tick=True):
        self.wait(*tickets)
        if not tick:
            self.items.append(lambda e: make(e))
            return None
        self.count += 1
        self.items.append(lambda e: make(e).then_inc(self.sem, 1))
        return (self.sem, self.count)

    def last(self):
        return (self.sem, self.count) if self.count else None


class Arrival:

    def __init__(self, sem):
        self.sem, self.count = sem, 0

    def dma(self, lane, out, in_, *tickets):
        lane.wait(*tickets)
        self.count += 16
        lane.items.append(lambda e: e.dma_start(out, in_).then_inc(self.sem, 16))
        return (self.sem, self.count)


class Slot:

    def __init__(self, at):
        self.at, self.free = at, []


class Ring:
    def __init__(self, slots):
        self.slots, self.n = [Slot(s) for s in slots], 0

    def next(self):
        s = self.slots[self.n % len(self.slots)]
        self.n += 1
        return s


class Program:
    def __init__(self, nc, ctx, a, out, stages):
        self.nc, self.ctx, self.a, self.out = nc, ctx, a, out
        self.nsem = 0
        self.pe, self.act, self.dve, self.pool, self.sp = (
            Lane(n, self.sem("s_" + n)) for n in ("pe", "act", "dve", "pool", "sp"))
        self.lanes = [self.pe, self.act, self.dve, self.pool]
        self.arrivals = []
        self.ps = ctx.enter_context(nc.psum_tensor("psum", [P, 8, BANK], F32))
        self.banks = Ring(range(8))
        self.stages = stages
        self.build()

    def sem(self, name):
        self.nsem += 1
        return self.ctx.enter_context(self.nc.semaphore(name))

    def arrival(self, name):
        s = Arrival(self.sem("d_" + name))
        self.arrivals.append(s)
        return s

    def sb(self, name, shape, dt=F32, ctx=None):
        return (ctx or self.ctx).enter_context(self.nc.sbuf_tensor(name, shape, dt))

    def fence(self, *tickets):
        last = [l.last() for l in self.lanes]
        for l in self.lanes + [self.sp]:
            l.wait(*last, *tickets)

    def chain(self, out, terms, *tickets, tick=True):
        self.pe.wait(*tickets)
        for i, (l, r) in enumerate(terms):
            end = i == len(terms) - 1
            t = self.pe.do(lambda e, l=l, r=r, i=i, end=end: e.matmul(out, l, r, start=i == 0, stop=end),
                           tick=tick and end)
        return t

    def V(self, make, *tickets):
        return self.dve.do(make, *tickets)

    def A(self, make, *tickets):
        return self.act.do(make, *tickets)

    def G(self, make, *tickets):
        return self.pool.do(make, self.pool.last(), *tickets)

    def copy(self, lane, out, in_, *tickets):
        if lane is self.act:
            return lane.do(lambda e: e.activation(out, in_, ACT.Copy), *tickets)
        return lane.do(lambda e: e.tensor_copy(out, in_), *tickets)

    def constants(self):
        z = self.sb("ident", [P, P])
        self.ident = z
        t = self.G(lambda e: e.memset(z[:, :], 0.0))
        t = self.G(lambda e: e.affine_select(out=z[:, :], in_=z[:, :], compare_op=ALU.not_equal, fill=1.0, base=0,
                                             pattern=[[-1, P]], channel_multiplier=1), t)
        self.t_ident = t
        self.ones = self.sb("ones", [P, P])
        self.t_ones = self.G(lambda e: e.memset(self.ones[:, :], 1.0))
        self.identb = self.sb("identb", [P, P], BF16)
        t_b = self.G(lambda e: e.tensor_copy(self.identb[:, :], z[:, :]), t)
        mf = self.sb("maskf", [P, 2, P])
        self.mask_qk = self.sb("mask_qk", [P, P], BF16)
        self.mask_kq = self.sb("mask_kq", [P, P], BF16)
        t = self.G(lambda e: e.memset(mf[:, :, :], 0.0))
        t1 = self.G(lambda e: e.affine_select(out=mf[:, 0, :], in_=mf[:, 0, :], compare_op=ALU.is_ge, fill=NEG,
                                              base=0, pattern=[[-1, P]], channel_multiplier=1), t)
        t2 = self.G(lambda e: e.affine_select(out=mf[:, 1, :], in_=mf[:, 1, :], compare_op=ALU.is_ge, fill=NEG,
                                              base=0, pattern=[[1, P]], channel_multiplier=-1), t)
        self.G(lambda e: e.tensor_copy(self.mask_qk[:, :], mf[:, 0, :]), t1)
        self.t_const = self.G(lambda e: e.tensor_copy(self.mask_kq[:, :], mf[:, 1, :]), t2)

    def normalize(self, src, dst, chunks, width, after, name):
        raw, agg, std = self.ln_raw, self.ln_agg, self.ln_std
        self.dve.wait(*self.ln_free)
        for c in range(chunks):
            t = self.V(lambda e, c=c: e.bn_stats(raw[:, c, :], src[:, c, :]), after[c])
        for c in range(chunks):
            t = self.V(lambda e, c=c: e.bn_aggr(agg[:, c, :], raw[:, c, :]), t if c == 0 else None)
        t = self.V(lambda e: e.tensor_scalar(std[:, 0:chunks, 0], agg[:, 0:chunks, 1], LN_EPS, None, ALU.add), t)
        t = self.A(lambda e: e.activation(std[:, 0:chunks, 1], std[:, 0:chunks, 0], ACT.Sqrt), t)
        t = self.V(lambda e: e.reciprocal(std[:, 0:chunks, 0], std[:, 0:chunks, 1]), t)
        done = []
        for c in range(chunks):
            done.append(self.V(lambda e, c=c: e.tensor_scalar(dst[:, c, :], src[:, c, :], agg[:, c, 0:1], std[:, c, 0:1],
                                                              ALU.subtract, ALU.mult), t))
        self.ln_free = [done[-1]]
        return done

    def to_features(self, src, width, chunks, ready, emit):
        out = []
        for n in range(chunks // 4):
            for f in range(width // P):
                bank = self.banks.next()
                self.pe.wait(*bank.free, self.t_ident)
                for k in range(4):
                    c = 4 * n + k
                    t = self.pe.do(lambda e, k=k, c=c, f=f, b=bank.at: e.transpose(
                        self.ps[:, b, k * P:(k + 1) * P], src[:, c, f * P:(f + 1) * P], self.ident[:, :]),
                        ready[c], tick=k == 3)
                t = emit(f, n, self.ps[:, bank.at, :], t)
                bank.free = [t]
                out.append(t)
        return out

    def feature_copy(self, dst):
        def emit(f, n, view, t):
            lane = self.act if (f + n) % 2 == 0 else self.dve
            return self.copy(lane, dst[:, f, n * BANK:(n + 1) * BANK], view, t)
        return emit

    def build(self):
        nc, a = self.nc, self.a
        self.ln_free = []
        self.ln_raw = self.sb("ln_raw", [P, MC, 6])
        self.ln_agg = self.sb("ln_agg", [P, MC, 2])
        self.ln_std = self.sb("ln_std", [P, MC, 2])
        self.split_bufs = {}
        self.constants()
        self.x = self.sb("x", [P, NC, D])
        self.xn = self.sb("xn", [P, NC, D])
        self.xnT = self.sb("xnT", [P, FC, T])
        self.ctxT = self.sb("ctxT", [P, TM])
        d_x = self.arrival("x")
        xin = a["x"].rearrange("b (c p) d -> p (b c) d", p=P)
        d_xs = [self.arrival(f"x{i}") for i in range(2)]
        t_x = [d_xs[i].dma(self.sp, self.x[:, 4 * i:4 * i + 4, :], xin[:, 4 * i:4 * i + 4, :]) for i in range(2)]
        self.x_ready = [t_x[c // 4] for c in range(NC)]
        for s in self.stages:
            STAGE_FUNCTIONS[s](self)
        d_out = self.arrival("out")
        yout = self.out.rearrange("b (c p) d -> p (b c) d", p=P)
        self.t_out = d_out.dma(self.sp, yout, self.x[:, :, :], *self.x_ready)
        self.sp.wait(self.t_out)
        for d in self.arrivals:
            if d.count:
                self.sp.wait((d.sem, d.count))

    def norm_x(self):
        done = self.normalize(self.x, self.xn, NC, D, self.x_ready, f"x{self.nsem}")
        t = self.to_features(self.xn, D, NC, done, self.feature_copy(self.xnT))
        self.xn_ready = done
        self.xnT_ready = t

    def performer(self):
        a, ps = self.a, self.ps
        with ExitStack() as mem:
            sb = lambda n, s, dt=F32: self.sb("pf_" + n, s, dt, mem)
            wq, wk, wv = (sb(n, [P, FC, H * PH]) for n in ("wq", "wk", "wv"))
            wo = sb("wo", [P, PAIRS, D])
            praw = sb("praw", [P, P])
            pbd = sb("pbd", [P, P])
            half = sb("half", [P, 2])
            bo = sb("bo", [P, D])
            kdd = sb("kdd", [P, PAIRS, NC, P])
            diag = sb("diag", [P, 2, PAIRS, NC, 2])
            kmax = sb("kmax", [P, 2 * PAIRS])
            gm = sb("gm", [P, 4])
            grow = sb("grow", [1, P])
            headT = Ring([sb(f"hT{i}", [P, T]) for i in range(2)])
            sq = Ring([sb(f"sq{i}", [P, T]) for i in range(2)])
            qp = Ring([sb(f"qp{i}", [P, NC, P]) for i in range(2)])
            qpT = Ring([sb(f"qpT{i}", [P, T]) for i in range(1)])
            vv = Ring([sb(f"v{i}", [P, NC, P]) for i in range(1)])
            rden = Ring([sb(f"rd{i}", [P, BANK]) for i in range(2)])
            qmx = Ring([sb(f"qmx{i}", [P, NC, 2]) for i in range(2)])
            bd = Ring([sb(f"bd{i}", [P, 2, P]) for i in range(2)])
            loads = {}
            for n, tile, src in (("k", wk, "L0_attn_Wk"), ("q", wq, "L0_attn_Wq"), ("v", wv, "L0_attn_Wv")):
                loads[n] = self.arrival("pf" + n).dma(self.sp, tile[:, :, :], a[src].rearrange("(f p) n -> p f n", p=P))
            t_z = self.G(lambda e: e.memset(praw[:, :], 0.0))
            d_p = self.arrival("pfp")
            for j in range(2):
                t_p = d_p.dma(self.sp, praw[64 * j:64 * j + 64, 64 * j:64 * j + 64], a["L0_attn_P"], t_z)
            t_bo = self.arrival("pfbo").dma(self.sp, bo[:, :], a["L0_attn_bo"].partition_broadcast(P))
            t_wo = self.arrival("pfwo").dma(self.sp, wo[:, :, :], a["L0_attn_Wo"].rearrange("(f p) n -> p f n", p=P))
            t_h = self.G(lambda e: e.memset(half[:, :], 0.0))
            for j in range(2):
                t_h = self.G(lambda e, j=j: e.memset(half[64 * j:64 * j + 64, j:j + 1], 0.5 * DN * DN), t_h)
            for s in bd.slots:
                s.free = [self.G(lambda e, s=s: e.memset(s.at[:, :, :], 0.0))]
            bank = self.banks.next()
            t = self.pe.do(lambda e, b=bank.at: e.transpose(ps[:, b, 0:P], praw[:, :], self.ident[:, :]), t_p, self.t_ident)
            t_pbd = self.copy(self.act, pbd[:, :], ps[:, bank.at, 0:P], t)
            bank.free = [t_pbd]

            self.norm_x()
            t_xb = None
            for c in range(NC):
                t_xb = self.G(lambda e, c=c: e.tensor_tensor(self.x[:, c, :], self.x[:, c, :], bo[:, :], ALU.add),
                              self.xn_ready[-1], t_bo)

            def head_features(w, pair, t_w, which):
                hT, s2 = headT.next(), sq.next()
                t_hT, t_sq = [], []
                for n in range(T // BANK):
                    bank = self.banks.next()
                    t = self.chain(ps[:, bank.at, :], [(w[:, f, pair * P:(pair + 1) * P], self.xnT[:, f, n * BANK:(n + 1) * BANK])
                                                       for f in range(FC)], bank.free, t_w, self.xnT_ready)
                    cols = slice(n * BANK, (n + 1) * BANK)
                    t1 = self.A(lambda e, b=bank.at, cols=cols: e.activation(hT.at[:, cols], ps[:, b, :], ACT.Copy), t, hT.free)
                    t2 = self.A(lambda e, b=bank.at, cols=cols: e.activation(s2.at[:, cols], ps[:, b, :], ACT.Square), t, s2.free)
                    bank.free = [t2]
                    t_hT.append(t1)
                    t_sq.append(t2)
                bank = self.banks.next()
                for c in range(NC):
                    t = self.chain(ps[:, bank.at, 2 * c:2 * c + 2], [(s2.at[:, c * P:(c + 1) * P], half[:, :])],
                                   bank.free, t_sq[c // 4], t_h, tick=c == NC - 1)
                s2.free = [t]
                t_d = self.V(lambda e, b=bank.at: e.tensor_copy(diag[:, which, pair, :, :],
                                                                ps[:, b, 0:2 * NC].rearrange("p (c h) -> p c h", h=2)), t)
                bank.free = [t_d]
                res = []
                for n in range(2):
                    bank = self.banks.next()
                    for k in range(4):
                        c = 4 * n + k
                        t = self.chain(ps[:, bank.at, k * P:(k + 1) * P], [(hT.at[:, c * P:(c + 1) * P], pbd[:, :])],
                                       bank.free, t_hT[n], t_pbd, tick=k == 3)
                    res.append((bank, t))
                hT.free = [t]
                return res, t_d

            t_kd = []
            for pair in range(PAIRS):
                res, t_d = head_features(wk, pair, loads["k"], 1)
                for n, (bank, t) in enumerate(res):
                    t1 = self.V(lambda e, b=bank.at, i=2 * pair + n: e.tensor_reduce(kmax[:, i:i + 1], ps[:, b, :], AX.X, ALU.max), t)
                    t2 = self.A(lambda e, b=bank.at, n=n, pair=pair: e.activation(
                        kdd[:, pair, 4 * n:4 * n + 4, :], ps[:, b, :].rearrange("p (c m) -> p c m", c=4), ACT.Copy), t, t1)
                    bank.free = [t2]
                t_kd.append([t2, t_d])
            t = self.V(lambda e: e.tensor_reduce(gm[:, 0:1], kmax[:, :], AX.X, ALU.max), t1)
            bank = self.banks.next()
            t = self.pe.do(lambda e, b=bank.at: e.transpose(ps[0:1, b, 0:P], gm[:, 0:1], self.ident[:, :]), t, bank.free)
            t = self.V(lambda e, b=bank.at: e.tensor_reduce(gm[0:1, 1:2], ps[0:1, b, 0:P], AX.X, ALU.max), t)
            t = self.chain(ps[:, bank.at, 0:1], [(self.ones[0:1, :], gm[0:1, 1:2])], t, self.t_ones)
            t_gm = self.V(lambda e, b=bank.at: e.tensor_scalar(gm[:, 2:3], ps[:, b, 0:1], DN, None, ALU.mult), t)
            bank.free = [t_gm]

            heads_of = lambda v: v.rearrange("p c (h m) -> p (c h) m", h=2)
            t_y = []
            for pair in range(PAIRS):
                kv = heads_of(kdd[:, pair, :, :])
                kb = diag[:, 1, pair, :, :].rearrange("p c h -> p (c h)")
                t = self.V(lambda e, kb=kb: e.tensor_scalar(kb, kb, gm[:, 2:3], None, ALU.add), t_gm, t_kd[pair])
                t = self.V(lambda e, kv=kv, kb=kb: e.scalar_tensor_tensor(
                    kv, kv, DN, kb.unsqueeze(2).broadcast_to([P, 2 * NC, PM]), ALU.mult, ALU.subtract), t)
                t = self.A(lambda e, pair=pair: e.activation(kdd[:, pair, :, :], kdd[:, pair, :, :], ACT.Exp), t)
                t_kp = self.G(lambda e, pair=pair: e.tensor_scalar(kdd[:, pair, :, :], kdd[:, pair, :, :], KEPS, None, ALU.add), t)
                res, t_d = head_features(wq, pair, loads["q"], 0)
                mx, q = qmx.next(), qp.next()
                t_e = []
                for n, (bank, t) in enumerate(res):
                    view = ps[:, bank.at, :].rearrange("p (c m) -> p c m", m=PM)
                    mview = mx.at[:, 4 * n:4 * n + 4, :].rearrange("p c h -> p (c h)")
                    dview = diag[:, 0, pair, 4 * n:4 * n + 4, :].rearrange("p c h -> p (c h)")
                    t1 = self.V(lambda e, m=mview, v=view: e.tensor_reduce(m, v, AX.X, ALU.max), t, mx.free)
                    t1 = self.V(lambda e, m=mview, d=dview: e.scalar_tensor_tensor(m, m, DN, d, ALU.mult, ALU.add), t1, t_d)
                    qv = heads_of(q.at[:, 4 * n:4 * n + 4, :])
                    t1 = self.V(lambda e, m=mview, v=view, qv=qv: e.scalar_tensor_tensor(
                        qv, v, DN, m.unsqueeze(2).broadcast_to([P, 8, PM]), ALU.mult, ALU.subtract), t1, q.free)
                    bank.free = [t1]
                    t_e.append(t1)
                mx.free = [t1]
                t = self.A(lambda e, q=q: e.activation(q.at[:, :, :], q.at[:, :, :], ACT.Exp), t_e)
                t_qp = self.G(lambda e, q=q: e.tensor_scalar(q.at[:, :, :], q.at[:, :, :], KEPS, None, ALU.add), t)
                v = vv.next()
                t_v = []
                for n in range(2):
                    bank = self.banks.next()
                    for k in range(4):
                        c = 4 * n + k
                        t = self.chain(ps[:, bank.at, k * P:(k + 1) * P],
                                       [(self.xnT[:, f, c * P:(c + 1) * P], wv[:, f, pair * P:(pair + 1) * P]) for f in range(FC)],
                                       bank.free, loads["v"], tick=k == 3)
                    t = self.A(lambda e, v=v, n=n, b=bank.at: e.activation(
                        v.at[:, 4 * n:4 * n + 4, :], ps[:, b, :].rearrange("p (c m) -> p c m", c=4), ACT.Copy), t, v.free)
                    bank.free = [t]
                    t_v.append(t)
                bank = self.banks.next()
                for b in range(B):
                    self.chain(ps[:, bank.at, b * P:(b + 1) * P],
                               [(kdd[:, pair, c, :], v.at[:, c, :]) for c in range(SC * b, SC * b + SC)],
                               bank.free, t_kp, t_v, tick=False)
                    t_c = self.chain(ps[:, bank.at, 256 + b * 64:256 + (b + 1) * 64],
                                     [(kdd[:, pair, c, :], self.ones[:, 0:64]) for c in range(SC * b, SC * b + SC)])
                v.free = [t_c]
                qT = qpT.next()
                t_qT = self.to_features(q.at, P, NC, [t_qp] * NC, lambda f, n, view, t, qT=qT: self.copy(
                    self.act if n else self.dve, qT.at[:, n * BANK:(n + 1) * BANK], view, t, qT.free))
                q.free = list(t_qT)
                yT = kdd[:, pair, :, :].rearrange("p c m -> p (c m)")
                for b in range(B):
                    blk = bd.next()
                    for j in range(2):
                        r = slice(64 * j, 64 * j + 64)
                        self.V(lambda e, r=r, blk=blk, b=b, bk=bank.at: e.tensor_copy(
                            blk.at[r, 0, r], ps[r, bk, b * P + r.start:b * P + r.stop]), t_c, blk.free)
                        t_b = self.V(lambda e, r=r, blk=blk, b=b, bk=bank.at: e.tensor_copy(
                            blk.at[r, 1, r], ps[r, bk, 256 + b * 64:256 + (b + 1) * 64]))
                    num, den = self.banks.next(), self.banks.next()
                    t1 = self.chain(ps[:, num.at, :], [(blk.at[:, 0, :], qT.at[:, b * S:(b + 1) * S])], num.free, t_b, t_qT)
                    t2 = self.chain(ps[:, den.at, :], [(blk.at[:, 1, :], qT.at[:, b * S:(b + 1) * S])], den.free)
                    blk.free = [t2]
                    rd = rden.next()
                    t = self.V(lambda e, rd=rd, b=den.at: e.reciprocal(rd.at[:, :], ps[:, b, :]), t2, rd.free)
                    den.free = [t]
                    t = self.V(lambda e, rd=rd, b=b, bk=num.at, yT=yT: e.tensor_tensor(
                        yT[:, b * S:(b + 1) * S], ps[:, bk, :], rd.at[:, :], ALU.mult), t, t1)
                    num.free, rd.free = [t], [t]
                bank.free = [t_b]
                qT.free = [t2]
                t_y.append(t)
            self.x_ready = []
            for c in range(NC):
                bank = self.banks.next()
                t = self.chain(ps[:, bank.at, 0:D], [(kdd[:, p, c, :], wo[:, p, :]) for p in range(PAIRS)], bank.free, t_y, t_wo)
                t = self.V(lambda e, c=c, b=bank.at: e.tensor_tensor(self.x[:, c, :], self.x[:, c, :], ps[:, b, 0:D], ALU.add), t, t_xb)
                bank.free = [t]
                self.x_ready.append(t)
            self.fence()

    def columns(self, mem, tag, names):
        sizes = [int(np.prod(self.a[n].shape)) // P for n in names]
        total = sum(sizes)
        rows = self.sb(tag + "_rows", [total, P], F32, mem)
        cols = self.sb(tag + "_cols", [P, total], F32, mem)
        arr = self.arrival(tag + "_cols")
        at, views = 0, {}
        for n, k in zip(names, sizes):
            src = self.a[n] if len(self.a[n].shape) == 1 else self.a[n].rearrange("e n -> (e n)")
            t = arr.dma(self.sp, rows[at:at + k, :], src.rearrange("(k p) -> k p", p=P))
            views[n] = cols[:, at:at + k]
            at += k
        bank = self.banks.next()
        t = self.pe.do(lambda e: e.transpose(self.ps[:, bank.at, 0:total], rows[:, :], self.ident[0:total, 0:total]),
                       t, bank.free, self.t_ident)
        t = self.copy(self.act, cols[:, :], self.ps[:, bank.at, 0:total], t)
        bank.free = [t]
        return views, t

    PARTS16 = [([(0, 0), (0, 1), (1, 0), (0, 2), (2, 0), (1, 1)], 96)]
    PARTS32 = [([(0, 0), (0, 1), (1, 0), (1, 1)], None), ([(0, 2), (2, 0)], 64)]

    def split3(self, lane, src, parts, tmp, *tickets):
        t = lane.do(lambda e: e.tensor_copy(parts[:, 0, :], src), lane.last(), *tickets)
        t = lane.do(lambda e: e.tensor_tensor(tmp, src, parts[:, 0, :], ALU.subtract), t)
        t = lane.do(lambda e: e.tensor_copy(parts[:, 1, :], tmp), t)
        return lane.do(lambda e: e.tensor_tensor(parts[:, 2, :], tmp, parts[:, 1, :], ALU.subtract), t)

    def scratch(self, name, feats, tokens):
        return self.nc.dram_tensor("scratch_" + name, (3, feats, tokens), BF16).ap()

    def parts_out(self, mem, tag):
        if tag not in self.split_bufs:
            self.split_bufs[tag] = Ring([(self.sb(f"{tag}_s{i}", [P, BANK], F32, mem), self.sb(f"{tag}_t{i}", [P, BANK], F32, mem),
                                          self.sb(f"{tag}_p{i}", [P, 3, BANK], BF16, mem), self.arrival(f"{tag}_w{i}")) for i in range(4)])
            self.split_n = 0
        return self.split_bufs[tag]

    def send_parts(self, ring, fill, dram, f, n):
        slot = ring.next()
        src, tmp, parts, arr = slot.at
        t = fill(src[:, :], slot.free)
        lane = self.pool if self.split_n % 3 == 0 else self.dve
        self.split_n += 1
        t = self.split3(lane, src[:, :], parts, tmp[:, :], t)
        t = arr.dma(self.sp, dram[:, f * P:(f + 1) * P, n * BANK:(n + 1) * BANK].rearrange("s p t -> p s t"), parts[:, :, :], t)
        slot.free = [t]
        return t

    def project_parts(self, ring, w, fs, rhs, t_w, t_in, bias, dram, tokens, feats):
        done = {}
        for n in range(tokens // BANK):
            for m in range(feats // P):
                bank = self.banks.next()
                t = self.chain(self.ps[:, bank.at, :], [(w[:, f, m * P:(m + 1) * P], rhs(f, n)) for f in range(fs)],
                               bank.free, t_w, t_in)

                def fill(dst, free, b=bank, m=m, t=t):
                    if bias is None:
                        t1 = self.A(lambda e: e.activation(dst, self.ps[:, b.at, :], ACT.Copy), t, free)
                    else:
                        t1 = self.A(lambda e: e.activation(dst, self.ps[:, b.at, :], ACT.Identity, bias=bias[:, m:m + 1]), t, free)
                    b.free = [t1]
                    return t1
                done[m, n] = self.send_parts(ring, fill, dram, m, n)
        return done

    def attend(self, tag, jobs, d, scale, mem):
        ps, pe = self.ps, self.pe
        spec = self.PARTS16 if d == 16 else self.PARTS32
        kmax = max(j["keys"] for j in jobs)
        softmax = jobs[0].get("decay") is None
        nbuf = 2
        sets = []
        for i in range(nbuf):
            qs = [self.sb(f"{tag}_qs{i}{u}", [P, 4, S], BF16, mem) for u in range(len(spec))]
            ks = [self.sb(f"{tag}_ks{i}{u}", [P, 4, kmax], BF16, mem) for u in range(len(spec))]
            nm = self.sb(f"{tag}_nm{i}", [P, 4, 4], F32, mem)
            nt = self.sb(f"{tag}_nt{i}", [P, 4, 4], F32, mem)
            np_ = self.sb(f"{tag}_np{i}", [P, 4, 4, 3], BF16, mem)
            nmT = self.sb(f"{tag}_nmT{i}", [12, S], BF16, mem)
            st = dict(qs=qs, ks=ks, nm=nm, nt=nt, np=np_, nmT=nmT, arr=self.arrival(f"{tag}_l{i}"), arm=self.arrival(f"{tag}_m{i}"),
                      free=[], t_one=None)
            if softmax:
                for u, (pairs, row) in enumerate(spec):
                    if row is not None:
                        st["t_one"] = self.G(lambda e, k=ks[u], row=row: e.memset(k[row:row + 3, :, :], 1.0))
            sets.append(st)
        wts = Ring([self.sb(f"{tag}_w{i}", [P, 2, S], F32, mem) for i in range(4)])
        if jobs[0]["mode"] == "upper":
            wds = Ring([self.sb(f"{tag}_wd{i}", [P, 2, P], F32, mem) for i in range(3)])
        pairs_ring = Ring([0, 2, 4])
        for i, s in enumerate(pairs_ring.slots):
            s.free = self.banks.slots[2 * i].free + self.banks.slots[2 * i + 1].free
        acc = Slot(6)
        acc.free = self.banks.slots[6].free + self.banks.slots[7].free

        def load(n):
            job, st = jobs[n], sets[n % nbuf]
            arr = st["arr"]
            self.sp.wait(st["free"], job["ready"])
            for u, (pairs, row) in enumerate(spec):
                for i, (qp, kp) in enumerate(pairs):
                    for (dram, first), part, tile, width in ((job["q"], qp, st["qs"][u], S), (job["k"], kp, st["ks"][u], job["keys"])):
                        src = dram[part, job["rows"]:job["rows"] + 4 * d, first:first + width].rearrange("(h i) t -> i h t", h=4)
                        t = arr.dma(self.sp, tile[i * d:(i + 1) * d, :, 0:width], src)
            st["loaded"] = t

        def pass1(n):
            job, st = jobs[n], sets[n % nbuf]
            pairs = spec[0][0]
            K = len(pairs) * d
            q, k = st["qs"][0], st["ks"][0]
            t_r = None
            for i in range(SC):
                if job["mode"] == "causal":
                    for jj in range(2):
                        pr = pairs_ring.next()
                        N = (i + 1) * P
                        for j in range(2):
                            h = 2 * jj + j
                            pe.do(lambda e, h=h, b=pr.at + j, i=i, N=N: e.matmul(
                                ps[:, b, 0:N], q[0:K, h, i * P:(i + 1) * P], k[0:K, h, 0:N], start=True, stop=False),
                                pr.free, st["loaded"], tick=False)
                            t = pe.do(lambda e, b=pr.at + j, i=i, N=N: e.matmul(
                                ps[:, b, N - P:N], self.identb[:, :], self.mask_qk[:, :], start=False, stop=True),
                                self.t_const, tick=j == 1)
                        t_r = self.V(lambda e, b=pr.at, i=i, jj=jj, N=N: e.tensor_reduce(
                            st["nm"][:, i, 2 * jj:2 * jj + 2], ps[:, b:b + 2, 0:N], AX.X, ALU.max, negate=True), t, st.get("nm_free"))
                        pr.free = [t_r]
                        yield
                elif job["keys"] == S:
                    for jj in range(2):
                        pr = pairs_ring.next()
                        for j in range(2):
                            t = pe.do(lambda e, h=2 * jj + j, b=pr.at + j, i=i: e.matmul(
                                ps[:, b, :], q[0:K, h, i * P:(i + 1) * P], k[0:K, h, 0:S], start=True, stop=True),
                                pr.free, st["loaded"], tick=j == 1)
                        t_r = self.V(lambda e, b=pr.at, i=i, jj=jj: e.tensor_reduce(
                            st["nm"][:, i, 2 * jj:2 * jj + 2], ps[:, b:b + 2, :], AX.X, ALU.max, negate=True), t, st.get("nm_free"))
                        pr.free = [t_r]
                        yield
                else:
                    for h in range(4):
                        pr = pairs_ring.next()
                        for j in range(2):
                            t = pe.do(lambda e, h=h, j=j, b=pr.at + j, i=i: e.matmul(
                                ps[:, b, :], q[0:K, h, i * P:(i + 1) * P], k[0:K, h, j * S:(j + 1) * S], start=True, stop=True),
                                pr.free, st["loaded"], tick=j == 1)
                        t_r = self.V(lambda e, b=pr.at, i=i, h=h: e.tensor_reduce(
                            st["nm"][:, i, h:h + 1], ps[:, b:b + 2, :], AX.XY, ALU.max, negate=True), t, st.get("nm_free"))
                        pr.free = [t_r]
                        yield
            nm, nt, np_, nmT = st["nm"], st["nt"], st["np"], st["nmT"]
            t = self.V(lambda e: e.tensor_copy(np_[:, :, :, 0], nm[:, :, :]), t_r, st.get("np_free"))
            t = self.V(lambda e: e.tensor_tensor(nt[:, :, :], nm[:, :, :], np_[:, :, :, 0], ALU.subtract), t)
            t = self.V(lambda e: e.tensor_copy(np_[:, :, :, 1], nt[:, :, :]), t)
            t = self.V(lambda e: e.tensor_tensor(np_[:, :, :, 2], nt[:, :, :], np_[:, :, :, 1], ALU.subtract), t)
            st["nm_free"] = t
            pr = pairs_ring.next()
            view = ps[0:12, pr.at, 0:S // 2].bitcast(BF16)
            for i in range(SC):
                t2 = pe.do(lambda e, i=i: e.transpose(view[:, i * P:(i + 1) * P], np_[:, i, :, :].rearrange("p h s -> p (h s)"),
                                                     self.identb[:, :]), t, pr.free, self.t_const, tick=i == SC - 1)
            st["np_free"] = t2
            t = self.V(lambda e: e.tensor_copy(nmT[:, :], view), t2, st.get("nmT_free"))
            pr.free = [t]
            u = len(spec) - 1
            row = spec[u][1]
            for h in range(4):
                t3 = st["arm"].dma(self.sp, st["qs"][u][row:row + 3, h, :], nmT[3 * h:3 * h + 3, :], t)
            st["maxed"] = st["nmT_free"] = t3
            yield

        def pass2(n):
            job, st = jobs[n], sets[n % nbuf]
            chunks = job["keys"] // P
            order = list(range(chunks))[::-1] if job["mode"] == "upper" else list(range(chunks))
            late = []
            first = [True]

            def values(c, jj, w, wd, t, t_wd, last):
                lo = c * P if job["mode"] == "causal" else 0
                for j in range(2):
                    h = 2 * jj + j
                    o = ps[32 * h:32 * h + 32, 6, :]
                    start = c == order[0]
                    if job["mode"] == "upper":
                        if c:
                            pe.do(lambda e, o=o, w=w, j=j, c=c, h=h, start=start: e.matmul(
                                o[:, 0:c * P], job["v"](c, h), w.at[:, j, 0:c * P], start=start, stop=False), t, acc.free, job["v_ready"], tick=False)
                        t1 = pe.do(lambda e, o=o, wd=wd, j=j, c=c, h=h, last=last: e.matmul(
                            o[:, c * P:(c + 1) * P], job["v"](c, h), wd.at[:, j, :], start=False, stop=last), t_wd)
                    else:
                        t1 = pe.do(lambda e, o=o, w=w, j=j, c=c, h=h, start=start, last=last, lo=lo: e.matmul(
                            o[:, lo:S], job["v"](c, h), w.at[:, j, lo:S], start=start, stop=last), t, acc.free, job["v_ready"], tick=j == 1)
                    if softmax and d == 32:
                        t1 = pe.do(lambda e, j=j, w=w, h=h, start=start, last=last: e.matmul(
                            ps[32 * h:32 * h + 32, 7, :], self.ones[:, 0:32], w.at[:, j, :], start=start, stop=last), t, acc.free, tick=j == 1)
                w.free = [t1]
                if wd is not None:
                    wd.free = [t1]
                return t1

            for c in order:
                lo = c * P if job["mode"] == "causal" else 0
                for jj in range(2):
                    pr = pairs_ring.next()
                    for j in range(2):
                        h = 2 * jj + j
                        out = ps[:, pr.at + j, lo:S]
                        pe.wait(pr.free, st["loaded"], st["maxed"] if softmax else None, st["t_one"])
                        for u, (pairs, row) in enumerate(spec):
                            K = len(pairs) * d + (3 if softmax and row is not None else 0)
                            end = u == len(spec) - 1 and job["mode"] != "causal" or (u == len(spec) - 1 and not softmax)
                            t = pe.do(lambda e, u=u, K=K, h=h, c=c, out=out, lo=lo, end=end: e.matmul(
                                out, st["ks"][u][0:K, h, c * P:(c + 1) * P], st["qs"][u][0:K, h, lo:S], start=u == 0, stop=end),
                                tick=end and j == 1)
                        if job["mode"] == "causal" and softmax:
                            t = pe.do(lambda e, b=pr.at + j, lo=lo: e.matmul(
                                ps[:, b, lo:lo + P], self.identb[:, :], self.mask_kq[:, :], start=False, stop=True), tick=j == 1)
                    w = wts.next()
                    if softmax:
                        t = self.A(lambda e, w=w, b=pr.at, lo=lo: e.activation(w.at[:, :, lo:S], ps[:, b:b + 2, lo:S], ACT.Exp, scale=scale),
                                   t, w.free)
                    else:
                        t = self.V(lambda e, w=w, b=pr.at, lo=lo, jj=jj: e.tensor_tensor(
                            w.at[:, :, lo:S], ps[:, b:b + 2, lo:S], job["decay"](jj, S - lo), ALU.mult), t, w.free, job["decay_ready"])
                    pr.free = [t]
                    wd, t_wd = None, None
                    if job["mode"] == "upper":
                        wd = wds.next()
                        t_wd = self.G(lambda e, wd=wd, w=w, c=c: e.affine_select(
                            out=wd.at[:, :, :], in_=w.at[:, :, c * P:(c + 1) * P], compare_op=ALU.is_gt, fill=0.0, base=0,
                            pattern=[[0, 2], [-1, P]], channel_multiplier=1), t, wd.free)
                    late.append((c, jj, w, wd, t, t_wd, c == order[-1]))
                    if len(late) > 1:
                        values(*late.pop(0))
                    yield
            while late:
                t_end = values(*late.pop(0))
            st["free"] = [t_end]
            acc.free = [job["finish"](job, t_end, pairs_ring)]
            yield

        load(0)
        if softmax:
            for _ in pass1(0):
                pass
        for n in range(len(jobs)):
            nxt = iter(())
            if n + 1 < len(jobs):
                load(n + 1)
                if softmax:
                    nxt = pass1(n + 1)
            for _ in pass2(n):
                next(nxt, None)
                if jobs[n]["keys"] < (jobs[n + 1]["keys"] if n + 1 < len(jobs) else 0):
                    next(nxt, None)
            for _ in nxt:
                pass
        for i, s in enumerate(pairs_ring.slots):
            self.banks.slots[2 * i].free = list(s.free)
            self.banks.slots[2 * i + 1].free = list(s.free)
        for i in (6, 7):
            self.banks.slots[i].free = list(acc.free)

    def context(self):
        with ExitStack() as mem:
            ctx = self.sb("ctx", [P, MC, CW], F32, mem)
            src = self.a["ctx_512"].rearrange("b (c p) d -> p (b c) d", p=P)
            t_c = self.arrival("ctx").dma(self.sp, ctx[:, :, :], src)
            self.ctxT_ready = self.to_features(ctx, CW, MC, [t_c] * MC, lambda f, n, view, t: self.copy(
                self.act if n % 2 else self.dve, self.ctxT[:, n * BANK:(n + 1) * BANK], view, t))
            self.fence()

    def cross_attention(self):
        a, ps = self.a, self.ps
        self.context()
        with ExitStack() as mem:
            sb = lambda n, s, dt=F32: self.sb("xa_" + n, s, dt, mem)
            W = {}
            tW = {}
            for n, rows in (("Wq", FC), ("Wk", FC), ("Wcq", FC), ("Wck", 1), ("Wv", FC), ("Wcv", 1)):
                W[n] = sb(n, [P, rows, D])
                tW[n] = self.arrival("xa" + n).dma(self.sp, W[n][:, :, :], a["L0_xattn_" + n].rearrange("(f p) n -> p f n", p=P))
            bcol, t_bc = self.columns(mem, "xab", ["L0_xattn_" + n for n in ("bq", "bk", "bcq", "bck")])
            brow = sb("brow", [P, 3, D])
            abr = self.arrival("xabr")
            for i, n in enumerate(("bv", "bcv", "bp")):
                t_br = abr.dma(self.sp, brow[:, i, :], a["L0_xattn_" + n].partition_broadcast(P))
            dh = D // H
            wp = sb("wp", [P, 4, D])
            t_wz = self.G(lambda e: e.memset(wp[:, :, :], 0.0))
            awp = self.arrival("xawp")
            for h in range(4):
                t_wp = awp.dma(self.sp, wp[32 * h:32 * h + dh, :, :], a["L0_xattn_Wp"].rearrange("(g h i) n -> h i g n", g=4, h=4)[h], t_wz)
            v = sb("v", [P, NC, H, 32])
            vc = sb("vc", [P, MC, H, 32])
            t_vo = self.G(lambda e: e.memset(v[:, :, :, :], 1.0))
            t_vco = self.G(lambda e: e.memset(vc[:, :, :, :], 1.0))
            sel = sb("sel", [P, P])
            sel4 = sel[:, :].rearrange("p (h i) -> p h i", h=4)
            t = self.G(lambda e: e.memset(sel[:, :], 0.0))
            t_sel = self.G(lambda e: e.affine_select(out=sel4, in_=sel4, compare_op=ALU.not_equal, fill=1.0, base=-dh,
                                                     pattern=[[-32, 4], [0, 32]], channel_multiplier=1), t)
            yT = sb("yT", [P, 4, T])
            self.norm_x()
            dq, dk, dcq, dck = (self.scratch("xa" + n, D, w) for n, w in (("q", T), ("k", T), ("cq", T), ("ck", TM)))
            with ExitStack() as tmp:
                ring = self.parts_out(tmp, "xap")
                xT = lambda f, n: self.xnT[:, f, n * BANK:(n + 1) * BANK]
                cT = lambda f, n: self.ctxT[:, n * BANK:(n + 1) * BANK]
                r_q = self.project_parts(ring, W["Wq"], FC, xT, [tW["Wq"], t_bc], self.xnT_ready, bcol["L0_xattn_bq"], dq, T, D)
                r_k = self.project_parts(ring, W["Wk"], FC, xT, tW["Wk"], self.xnT_ready, bcol["L0_xattn_bk"], dk, T, D)
                r_cq = self.project_parts(ring, W["Wcq"], FC, xT, tW["Wcq"], self.xnT_ready, bcol["L0_xattn_bcq"], dcq, T, D)
                r_ck = self.project_parts(ring, W["Wck"], 1, cT, tW["Wck"], self.ctxT_ready, bcol["L0_xattn_bck"], dck, TM, D)
                t_v, t_vc = [], []
                for c in range(NC):
                    bank = self.banks.next()
                    t = self.chain(ps[:, bank.at, 0:D], [(self.xnT[:, f, c * P:(c + 1) * P], W["Wv"][:, f, :]) for f in range(FC)],
                                   bank.free, tW["Wv"])
                    t = self.V(lambda e, c=c, b=bank.at: e.tensor_tensor(
                        v[:, c, :, 0:dh], ps[:, b, 0:D].rearrange("p (h i) -> p h i", h=H), brow[:, 0, :].rearrange("p (h i) -> p h i", h=H),
                        ALU.add), t, t_br, t_vo)
                    bank.free = [t]
                    t_v.append(t)
                for c in range(MC):
                    bank = self.banks.next()
                    t = self.chain(ps[:, bank.at, 0:D], [(self.ctxT[:, c * P:(c + 1) * P], W["Wcv"][:, 0, :])], bank.free, tW["Wcv"])
                    t = self.V(lambda e, c=c, b=bank.at: e.tensor_tensor(
                        vc[:, c, :, 0:dh], ps[:, b, 0:D].rearrange("p (h i) -> p h i", h=H), brow[:, 1, :].rearrange("p (h i) -> p h i", h=H),
                        ALU.add), t, t_br, t_vco)
                    bank.free = [t]
                    t_vc.append(t)
                t_xb = None
                for c in range(NC):
                    t_xb = self.G(lambda e, c=c: e.tensor_tensor(self.x[:, c, :], self.x[:, c, :], brow[:, 2, :], ALU.add),
                                  self.xn_ready[-1], t_br)
                self.fence(*[s.free for s in ring.slots])
            raw = Ring([sb(f"raw{i}", [P, S]) for i in range(2)])
            yc = Ring([sb(f"yc{i}", [P, S]) for i in range(2)])
            t_self = {}
            t_y = []

            def finish(job, t, ring):
                r = raw.next()
                t_raw = self.A(lambda e: e.activation(r.at[:, :], ps[:, 6, :], ACT.Copy), t, r.free)
                pr = ring.next()
                t1 = self.chain(ps[:, pr.at, :], [(sel[:, :], r.at[:, :])], t_raw, pr.free, t_sel)
                b, g = job["b"], job["g"]
                y = yT[:, g, b * S:(b + 1) * S]
                q = yc.next()
                t2 = self.V(lambda e: e.reciprocal(q.at[:, :], ps[:, pr.at, :]), t1, q.free)
                pr.free = [t2]
                if not job["cross"]:
                    t3 = self.G(lambda e: e.tensor_tensor(y, r.at[:, :], q.at[:, :], ALU.mult), t2)
                    t_self[b, g] = t3
                else:
                    t3 = self.G(lambda e: e.tensor_tensor(q.at[:, :], r.at[:, :], q.at[:, :], ALU.mult), t2)
                    t3 = self.G(lambda e: e.tensor_tensor(y, y, q.at[:, :], ALU.add), t3, t_self[b, g])
                    t_y.append(t3)
                q.free = [t3]
                r.free = [t3]
                return t_raw

            def jobs(cross):
                out = []
                for b in range(B):
                    for g in range(4):
                        rows = g * 4 * dh
                        m = rows // P
                        kn = [b] if not cross else [2 * b, 2 * b + 1]
                        out.append(dict(q=((dcq if cross else dq), b * S), k=((dck, b * MEM) if cross else (dk, b * S)), rows=rows,
                                        keys=MEM if cross else S, mode="full" if cross else "causal", b=b, g=g, cross=cross,
                                        v=(lambda c, h, b=b, g=g: vc[:, b * MC // B + c, 4 * g + h, :]) if cross else
                                          (lambda c, h, b=b, g=g: v[:, b * SC + c, 4 * g + h, :]),
                                        v_ready=(t_vc if cross else t_v)[-1],
                                        ready=[(r_cq if cross else r_q)[m, b]] + [(r_ck if cross else r_k)[m, n] for n in kn],
                                        finish=finish))
                return out
            self.attend("xa", jobs(False) + jobs(True), dh, dh ** -0.5, mem)
            self.x_ready = []
            for c in range(NC):
                bank = self.banks.next()
                t = self.chain(ps[:, bank.at, 0:D], [(yT[:, g, c * P:(c + 1) * P], wp[:, g, :]) for g in range(4)], bank.free, t_y, t_wp)
                t = self.V(lambda e, c=c, b=bank.at: e.tensor_tensor(self.x[:, c, :], self.x[:, c, :], ps[:, b, 0:D], ALU.add), t, t_xb)
                bank.free = [t]
                self.x_ready.append(t)
            self.fence()

    def route(self, mem, tag, w, n_exp, bias_row, t_w):
        ps = self.ps
        lg = self.sb(tag + "_lg", [P, NC, 8], F32, mem)
        st = self.sb(tag + "_st", [P, NC, 2], F32, mem)
        top = self.sb(tag + "_top", [P, NC, 8], F32, mem)
        idx = self.sb(tag + "_idx", [P, NC, 8], U32, mem)
        who = self.sb(tag + "_who", [P, NC, 2], F32, mem)
        t_pad = self.V(lambda e: e.memset(lg[:, :, :], -1.0))
        bank = self.banks.next()
        for c in range(NC):
            t = self.chain(ps[:, bank.at, 8 * c:8 * c + n_exp], [(self.xnT[:, f, c * P:(c + 1) * P], w[:, f, :]) for f in range(FC)],
                           bank.free, self.xnT_ready, t_w, tick=c == NC - 1)
        live = lg[:, :, 0:n_exp]
        view = ps[:, bank.at, 0:8 * NC].rearrange("p (c e) -> p c e", e=8)[:, :, 0:n_exp]
        if bias_row is not None:
            t = self.V(lambda e: e.tensor_tensor(live, view, bias_row.unsqueeze(1).broadcast_to([P, NC, n_exp]), ALU.add), t, t_w, t_pad)
        else:
            t = self.V(lambda e: e.tensor_copy(live, view), t, t_pad)
        bank.free = [t]
        t = self.V(lambda e: e.tensor_reduce(st[:, :, 0], live, AX.X, ALU.max), t)
        bc = lambda i: st[:, :, i].unsqueeze(2).broadcast_to([P, NC, n_exp])
        t = self.V(lambda e: e.tensor_tensor(live, live, bc(0), ALU.subtract), t)
        t = self.A(lambda e: e.activation(live, live, ACT.Exp), t)
        t = self.V(lambda e: e.tensor_reduce(st[:, :, 0], live, AX.X, ALU.add), t)
        t = self.V(lambda e: e.reciprocal(st[:, :, 1], st[:, :, 0]), t)
        t = self.V(lambda e: e.tensor_tensor(live, live, bc(1), ALU.mult), t)
        for c in range(NC):
            t1 = self.V(lambda e, c=c: e.max(top[:, c, :], lg[:, c, :]), t if c == 0 else None)
        for c in range(NC):
            t = self.V(lambda e, c=c: e.max_index(idx[:, c, :], top[:, c, :], lg[:, c, :]), t1 if c == 0 else None)
        t = self.V(lambda e: e.tensor_copy(who[:, :, :], idx[:, :, 0:2]), t)
        return top, who, t

    def moe(self):
        a, ps = self.a, self.ps
        SLOTS = E0 * CAP
        NR = -(-SLOTS // P)
        with ExitStack() as mem:
            sb = lambda n, s, dt=F32: self.sb("mo_" + n, s, dt, mem)
            wr = sb("wr", [P, FC, E0])
            br = sb("br", [P, E0])
            t_wr = self.arrival("mowr").dma(self.sp, wr[:, :, :], a["L0_ffn_Wr"].rearrange("(f p) e -> p f e", p=P))
            t_br = self.arrival("mobr").dma(self.sp, br[:, :], a["L0_ffn_br"].partition_broadcast(P))
            b1, t_b1 = self.columns(mem, "mob1", ["L0_ffn_b1"])
            b1 = b1["L0_ffn_b1"]
            b2 = sb("b2", [1, E0 * D])
            t_b2 = self.arrival("mob2").dma(self.sp, b2[:, :], a["L0_ffn_b2"].rearrange("e d -> (e d)").unsqueeze(0))
            wring = Ring([(sb(f"w1_{i}", [P, FC, HID]), sb(f"w2_{i}", [P, HC, D]), self.arrival(f"mow{i}")) for i in range(4)])
            zero = sb("zero", [P, D])
            t_zero = self.G(lambda e: e.memset(zero[:, :], 0.0))
            xg = self.nc.dram_tensor("scratch_xg", (SLOTS + 2 * T, D), F32).ap()
            yo = self.nc.dram_tensor("scratch_yo", (SLOTS + 1, D), F32).ap()
            zrows = SLOTS // E0 // 2
            az = self.arrival("moz")
            az.dma(self.sp, xg[0:SLOTS, :].rearrange("(p k) d -> p k d", p=zrows), zero[0:zrows, :].unsqueeze(1).broadcast_to([zrows, SLOTS // zrows, D]), t_zero)
            t_z = az.dma(self.sp, yo[SLOTS:SLOTS + 1, :], zero[0:1, :], t_zero)
            weights = {}

            def load(e):
                slot = wring.next()
                w1, w2, arr = slot.at
                arr.dma(self.sp, w1[:, :, :], a["L0_ffn_W1"][e].rearrange("(f p) n -> p f n", p=P), slot.free)
                t = arr.dma(self.sp, w2[:, :, :], a["L0_ffn_W2"][e].rearrange("(f p) n -> p f n", p=P))
                weights[e] = (slot, w1, w2, t)
            for e in range(4):
                load(e)
            self.norm_x()
            top, who, t_top = self.route(mem, "mor", wr, E0, br[:, :], [t_wr, t_br])
            iota_e = sb("iota_e", [P, E0])
            t_i = self.G(lambda e: e.iota(iota_e[:, :], pattern=[[1, E0]], base=0, channel_multiplier=0, allow_small_or_imprecise_dtypes=True))
            dump = sb("dump", [P, 2, NC])
            t_i = self.G(lambda e: e.iota(dump[:, :, :], pattern=[[T, 2], [P, NC]], base=SLOTS, channel_multiplier=1, allow_small_or_imprecise_dtypes=True))
            tri = sb("tri", [P, P])
            t_tri = self.G(lambda e: e.memset(tri[:, :], 1.0))
            t_tri = self.G(lambda e: e.affine_select(out=tri[:, :], in_=tri[:, :], compare_op=ALU.is_gt, fill=0.0, base=0,
                                                     pattern=[[-1, P]], channel_multiplier=1), t_tri)
            chosen = sb("chosen", [P, 2, NC, E0])
            G = sb("G", [P, NC, E0])
            G2 = sb("G2", [P, NC, E0])
            ib = iota_e[:, :].unsqueeze(1).broadcast_to([P, NC, E0])
            for k in range(2):
                t = self.V(lambda e, k=k: e.tensor_tensor(chosen[:, k, :, :], ib, who[:, :, k:k + 1].broadcast_to([P, NC, E0]), ALU.is_equal), t_top, t_i)
            t = self.V(lambda e: e.tensor_tensor(G[:, :, :], chosen[:, 0, :, :], top[:, :, 0:1].broadcast_to([P, NC, E0]), ALU.mult), t)
            t = self.V(lambda e: e.tensor_tensor(G2[:, :, :], chosen[:, 1, :, :], top[:, :, 1:2].broadcast_to([P, NC, E0]), ALU.mult), t)
            t = self.V(lambda e: e.tensor_tensor(G[:, :, :], G[:, :, :], G2[:, :, :], ALU.add), t)
            t = self.V(lambda e: e.tensor_tensor(G2[:, :, :], chosen[:, 0, :, :], chosen[:, 1, :, :], ALU.add), t)
            t_G = self.V(lambda e: e.scalar_tensor_tensor(G[:, :, :], G2[:, :, :], -1.0, G[:, :, :], ALU.add, ALU.add), t)
            cnt = sb("cnt", [P, 3, NC, E0])
            junk = Ring([sb(f"junk{i}", [P, T]) for i in range(2)])
            t_c0 = self.V(lambda e: e.memset(cnt[:, :, :, :], 0.0))
            pr_ring = Ring([0, 2, 4, 6])
            for i, s in enumerate(pr_ring.slots):
                s.free = self.banks.slots[2 * i].free + self.banks.slots[2 * i + 1].free
            for x in range(E0):
                pr = pr_ring.next()
                for c in range(NC):
                    t = self.chain(ps[:, pr.at + c // 4, (c % 4) * P:(c % 4 + 1) * P],
                                   [(G[:, c, x:x + 1].broadcast_to([P, P]), self.ident[:, :])], pr.free, t_G, tick=c == NC - 1)
                row = ps[:, pr.at:pr.at + 2, :].rearrange("p b n -> p (b n)")
                for c in range(NC):
                    me = G[:, c, x:x + 1]
                    if c:
                        self.V(lambda e, c=c, me=me, row=row, x=x: e.tensor_scalar(
                            junk.slots[0].at[:, 0:c * P], row[:, 0:c * P], me, 0.0, ALU.is_ge, ALU.add, accum_out=cnt[:, 0, c, x:x + 1]), t, t_c0, self.dve.last())
                    self.V(lambda e, c=c, me=me, row=row, x=x: e.tensor_scalar(
                        junk.slots[0].at[:, c * P:T], row[:, c * P:T], me, 0.0, ALU.is_gt, ALU.add, accum_out=cnt[:, 1, c, x:x + 1]), t, t_c0, self.dve.last())
                    t1 = self.V(lambda e, c=c, me=me, row=row, x=x: e.scalar_tensor_tensor(
                        junk.slots[1].at[:, 0:P], row[:, c * P:(c + 1) * P], me, tri[:, :], ALU.is_equal, ALU.mult,
                        accum_out=cnt[:, 2, c, x:x + 1]), t, t_tri, self.dve.last())
                pr.free = [t1]
            for i, s in enumerate(pr_ring.slots):
                self.banks.slots[2 * i].free = list(s.free)
                self.banks.slots[2 * i + 1].free = list(s.free)
            t = self.V(lambda e: e.tensor_tensor(cnt[:, 0, :, :], cnt[:, 0, :, :], cnt[:, 1, :, :], ALU.add), t1)
            t_rank = self.V(lambda e: e.tensor_tensor(cnt[:, 0, :, :], cnt[:, 0, :, :], cnt[:, 2, :, :], ALU.add), t)
            slot = sb("slot", [P, 2, NC])
            rk = sb("rk", [P, 2, NC])
            ok = sb("ok", [P, 2, NC])
            to = sb("to", [P, 2, NC], U32)
            fro = sb("fro", [P, 2, NC], U32)
            for k in range(2):
                t = self.V(lambda e, k=k: e.tensor_tensor(chosen[:, k, :, :], chosen[:, k, :, :], cnt[:, 0, :, :], ALU.mult), t_rank)
                t = self.V(lambda e, k=k: e.tensor_reduce(rk[:, k, :], chosen[:, k, :, :], AX.X, ALU.add), t)
                t = self.V(lambda e, k=k: e.scalar_tensor_tensor(slot[:, k, :], who[:, :, k], float(CAP), rk[:, k, :], ALU.mult, ALU.add), t)
                t = self.V(lambda e, k=k: e.tensor_scalar(ok[:, k, :], rk[:, k, :], float(CAP), None, ALU.is_lt), t)
            t = self.V(lambda e: e.tensor_tensor(rk[:, :, :], slot[:, :, :], dump[:, :, :], ALU.subtract), t)
            t = self.V(lambda e: e.tensor_tensor(rk[:, :, :], rk[:, :, :], ok[:, :, :], ALU.mult), t)
            t_to = self.V(lambda e: e.tensor_tensor(to[:, :, :], rk[:, :, :], dump[:, :, :], ALU.add), t)
            t = self.V(lambda e: e.scalar_tensor_tensor(rk[:, :, :], slot[:, :, :], -float(SLOTS), ok[:, :, :], ALU.add, ALU.mult), t_to)
            t_fro = self.V(lambda e: e.tensor_scalar(fro[:, :, :], rk[:, :, :], float(SLOTS), None, ALU.add), t)
            sc = self.arrival("mosc")
            self.pool.wait(t_to, t_z)
            for c in range(NC):
                for k in range(2):
                    sc.count += 16
                    self.pool.items.append(lambda e, c=c, k=k: e.indirect_dma_start(
                        xg, bass.IndirectOffsetOnAxis(ap=to[:, k, c:c + 1], axis=0), self.xn[:, c, :], None).then_inc(sc.sem, 16))
            t_sc = (sc.sem, sc.count)
            xs = sb("xs", [P, NR, D])
            xgT = sb("xgT", [P, FC, NR * P])
            ax = self.arrival("moxg")
            full = SLOTS // P
            t = ax.dma(self.sp, xs[:, 0:full, :], xg[0:full * P, :].rearrange("(r p) d -> p r d", p=P), t_sc)
            rest = SLOTS - full * P
            if rest:
                t = ax.dma(self.sp, xs[0:rest, full, :], xg[full * P:SLOTS, :])
            t_g = []
            for f in range(FC):
                for r0 in range(0, NR, 4):
                    bank = self.banks.next()
                    rs = list(range(r0, min(NR, r0 + 4)))
                    for r in rs:
                        m = P if r < full else rest
                        t1 = self.pe.do(lambda e, r=r, m=m, b=bank.at, r0=r0, f=f: e.transpose(
                            ps[:, b, (r - r0) * P:(r - r0) * P + m], xs[0:m, r, f * P:(f + 1) * P], self.ident[0:m, 0:m]),
                            t, bank.free, tick=r == rs[-1])
                    n = (len(rs) - 1) * P + m
                    t1 = self.copy(self.act if f else self.dve, xgT[:, f, r0 * P:r0 * P + n], ps[:, bank.at, 0:n], t1)
                    bank.free = [t1]
                    t_g.append(t1)
            hT = Ring([sb(f"hT{i}", [P, HC, CAP]) for i in range(2)])
            os_ = Ring([(sb(f"o{i}", [P, 2, D]), self.arrival(f"moo{i}")) for i in range(2)])
            t_done = []
            for x in range(E0):
                wslot, w1, w2, t_w = weights[x]
                h = hT.next()
                t_h = []
                for m0 in range(0, HC, 2):
                    bank = self.banks.next()
                    for m in (m0, m0 + 1):
                        t = self.chain(ps[:, bank.at, (m - m0) * 256:(m - m0) * 256 + CAP],
                                       [(w1[:, f, m * P:(m + 1) * P], xgT[:, f, x * CAP:(x + 1) * CAP]) for f in range(FC)],
                                       bank.free, t_w, t_g, tick=m != m0)
                    for m in (m0, m0 + 1):
                        t1 = self.A(lambda e, m=m, m0=m0, b=bank.at, h=h, x=x: e.activation(
                            h.at[:, m, :], ps[:, b, (m - m0) * 256:(m - m0) * 256 + CAP], ACT.Silu,
                            bias=b1[:, x * HC + m:x * HC + m + 1]), t, h.free, t_b1)
                    bank.free = [t1]
                    t_h.append(t1)
                o = os_.next()
                ot, oarr = o.at
                for r, (lo, n) in enumerate(((0, P), (P, CAP - P))):
                    bank = self.banks.next()
                    t = self.chain(ps[0:n, bank.at, 0:D], [(h.at[:, m, lo:lo + n], w2[:, m, :]) for m in range(HC)] +
                                   [(self.ones[0:1, 0:n], b2[0:1, x * D:(x + 1) * D])], bank.free, t_h, t_b2, self.t_ones)
                    t1 = self.V(lambda e, n=n, r=r, b=bank.at, ot=ot: e.tensor_copy(ot[0:n, r, :], ps[0:n, b, 0:D]), t, o.free)
                    bank.free = [t1]
                    t2 = oarr.dma(self.sp, yo[x * CAP + lo:x * CAP + lo + n, :], ot[0:n, r, :], t1)
                    if r == 0:
                        first = t2
                h.free, wslot.free = [t], [t]
                o.free = [t2]
                t_done.append(t2)
                if x + 4 < E0:
                    load(x + 4)
            ga = [self.arrival(f"moga{i}") for i in range(8)]
            gb = Ring([(sb(f"g{i}", [P, D]), ga[i]) for i in range(8)])
            self.pool.wait(t_done, t_fro)
            self.x_ready = []
            for c in range(NC):
                for k in range(2):
                    g = gb.next()
                    gt, arr = g.at
                    self.pool.wait(g.free)
                    arr.count += 16
                    self.pool.items.append(lambda e, c=c, k=k, gt=gt, arr=arr: e.indirect_dma_start(
                        gt[:, :], None, yo, bass.IndirectOffsetOnAxis(ap=fro[:, k, c:c + 1], axis=0)).then_inc(arr.sem, 16))
                    t = self.V(lambda e, c=c, k=k, gt=gt: e.scalar_tensor_tensor(
                        self.x[:, c, :], gt[:, :], top[:, c, k:k + 1], self.x[:, c, :], ALU.mult, ALU.add),
                        (arr.sem, arr.count), self.dve.last())
                    g.free = [t]
                self.x_ready.append(t)
            self.fence()

    def retention(self):
        a, ps = self.a, self.ps
        dk = D // H
        with ExitStack() as mem:
            sb = lambda n, s, dt=F32: self.sb("re_" + n, s, dt, mem)
            wT = sb("wT", [P, FC, 3 * D])
            woT = sb("woT", [P, 4, D])
            yT = sb("yT", [P, 4, T])
            v = sb("v", [P, NC, H, 32])
            decay = sb("decay", [P, H, S])
            lg = sb("lg", [P, 4, H])
            dq, dkk = self.scratch("req", D, T), self.scratch("rek", D, T)
            t_v0 = self.G(lambda e: e.memset(v[:, :, :, :], 0.0))
            t_lg = self.arrival("relg").dma(self.sp, lg[:, 0, :], a["L1_attn_log_gamma"].partition_broadcast(P))
            t = self.V(lambda e: e.tensor_scalar(lg[:, 1, :], lg[:, 0, :], -1.0, None, ALU.mult), t_lg)
            t = self.V(lambda e: e.tensor_tensor(lg[:, 1, :], lg[:, 1, :], lg[:, 0, :], ALU.min), t)
            t = self.A(lambda e: e.activation(lg[:, 2, :], lg[:, 1, :], ACT.Exp), t)
            t = self.A(lambda e: e.activation(lg[:, 3, :], lg[:, 2, :], ACT.Ln, bias=1.0), t)
            t = self.V(lambda e: e.tensor_scalar(lg[:, 0, :], lg[:, 0, :], 0.0, None, ALU.min), t)
            t_gamma = self.V(lambda e: e.tensor_tensor(lg[:, 0, :], lg[:, 0, :], lg[:, 3, :], ALU.subtract), t)
            with ExitStack() as tmp:
                tb = lambda n, s, dt=F32: self.sb("ret_" + n, s, dt, tmp)
                raw = tb("raw", [P, 3 * FC, D])
                rawo = tb("rawo", [P, FC, H, 32])
                dist = tb("dist", [P, S])
                kt = tb("kt", [P, NC, D])
                kst = tb("kst", [P, 4, NC, H])
                ksq = tb("ksq", [P, NC, D])
                t_r = self.arrival("rew").dma(self.sp, raw[:, :, :], a["L1_attn_W_qkv"].rearrange("(o p) i -> p o i", p=P))
                t_z = self.G(lambda e: e.memset(rawo[:, :, :, :], 0.0))
                aw = self.arrival("rewo")
                for f in range(FC):
                    t_ro = aw.dma(self.sp, rawo[:, f, :, 0:dk], a["L1_attn_W_o"][f * P:(f + 1) * P, :].rearrange("p (h i) -> p h i", h=H), t_z)
                t = self.G(lambda e: e.iota(dist[:, :], pattern=[[1, S]], base=0, channel_multiplier=-1, allow_small_or_imprecise_dtypes=True))
                t_di = self.G(lambda e: e.tensor_scalar(dist[:, :], dist[:, :], 0.0, None, ALU.max), t)
                for h in range(H):
                    t = self.A(lambda e, h=h: e.activation(decay[:, h, :], dist[:, :], ACT.Exp, scale=lg[:, 0, h:h + 1]), t_di, t_gamma)
                t_dec = self.G(lambda e: e.affine_select(out=decay[:, :, 0:P], in_=decay[:, :, 0:P], compare_op=ALU.is_ge, fill=0.0, base=0,
                                                         pattern=[[0, H], [1, P]], channel_multiplier=-1), t)
                self.norm_x()
                t_wT = []
                for f in range(FC):
                    for o0 in (0, 3):
                        bank = self.banks.next()
                        for o in range(3):
                            t = self.pe.do(lambda e, o=o, o0=o0, f=f, b=bank.at: e.transpose(
                                ps[:, b, o * P:(o + 1) * P], raw[:, o0 + o, f * P:(f + 1) * P], self.ident[:, :]), t_r, bank.free, tick=o == 2)
                        t = self.copy(self.act, wT[:, f, o0 * P:(o0 + 3) * P], ps[:, bank.at, 0:3 * P], t)
                        bank.free = [t]
                        t_wT.append(t)
                for g in range(4):
                    bank = self.banks.next()
                    for f in range(FC):
                        t = self.pe.do(lambda e, f=f, g=g, b=bank.at: e.transpose(
                            ps[:, b, f * P:(f + 1) * P], rawo[:, f, 4 * g:4 * g + 4, :].rearrange("p h i -> p (h i)"), self.ident[:, :]),
                            t_ro, bank.free, tick=f == 1)
                    t_wo = self.copy(self.act, woT[:, g, :], ps[:, bank.at, 0:D], t)
                    bank.free = [t_wo]
                t_v, t_k = [], []
                for c in range(NC):
                    bank = self.banks.next()
                    t = self.chain(ps[:, bank.at, :], [(self.xnT[:, f, c * P:(c + 1) * P], wT[:, f, D:3 * D]) for f in range(FC)],
                                   bank.free, t_wT, self.xnT_ready)
                    t1 = self.A(lambda e, c=c, b=bank.at: e.activation(kt[:, c, :], ps[:, b, 0:D], ACT.Copy), t)
                    t2 = self.A(lambda e, c=c, b=bank.at: e.activation(
                        v[:, c, :, 0:dk], ps[:, b, D:2 * D].rearrange("p (h i) -> p h i", h=H), ACT.Copy), t, t_v0)
                    bank.free = [t2]
                    t_k.append(t1)
                    t_v.append(t2)
                k4 = kt[:, :, :].rearrange("p c (h i) -> p (c h) i", h=H)
                q4 = ksq[:, :, :].rearrange("p c (h i) -> p (c h) i", h=H)
                s4 = lambda i: kst[:, i, :, :].rearrange("p c h -> p (c h)")
                t = self.V(lambda e: e.tensor_reduce(s4(0), k4, AX.X, ALU.add), t_k)
                t = self.V(lambda e: e.tensor_scalar(s4(0), s4(0), 1.0 / dk, None, ALU.mult), t)
                t = self.V(lambda e: e.tensor_tensor(k4, k4, s4(0).unsqueeze(2).broadcast_to([P, NC * H, dk]), ALU.subtract), t)
                t = self.V(lambda e: e.tensor_tensor(q4, k4, k4, ALU.mult), t)
                t = self.V(lambda e: e.tensor_reduce(s4(1), q4, AX.X, ALU.add), t)
                t = self.V(lambda e: e.tensor_scalar(s4(1), s4(1), 1.0 / dk, LN_EPS, ALU.mult, ALU.add), t)
                t = self.A(lambda e: e.activation(s4(2), s4(1), ACT.Sqrt), t)
                t = self.V(lambda e: e.reciprocal(s4(3), s4(2)), t)
                t_kn = self.V(lambda e: e.tensor_tensor(k4, k4, s4(3).unsqueeze(2).broadcast_to([P, NC * H, dk]), ALU.mult), t)
                ring = self.parts_out(tmp, "rep")
                r_q = self.project_parts(ring, wT, FC, lambda f, n: self.xnT[:, f, n * BANK:(n + 1) * BANK], t_wT, None, None, dq, T, D)
                r_k = {}

                def send(f, n, view, t):
                    got = []

                    def fill(dst, free):
                        got.append(self.A(lambda e: e.activation(dst, view, ACT.Copy), t, free))
                        return got[0]
                    r_k[f, n] = self.send_parts(ring, fill, dkk, f, n)
                    return got[0]
                self.to_features(kt, D, NC, [t_kn] * NC, send)
                self.fence(*[s.free for s in ring.slots])

            t_y = []

            def finish(job, t, ring):
                b, g = job["b"], job["g"]
                t1 = self.A(lambda e: e.activation(yT[:, g, b * S:(b + 1) * S], ps[:, 6, :], ACT.Copy), t)
                t_y.append(t1)
                return t1

            jobs = []
            for b in range(B):
                for g in range(4):
                    rows = g * 4 * dk
                    jobs.append(dict(q=(dq, b * S), k=(dkk, b * S), rows=rows, keys=S, mode="causal", b=b, g=g,
                                     v=lambda c, h, b=b, g=g: v[:, b * SC + c, 4 * g + h, :], v_ready=t_v[-1],
                                     decay=lambda jj, n, g=g: decay[:, 4 * g + 2 * jj:4 * g + 2 * jj + 2, 0:n], decay_ready=t_dec,
                                     ready=[r_q[rows // P, b], r_k[rows // P, b]], finish=finish))
            self.attend("re", jobs, dk, 1.0, mem)
            self.x_ready = []
            for c in range(NC):
                bank = self.banks.next()
                t = self.chain(ps[:, bank.at, 0:D], [(yT[:, g, c * P:(c + 1) * P], woT[:, g, :]) for g in range(4)], bank.free, t_y, t_wo)
                t = self.V(lambda e, c=c, b=bank.at: e.tensor_tensor(self.x[:, c, :], self.x[:, c, :], ps[:, b, 0:D], ALU.add), t)
                bank.free = [t]
                self.x_ready.append(t)
            self.fence()

    def mha(self, pre, xb, xb_ready, cross):
        a, ps = self.a, self.ps
        A = "L1_xattn_" + pre + "_"
        dh = 32
        HD = H * dh
        cy = CW if cross else D
        fy = cy // P
        ty = TM if cross else T
        ny = ty // P
        with ExitStack() as mem:
            sb = lambda n, s, dt=F32: self.sb(pre + n, s, dt, mem)
            vecs, t_c = self.columns(mem, pre + "c", [A + n for n in ("lnx_g", "lnx_b", "lny_g", "lny_b", "ln3_g", "ln3_b", "li2_b")])
            rows = sb("rows", [P, 2, D])
            ar = self.arrival(pre + "rows")
            for i, n in enumerate(("li1_b", "li3_b")):
                t_rows = ar.dma(self.sp, rows[:, i, :], a[A + n].partition_broadcast(P))
            li1 = sb("li1", [P, HD // P, D])
            t_li1 = self.arrival(pre + "li1").dma(self.sp, li1[:, :, :], a[A + "li1_w"].rearrange("(f p) n -> p f n", p=P))
            core = sb("core", [P, NC, D])
            y = sb("y", [P, NC, D])
            oT = sb("oT", [P, 4, T])
            w_core_free = []

            def affine(g, b, dst):
                def emit(f, n, view, t):
                    return self.A(lambda e: e.activation(dst[:, f, n * BANK:(n + 1) * BANK], view, ACT.Identity,
                                                         bias=vecs[A + b][:, f:f + 1], scale=vecs[A + g][:, f:f + 1]), t, t_c)
                return emit
            with ExitStack() as att:
                ab = lambda n, s, dt=F32: self.sb(pre + n, s, dt, att)
                v = ab("v", [P, ny, HD])
                dq, dk = self.scratch(pre + "q", HD, T), self.scratch(pre + "k", HD, ty)
                with ExitStack() as tmp:
                    tb = lambda n, s, dt=F32: self.sb(pre + n, s, dt, tmp)
                    wq, wk, wv = tb("wq", [P, FC, HD]), tb("wk", [P, fy, HD]), tb("wv", [P, fy, HD])
                    tw = {}
                    for n, w, fs in (("wq", wq, FC), ("wk", wk, fy), ("wv", wv, fy)):
                        arr = self.arrival(pre + n)
                        for f in range(fs):
                            tw[n] = arr.dma(self.sp, w[:, f, :].rearrange("p (h d) -> p h d", h=H),
                                            a[A + n][:, f * P:(f + 1) * P, :].rearrange("h p d -> p h d"))
                    done = self.normalize(xb, core, NC, D, xb_ready, pre + "x")
                    if not cross:
                        yT = tb("ynT", [P, FC, T])

                        def both(f, n, view, t):
                            affine("lnx_g", "lnx_b", self.xnT)(f, n, view, t)
                            return affine("lny_g", "lny_b", yT)(f, n, view, t)
                        t_x = t_yn = self.to_features(core, D, NC, done, both)
                        ysrc = lambda f, n: yT[:, f, n * BANK:(n + 1) * BANK]
                        ychunk = lambda f, c: yT[:, f, c * P:(c + 1) * P]
                    else:
                        t_x = self.to_features(core, D, NC, done, affine("lnx_g", "lnx_b", self.xnT))
                        ctx = tb("ctx", [P, MC, CW])
                        t_ctx = self.arrival(pre + "ctx").dma(self.sp, ctx[:, :, :], a["ctx_512"].rearrange("b (c p) d -> p (b c) d", p=P))
                        dc = self.normalize(ctx, ctx, MC, CW, [t_ctx] * MC, pre + "ctx")
                        cT = self.ctxT[:, :].unsqueeze(1)
                        t_yn = self.to_features(ctx, CW, MC, dc, affine("lny_g", "lny_b", cT))
                        ysrc = lambda f, n: self.ctxT[:, n * BANK:(n + 1) * BANK]
                        ychunk = lambda f, c: self.ctxT[:, c * P:(c + 1) * P]
                    ring = self.parts_out(tmp, pre + "p")
                    r_q = self.project_parts(ring, wq, FC, lambda f, n: self.xnT[:, f, n * BANK:(n + 1) * BANK], tw["wq"], t_x, None, dq, T, HD)
                    r_k = self.project_parts(ring, wk, fy, ysrc, tw["wk"], t_yn, None, dk, ty, HD)
                    t_v = []
                    for c in range(ny):
                        bank = self.banks.next()
                        t = self.chain(ps[:, bank.at, :], [(ychunk(f, c), wv[:, f, :]) for f in range(fy)], bank.free, tw["wv"])
                        t = self.copy(self.act if c % 2 else self.dve, v[:, c, :], ps[:, bank.at, :], t)
                        bank.free = [t]
                        t_v.append(t)
                    for c in range(NC):
                        t_yb = self.G(lambda e, c=c: e.tensor_tensor(y[:, c, :], xb[:, c, :], rows[:, 0, :], ALU.add), xb_ready[c], t_rows)
                    self.fence(*[s.free for s in ring.slots])
                rd = Ring([ab(f"rd{i}", [P, S]) for i in range(2)])
                t_o = []

                def finish(job, t, ring):
                    b, g = job["b"], job["g"]
                    r = rd.next()
                    t1 = self.V(lambda e: e.reciprocal(r.at[:, :], ps[:, 7, :]), t, r.free)
                    t2 = self.V(lambda e: e.tensor_tensor(oT[:, g, b * S:(b + 1) * S], ps[:, 6, :], r.at[:, :], ALU.mult), t1)
                    r.free = [t2]
                    t_o.append(t2)
                    return t2
                jobs = []
                for b in range(B):
                    for g in range(4):
                        kn = [2 * b, 2 * b + 1] if cross else [b]
                        jobs.append(dict(q=(dq, b * S), k=(dk, b * (ty // B)), rows=g * P, keys=ty // B, mode="full" if cross else "upper",
                                         b=b, g=g, v=lambda c, h, b=b, g=g: v[:, b * (ny // B) + c, (4 * g + h) * dh:(4 * g + h + 1) * dh],
                                         v_ready=t_v[-2:], ready=[r_q[g, b]] + [r_k[g, n] for n in kn], finish=finish))
                self.attend(pre, jobs, dh, dh ** -0.5, att)
                t_y = []
                for c in range(NC):
                    bank = self.banks.next()
                    t = self.chain(ps[:, bank.at, 0:D], [(oT[:, g, c * P:(c + 1) * P], li1[:, g, :]) for g in range(4)], bank.free, t_o, t_li1)
                    t = self.V(lambda e, c=c, b=bank.at: e.tensor_tensor(y[:, c, :], y[:, c, :], ps[:, b, 0:D], ALU.add), t, t_yb)
                    bank.free = [t]
                    t_y.append(t)
                self.fence()
            li2, li3 = sb("li2", [P, FC, HID]), sb("li3", [P, HC, D])
            t_li2 = self.arrival(pre + "li2").dma(self.sp, li2[:, :, :], a[A + "li2_w"].rearrange("(f p) n -> p f n", p=P))
            t_li3 = self.arrival(pre + "li3").dma(self.sp, li3[:, :, :], a[A + "li3_w"].rearrange("(f p) n -> p f n", p=P))
            hT = sb("hT", [P, HC, T])
            done = self.normalize(y, core, NC, D, t_y, pre + "m")
            t_m = self.to_features(core, D, NC, done, affine("ln3_g", "ln3_b", self.xnT))
            for c in range(NC):
                t_1 = self.G(lambda e, c=c: e.tensor_tensor(y[:, c, :], y[:, c, :], xb[:, c, :], ALU.add), done[c])
                t_1 = self.G(lambda e, c=c: e.tensor_tensor(y[:, c, :], y[:, c, :], rows[:, 1, :], ALU.add), t_1)
            t_h = []
            for n in range(T // BANK):
                for m in range(HC):
                    bank = self.banks.next()
                    t = self.chain(ps[:, bank.at, :], [(li2[:, f, m * P:(m + 1) * P], self.xnT[:, f, n * BANK:(n + 1) * BANK]) for f in range(FC)],
                                   bank.free, t_li2, t_m)
                    t = self.A(lambda e, m=m, n=n, b=bank.at: e.activation(hT[:, m, n * BANK:(n + 1) * BANK], ps[:, b, :], ACT.Gelu,
                                                                          bias=vecs[A + "li2_b"][:, m:m + 1]), t, t_c)
                    bank.free = [t]
                t_h.append(t)
            out = []
            for c in range(NC):
                bank = self.banks.next()
                t = self.chain(ps[:, bank.at, 0:D], [(hT[:, m, c * P:(c + 1) * P], li3[:, m, :]) for m in range(HC)], bank.free, t_h[c // SC], t_li3)
                t = self.V(lambda e, c=c, b=bank.at: e.tensor_tensor(xb[:, c, :], y[:, c, :], ps[:, b, 0:D], ALU.add), t, t_1)
                bank.free = [t]
                out.append(t)
            self.fence()
        return out

    def scale_shift(self, tile, g, b, ready, t_gb):
        out = []
        for c in range(NC):
            t = self.G(lambda e, c=c: e.tensor_tensor(tile[:, c, :], tile[:, c, :], g, ALU.mult), ready[c], t_gb)
            out.append(self.G(lambda e, c=c: e.tensor_tensor(tile[:, c, :], tile[:, c, :], b, ALU.add), t))
        return out

    def double_attention(self):
        a = self.a
        with ExitStack() as mem:
            gb = self.sb("da_gb", [P, 4, D], F32, mem)
            arr = self.arrival("dagb")
            for i, n in enumerate(("ln1_g", "ln1_b", "ln2_g", "ln2_b")):
                t_gb = arr.dma(self.sp, gb[:, i, :], a["L1_xattn_" + n].partition_broadcast(P))
            xb = self.xn
            done = self.normalize(self.x, xb, NC, D, self.x_ready, "dax")
            done = self.normalize(xb, xb, NC, D, done, "da1")
            done = self.scale_shift(xb, gb[:, 0, :], gb[:, 1, :], done, t_gb)
            done = self.mha("a1", xb, done, False)
            done = self.normalize(xb, xb, NC, D, done, "da2")
            done = self.scale_shift(xb, gb[:, 2, :], gb[:, 3, :], done, t_gb)
            done = self.mha("a2", xb, done, True)
            self.x_ready = [self.G(lambda e, c=c: e.tensor_tensor(self.x[:, c, :], self.x[:, c, :], xb[:, c, :], ALU.add), done[c])
                            for c in range(NC)]
            self.fence()

    def swiglu(self):
        a, ps = self.a, self.ps
        with ExitStack() as mem:
            sb = lambda n, s, dt=F32: self.sb("sw_" + n, s, dt, mem)
            wr = sb("wr", [P, FC, E1])
            t_wr = self.arrival("swwr").dma(self.sp, wr[:, :, :], a["L1_ffn_w_router"].rearrange("(f p) e -> p f e", p=P))
            wring = Ring([(sb(f"wv{i}", [P, FC, 2 * HID]), sb(f"wp{i}", [P, HC, D]), self.arrival(f"sww{i}")) for i in range(2)])
            hT = Ring([sb(f"hT{i}", [P, HC, BANK]) for i in range(2)])
            gt = Ring([sb(f"gt{i}", [P, BANK]) for i in range(3)])
            pick = sb("pick", [P, NC, E1])
            iota_e = sb("iota_e", [P, E1])
            weights = {}

            def load(e):
                slot = wring.next()
                wv, wp, arr = slot.at
                arr.dma(self.sp, wv[:, :, :], a["L1_ffn_w_v"][e].rearrange("(f p) n -> p f n", p=P), slot.free)
                t = arr.dma(self.sp, wp[:, :, :], a["L1_ffn_w_proj"][e].rearrange("(f p) n -> p f n", p=P))
                weights[e] = (slot, wv, wp, t)
            load(0)
            load(1)
            self.norm_x()
            top, who, t = self.route(mem, "swr", wr, E1, None, t_wr)
            t_i = self.G(lambda e: e.iota(iota_e[:, :], pattern=[[1, E1]], base=0, channel_multiplier=0, allow_small_or_imprecise_dtypes=True))
            t_pick = self.V(lambda e: e.tensor_tensor(pick[:, :, :], iota_e[:, :].unsqueeze(1).broadcast_to([P, NC, E1]),
                                                      who[:, :, 0:1].broadcast_to([P, NC, E1]), ALU.is_equal), t, t_i)
            ready = [t_pick] * NC
            for x in range(E1):
                slot, wv, wp, t_w = weights[x]
                for n in range(T // BANK):
                    h = hT.next()
                    for m in range(HC):
                        gate, val = self.banks.next(), self.banks.next()
                        for bank, off in ((gate, 0), (val, HID)):
                            t = self.chain(ps[:, bank.at, :], [(wv[:, f, off + m * P:off + (m + 1) * P], self.xnT[:, f, n * BANK:(n + 1) * BANK])
                                                               for f in range(FC)], bank.free, t_w, self.xnT_ready)
                            if off == 0:
                                g = gt.next()
                                t_g = self.A(lambda e, g=g, b=bank.at: e.activation(g.at[:, :], ps[:, b, :], ACT.Silu), t, g.free)
                                gate.free = [t_g]
                        t_h = self.V(lambda e, g=g, m=m, h=h, b=val.at: e.tensor_tensor(h.at[:, m, :], g.at[:, :], ps[:, b, :], ALU.mult), t, t_g, h.free)
                        val.free, g.free = [t_h], [t_h]
                    for k in range(BANK // P):
                        c = n * (BANK // P) + k
                        bank = self.banks.next()
                        t = self.chain(ps[:, bank.at, 0:D], [(h.at[:, m, k * P:(k + 1) * P], wp[:, m, :]) for m in range(HC)], bank.free, t_h)
                        t1 = self.V(lambda e, c=c, b=bank.at, x=x: e.scalar_tensor_tensor(
                            self.x[:, c, :], ps[:, b, 0:D], pick[:, c, x:x + 1], self.x[:, c, :], ALU.mult, ALU.add), t, ready[c], self.x_ready[c])
                        ready[c] = t1
                        bank.free = [t1]
                    h.free = [t]
                slot.free = [t]
                if x + 2 < E1:
                    load(x + 2)
            self.x_ready = ready
            self.fence()


STAGE_FUNCTIONS = {0: Program.performer, 1: Program.cross_attention, 2: Program.moe, 3: Program.retention,
                   4: Program.double_attention, 5: Program.swiglu}


def build(nc, names, aps, out, stages):
    with ExitStack() as ctx:
        p = Program(nc, ctx, dict(zip(names, aps)), out, stages)
        block = ctx.enter_context(nc.Block())

        @block.sync
        def _(e):
            for f in p.sp.items:
                f(e)

        @block.tensor
        def _(e):
            for f in p.pe.items:
                f(e)

        @block.scalar
        def _(e):
            for f in p.act.items:
                f(e)

        @block.vector
        def _(e):
            for f in p.dve.items:
                f(e)

        @block.gpsimd
        def _(e):
            for f in p.pool.items:
                f(e)
    return p


NAMES = ["x", "ctx_512"] + ["L0_attn_" + n for n in ("Wq", "Wk", "Wv", "Wo", "bo", "P")] \
    + ["L0_xattn_" + n for n in ("Wk", "bk", "Wq", "bq", "Wv", "bv", "Wck", "bck", "Wcq", "bcq", "Wcv", "bcv", "Wp", "bp")] \
    + ["L0_ffn_" + n for n in ("Wr", "br", "W1", "b1", "W2", "b2")] \
    + ["L1_attn_" + n for n in ("W_qkv", "W_o", "log_gamma")] \
    + ["L1_xattn_" + n for n in ("ln1_g", "ln1_b", "ln2_g", "ln2_b")] \
    + [f"L1_xattn_{a}_{n}" for a in ("a1", "a2") for n in (
        "wq", "wk", "wv", "li1_w", "li1_b", "lnx_g", "lnx_b", "lny_g", "lny_b", "ln3_g", "ln3_b",
        "li2_w", "li2_b", "li3_w", "li3_b")] \
    + ["L1_ffn_" + n for n in ("w_router", "w_v", "w_proj")]

STAGES = (0, 1, 2, 3, 4, 5)


def kernel(**inputs):
    import concourse.bacc as bacc
    from concourse.bass_utils import run_bass_kernel_spmd as run

    nc = bacc.Bacc("TRN2", target_bir_lowering=False, num_devices=1)
    arrays, aps = {}, []
    for name in NAMES:
        v = np.ascontiguousarray(inputs[name])
        arrays["in_" + name] = v
        aps.append(nc.dram_tensor("in_" + name, v.shape, mybir.dt.from_np(v.dtype), kind="ExternalInput").ap())
    out = nc.dram_tensor("out_0", (B, S, D), F32, kind="ExternalOutput").ap()
    build(nc, NAMES, aps, out, STAGES)
    r = run(nc, [arrays], core_ids=[0])
    return np.asarray(r.results[0]["out_0"])
```

```python
from contextlib import ExitStack

import numpy as np

import concourse.bass as bass
from concourse import mybir

F32 = mybir.dt.float32
BF16 = mybir.dt.bfloat16
U32 = mybir.dt.uint32
I32 = mybir.dt.int32
ALU = mybir.AluOpType
ACT = mybir.ActivationFunctionType
AX = mybir.AxisListType

P = 128
B, S, D = 2, 512, 256
T = B * S
NC = T // P
SC = S // P
FC = D // P
MEM, CW = 1024, 128
TM = B * MEM
MC = TM // P
H = 16
LN_EPS = 1e-5
PH, PM = 64, 64
PAIRS = H * PH // P
DN = PH ** -0.25
KEPS = 1e-4
E0, HID = 8, 1024
CAP = -(-12 * T // (10 * E0))
E1 = 4
HC = HID // P
NEG = -1e30
BANK = 512


class Lane:

    def __init__(self, name, sem):
        self.name, self.sem, self.count, self.items, self.seen = name, sem, 0, [], {}

    def wait(self, *tickets):
        for t in tickets:
            if t is None:
                continue
            if isinstance(t, list):
                self.wait(*t)
                continue
            sem, value = t
            if self.seen.get(id(sem), 0) < value:
                self.seen[id(sem)] = value
                self.items.append(lambda e, s=sem, v=value: e.wait_ge(s, v))

    def do(self, make, *tickets, tick=True):
        self.wait(*tickets)
        if not tick:
            self.items.append(lambda e: make(e))
            return None
        self.count += 1
        self.items.append(lambda e: make(e).then_inc(self.sem, 1))
        return (self.sem, self.count)

    def last(self):
        return (self.sem, self.count) if self.count else None


class Arrival:

    def __init__(self, sem):
        self.sem, self.count = sem, 0

    def dma(self, lane, out, in_, *tickets):
        lane.wait(*tickets)
        self.count += 16
        lane.items.append(lambda e: e.dma_start(out, in_).then_inc(self.sem, 16))
        return (self.sem, self.count)


class Slot:

    def __init__(self, at):
        self.at, self.free = at, []


class Ring:
    def __init__(self, slots):
        self.slots, self.n = [Slot(s) for s in slots], 0

    def next(self):
        s = self.slots[self.n % len(self.slots)]
        self.n += 1
        return s


class Program:
    def __init__(self, nc, ctx, a, out, stages):
        self.nc, self.ctx, self.a, self.out = nc, ctx, a, out
        self.nsem = 0
        self.pe, self.act, self.dve, self.pool, self.sp = (
            Lane(n, self.sem("s_" + n)) for n in ("pe", "act", "dve", "pool", "sp"))
        self.lanes = [self.pe, self.act, self.dve, self.pool]
        self.arrivals = []
        self.ps = ctx.enter_context(nc.psum_tensor("psum", [P, 8, BANK], F32))
        self.banks = Ring(range(8))
        self.stages = stages
        self.build()

    def sem(self, name):
        self.nsem += 1
        return self.ctx.enter_context(self.nc.semaphore(name))

    def arrival(self, name):
        s = Arrival(self.sem("d_" + name))
        self.arrivals.append(s)
        return s

    def sb(self, name, shape, dt=F32, ctx=None):
        return (ctx or self.ctx).enter_context(self.nc.sbuf_tensor(name, shape, dt))

    def fence(self, *tickets):
        last = [l.last() for l in self.lanes]
        for l in self.lanes + [self.sp]:
            l.wait(*last, *tickets)

    def chain(self, out, terms, *tickets, tick=True):
        self.pe.wait(*tickets)
        for i, (l, r) in enumerate(terms):
            end = i == len(terms) - 1
            t = self.pe.do(lambda e, l=l, r=r, i=i, end=end: e.matmul(out, l, r, start=i == 0, stop=end),
                           tick=tick and end)
        return t

    def V(self, make, *tickets):
        return self.dve.do(make, *tickets)

    def A(self, make, *tickets):
        return self.act.do(make, *tickets)

    def G(self, make, *tickets):
        return self.pool.do(make, self.pool.last(), *tickets)

    def copy(self, lane, out, in_, *tickets):
        if lane is self.act:
            return lane.do(lambda e: e.activation(out, in_, ACT.Copy), *tickets)
        return lane.do(lambda e: e.tensor_copy(out, in_), *tickets)

    def constants(self):
        z = self.sb("ident", [P, P])
        self.ident = z
        t = self.G(lambda e: e.memset(z[:, :], 0.0))
        t = self.G(lambda e: e.affine_select(out=z[:, :], in_=z[:, :], compare_op=ALU.not_equal, fill=1.0, base=0,
                                             pattern=[[-1, P]], channel_multiplier=1), t)
        self.t_ident = t
        self.ones = self.sb("ones", [P, P])
        self.t_ones = self.G(lambda e: e.memset(self.ones[:, :], 1.0))
        self.identb = self.sb("identb", [P, P], BF16)
        t_b = self.G(lambda e: e.tensor_copy(self.identb[:, :], z[:, :]), t)
        mf = self.sb("maskf", [P, 2, P])
        self.mask_qk = self.sb("mask_qk", [P, P], BF16)
        self.mask_kq = self.sb("mask_kq", [P, P], BF16)
        t = self.G(lambda e: e.memset(mf[:, :, :], 0.0))
        t1 = self.G(lambda e: e.affine_select(out=mf[:, 0, :], in_=mf[:, 0, :], compare_op=ALU.is_ge, fill=NEG,
                                              base=0, pattern=[[-1, P]], channel_multiplier=1), t)
        t2 = self.G(lambda e: e.affine_select(out=mf[:, 1, :], in_=mf[:, 1, :], compare_op=ALU.is_ge, fill=NEG,
                                              base=0, pattern=[[1, P]], channel_multiplier=-1), t)
        self.G(lambda e: e.tensor_copy(self.mask_qk[:, :], mf[:, 0, :]), t1)
        self.t_const = self.G(lambda e: e.tensor_copy(self.mask_kq[:, :], mf[:, 1, :]), t2)

    def normalize(self, src, dst, chunks, after, gain=None, shift=None, t_gb=None):
        raw, agg, std = self.ln_raw, self.ln_agg, self.ln_std
        self.dve.wait(*self.ln_free)
        groups = [slice(c, c + 4) for c in range(0, chunks, 4)]
        roots, done = [], []
        for g in groups:
            for c in range(g.start, g.stop):
                t = self.V(lambda e, c=c: e.bn_stats(raw[:, c, :], src[:, c, :]), after[c])
            for c in range(g.start, g.stop):
                t = self.V(lambda e, c=c: e.bn_aggr(agg[:, c, :], raw[:, c, :]), t if c == g.start else None)
            t = self.V(lambda e, g=g: e.tensor_scalar(std[:, g, 0], agg[:, g, 1], LN_EPS, None, ALU.add), t)
            roots.append(self.A(lambda e, g=g: e.activation(std[:, g, 1], std[:, g, 0], ACT.Sqrt), t))
        for g, root in zip(groups, roots):
            t = self.V(lambda e, g=g: e.reciprocal(std[:, g, 0], std[:, g, 1]), root)
            for c in range(g.start, g.stop):
                if gain is None:
                    done.append(self.V(lambda e, c=c: e.tensor_scalar(dst[:, c, :], src[:, c, :], agg[:, c, 0:1], std[:, c, 0:1],
                                                                      ALU.subtract, ALU.mult), t))
                    continue
                t1 = self.V(lambda e, c=c: e.scalar_tensor_tensor(dst[:, c, :], src[:, c, :], agg[:, c, 0:1], gain, ALU.subtract, ALU.mult), t, t_gb)
                done.append(self.V(lambda e, c=c: e.scalar_tensor_tensor(dst[:, c, :], dst[:, c, :], std[:, c, 0:1], shift, ALU.mult, ALU.add), t1))
        self.ln_free = [done[-1]]
        return done

    def to_features(self, src, width, chunks, ready, emit):
        out = []
        for n in range(chunks // 4):
            for f in range(width // P):
                bank = self.banks.next()
                self.pe.wait(*bank.free, self.t_ident)
                for k in range(4):
                    c = 4 * n + k
                    t = self.pe.do(lambda e, k=k, c=c, f=f, b=bank.at: e.transpose(
                        self.ps[:, b, k * P:(k + 1) * P], src[:, c, f * P:(f + 1) * P], self.ident[:, :]),
                        ready[c], tick=k == 3)
                t = emit(f, n, self.ps[:, bank.at, :], t)
                bank.free = [t]
                out.append(t)
        return out

    def feature_copy(self, dst):
        def emit(f, n, view, t):
            lane = self.act if (f + n) % 2 == 0 else self.dve
            return self.copy(lane, dst[:, f, n * BANK:(n + 1) * BANK], view, t)
        return emit

    def build(self):
        nc, a = self.nc, self.a
        self.ln_free, self.unsent = [], None
        self.ln_raw = self.sb("ln_raw", [P, MC, 6])
        self.ln_agg = self.sb("ln_agg", [P, MC, 2])
        self.ln_std = self.sb("ln_std", [P, MC, 2])
        self.constants()
        self.x = self.sb("x", [P, NC, D])
        self.xn = self.sb("xn", [P, NC, D])
        self.xnT = self.sb("xnT", [P, FC, T])
        self.ctxT = self.sb("ctxT", [P, TM])
        d_x = self.arrival("x")
        xin = a["x"].rearrange("b (c p) d -> p (b c) d", p=P)
        d_xs = [self.arrival(f"x{i}") for i in range(2)]
        t_x = [d_xs[i].dma(self.sp, self.x[:, 4 * i:4 * i + 4, :], xin[:, 4 * i:4 * i + 4, :]) for i in range(2)]
        self.x_ready = [t_x[c // 4] for c in range(NC)]
        for s in self.stages:
            STAGE_FUNCTIONS[s](self)
        d_out = self.arrival("out")
        yout = self.out.rearrange("b (c p) d -> p (b c) d", p=P)
        self.t_out = d_out.dma(self.sp, yout, self.x[:, :, :], *self.x_ready)
        self.sp.wait(self.t_out)
        for d in self.arrivals:
            if d.count:
                self.sp.wait((d.sem, d.count))

    def norm_x(self):
        done = self.normalize(self.x, self.xn, NC, self.x_ready)
        t = self.to_features(self.xn, D, NC, done, self.feature_copy(self.xnT))
        self.xn_ready = done
        self.xnT_ready = t

    def performer(self):
        a, ps = self.a, self.ps
        with ExitStack() as mem:
            sb = lambda n, s, dt=F32: self.sb("pf_" + n, s, dt, mem)
            wq, wk, wv = (sb(n, [P, FC, H * PH]) for n in ("wq", "wk", "wv"))
            wo = sb("wo", [P, PAIRS, D])
            praw = sb("praw", [P, P])
            pbd = sb("pbd", [P, P])
            half = sb("half", [P, 2])
            bo = sb("bo", [P, D])
            kdd = sb("kdd", [P, PAIRS, NC, P])
            diag = sb("diag", [P, 2, PAIRS, NC, 2])
            kmax = sb("kmax", [P, 2 * PAIRS])
            gm = sb("gm", [P, 4])
            headT = Ring([sb(f"hT{i}", [P, T]) for i in range(2)])
            sq = Ring([sb(f"sq{i}", [P, T]) for i in range(2)])
            qp = Ring([sb(f"qp{i}", [P, NC, P]) for i in range(3)])
            qpT = Ring([sb(f"qpT{i}", [P, T]) for i in range(2)])
            vv = Ring([sb(f"v{i}", [P, NC, 2, PH + 1]) for i in range(2)])
            rden = Ring([sb(f"rd{i}", [P, 2, 2]) for i in range(4)])
            qmx = Ring([sb(f"qmx{i}", [P, NC, 2]) for i in range(2)])
            bd = Ring([sb(f"bd{i}", [P, 2, PH + 1]) for i in range(4)])
            loads = {}
            for n, tile, src in (("k", wk, "L0_attn_Wk"), ("q", wq, "L0_attn_Wq"), ("v", wv, "L0_attn_Wv")):
                loads[n] = self.arrival("pf" + n).dma(self.sp, tile[:, :, :], a[src].rearrange("(f p) n -> p f n", p=P))
            t_z = self.G(lambda e: e.memset(praw[:, :], 0.0))
            d_p = self.arrival("pfp")
            for j in range(2):
                t_p = d_p.dma(self.sp, praw[64 * j:64 * j + 64, 64 * j:64 * j + 64], a["L0_attn_P"], t_z)
            t_bo = self.arrival("pfbo").dma(self.sp, bo[:, :], a["L0_attn_bo"].partition_broadcast(P))
            t_wo = self.arrival("pfwo").dma(self.sp, wo[:, :, :], a["L0_attn_Wo"].rearrange("(f p) n -> p f n", p=P))
            t_h = self.G(lambda e: e.memset(half[:, :], 0.0))
            for j in range(2):
                t_h = self.G(lambda e, j=j: e.memset(half[64 * j:64 * j + 64, j:j + 1], 0.5 * DN * DN), t_h)
            for s in bd.slots:
                s.free = [self.G(lambda e, s=s: e.memset(s.at[:, :, :], 0.0))]
            for s in vv.slots:
                s.free = [self.G(lambda e, s=s: e.memset(s.at[:, :, :, PH:PH + 1], 1.0))]
            bank = self.banks.next()
            t = self.pe.do(lambda e, b=bank.at: e.transpose(ps[:, b, 0:P], praw[:, :], self.ident[:, :]), t_p, self.t_ident)
            t_pbd = self.copy(self.act, pbd[:, :], ps[:, bank.at, 0:P], t)
            bank.free = [t_pbd]

            self.norm_x()
            t_xb = None
            for c in range(NC):
                t_xb = self.G(lambda e, c=c: e.tensor_tensor(self.x[:, c, :], self.x[:, c, :], bo[:, :], ALU.add),
                              self.xn_ready[-1], t_bo)

            def head_projection(w, pair, t_w):
                hT, s2 = headT.next(), sq.next()
                t_hT, t_sq = [], []
                for n in range(T // BANK):
                    bank = self.banks.next()
                    t = self.chain(ps[:, bank.at, :], [(w[:, f, pair * P:(pair + 1) * P], self.xnT[:, f, n * BANK:(n + 1) * BANK])
                                                       for f in range(FC)], bank.free, t_w, self.xnT_ready)
                    cols = slice(n * BANK, (n + 1) * BANK)
                    t1 = self.A(lambda e, b=bank.at, cols=cols: e.activation(hT.at[:, cols], ps[:, b, :], ACT.Copy), t, hT.free)
                    t2 = self.A(lambda e, b=bank.at, cols=cols: e.activation(s2.at[:, cols], ps[:, b, :], ACT.Square), t, s2.free)
                    bank.free = [t2]
                    t_hT.append(t1)
                    t_sq.append(t2)
                return pair, hT, s2, t_hT, t_sq

            def head_features(projection, which):
                pair, hT, s2, t_hT, t_sq = projection
                res = []
                for n in range(2):
                    bank = self.banks.next()
                    for k in range(4):
                        c = 4 * n + k
                        t = self.chain(ps[:, bank.at, k * P:(k + 1) * P], [(hT.at[:, c * P:(c + 1) * P], pbd[:, :])],
                                       bank.free, t_hT[n], t_pbd, tick=k == 3)
                    res.append((bank, t))
                hT.free = [t]
                bank = self.banks.next()
                for c in range(NC):
                    t = self.chain(ps[:, bank.at, 2 * c:2 * c + 2], [(s2.at[:, c * P:(c + 1) * P], half[:, :])],
                                   bank.free, t_sq[c // 4], t_h, tick=c == NC - 1)
                s2.free = [t]
                t_d = self.V(lambda e, b=bank.at: e.tensor_copy(diag[:, which, pair, :, :],
                                                                ps[:, b, 0:2 * NC].rearrange("p (c h) -> p c h", h=2)), t)
                bank.free = [t_d]
                return res, t_d

            heads_of = lambda v: v.rearrange("p c (h m) -> p (c h) m", h=2)
            t_kd, t_kp, queries, values, outputs = [], {}, {}, {}, {}

            def keys(projection):
                pair = projection[0]
                res, t_d = head_features(projection, 1)
                for n, (bank, t) in enumerate(res):
                    t1 = self.V(lambda e, b=bank.at, i=2 * pair + n: e.tensor_reduce(kmax[:, i:i + 1], ps[:, b, :], AX.X, ALU.max), t)
                    t2 = self.A(lambda e, b=bank.at, n=n: e.activation(
                        kdd[:, pair, 4 * n:4 * n + 4, :], ps[:, b, :].rearrange("p (c m) -> p c m", c=4), ACT.Copy), t, t1)
                    bank.free = [t2]
                t_kd.append([t2, t_d])
                return t1

            def key_exp(pair):
                kv = heads_of(kdd[:, pair, :, :])
                kb = diag[:, 1, pair, :, :].rearrange("p c h -> p (c h)")
                t = self.V(lambda e: e.tensor_scalar(kb, kb, gm[:, 2:3], None, ALU.add), t_gm, t_kd[pair])
                t = self.V(lambda e: e.scalar_tensor_tensor(
                    kv, kv, DN, kb.unsqueeze(2).broadcast_to([P, 2 * NC, PM]), ALU.mult, ALU.subtract), t)
                t = self.A(lambda e: e.activation(kdd[:, pair, :, :], kdd[:, pair, :, :], ACT.Exp), t)
                t_kp[pair] = self.G(lambda e: e.tensor_scalar(kdd[:, pair, :, :], kdd[:, pair, :, :], KEPS, None, ALU.add), t)

            def query_exp(projection):
                res, t_d = head_features(projection, 0)
                pair = projection[0]
                mx, q = qmx.next(), qp.next()
                t_e = []
                for n, (bank, t) in enumerate(res):
                    view = ps[:, bank.at, :].rearrange("p (c m) -> p c m", m=PM)
                    mview = mx.at[:, 4 * n:4 * n + 4, :].rearrange("p c h -> p (c h)")
                    dview = diag[:, 0, pair, 4 * n:4 * n + 4, :].rearrange("p c h -> p (c h)")
                    t1 = self.V(lambda e, m=mview, v=view: e.tensor_reduce(m, v, AX.X, ALU.max), t, mx.free)
                    t1 = self.V(lambda e, m=mview, d=dview: e.scalar_tensor_tensor(m, m, DN, d, ALU.mult, ALU.add), t1, t_d)
                    qv = heads_of(q.at[:, 4 * n:4 * n + 4, :])
                    t1 = self.V(lambda e, m=mview, v=view, qv=qv: e.scalar_tensor_tensor(
                        qv, v, DN, m.unsqueeze(2).broadcast_to([P, 8, PM]), ALU.mult, ALU.subtract), t1, q.free)
                    bank.free = [t1]
                    t_e.append(t1)
                mx.free = [t1]
                t = self.A(lambda e: e.activation(q.at[:, :, :], q.at[:, :, :], ACT.Exp), t_e)
                t_qp = self.G(lambda e: e.tensor_scalar(q.at[:, :, :], q.at[:, :, :], KEPS, None, ALU.add), t)
                queries[pair] = q, t_qp

            def value_projection(pair):
                v = vv.next()
                t_v = []
                for n in range(2):
                    bank = self.banks.next()
                    for k in range(4):
                        c = 4 * n + k
                        t = self.chain(ps[:, bank.at, k * P:(k + 1) * P],
                                       [(self.xnT[:, f, c * P:(c + 1) * P], wv[:, f, pair * P:(pair + 1) * P]) for f in range(FC)],
                                       bank.free, loads["v"], self.xnT_ready, tick=k == 3)
                    t = self.A(lambda e, n=n, b=bank.at: e.activation(
                        v.at[:, 4 * n:4 * n + 4, :, 0:PH], ps[:, b, :].rearrange("p (c h m) -> p c h m", c=4, h=2), ACT.Copy), t, v.free)
                    bank.free = [t]
                    t_v.append(t)
                values[pair] = v, t_v

            def contexts(pair):
                v, t_v = values[pair]
                bank = self.banks.next()
                W = 2 * (PH + 1)
                for b in range(B):
                    t = self.chain(ps[:, bank.at, b * W:(b + 1) * W],
                                   [(kdd[:, pair, c, :], v.at[:, c, :, :].rearrange("p h m -> p (h m)")) for c in range(SC * b, SC * b + SC)],
                                   bank.free, t_kp[pair], t_v, tick=b == B - 1)
                v.free = [t]
                blks = []
                for b in range(B):
                    blk = bd.next()
                    for j in range(2):
                        r = slice(64 * j, 64 * j + 64)
                        o = b * W + j * (PH + 1)
                        t_b = self.V(lambda e, r=r, blk=blk, j=j, o=o: e.tensor_copy(blk.at[r, j, :], ps[r, bank.at, o:o + PH + 1]), t, blk.free)
                    blks.append(blk)
                bank.free = [t_b]
                return blks, t_b

            def turn_queries(pair):
                q, t_qp = queries[pair]
                qT = qpT.next()
                t_qT = self.to_features(q.at, P, NC, [t_qp] * NC, lambda f, n, view, t: self.copy(
                    self.act if n else self.dve, qT.at[:, n * BANK:(n + 1) * BANK], view, t, qT.free))
                q.free = list(t_qT)
                return qT, t_qT

            def output(pair, blks, t_b, qT, t_qT):
                y = queries[pair][0]
                ready = []
                for n in range(NC // 2):
                    bank = self.banks.next()
                    view = ps[:, bank.at, 0:4 * (PH + 1)].rearrange("p (c h m) -> p c h m", c=2, h=2)
                    blk = blks[2 * n // SC]
                    for k in range(2):
                        c = 2 * n + k
                        t = self.chain(view[:, k, :, :].rearrange("p h m -> p (h m)"),
                                       [(qT.at[:, c * P:(c + 1) * P], blk.at[:, :, :].rearrange("p h m -> p (h m)"))],
                                       bank.free, t_b, t_qT, tick=k == 1)
                    blk.free = [t]
                    rd = rden.next()
                    t1 = self.V(lambda e, rd=rd, view=view: e.reciprocal(rd.at[:, :, :], view[:, :, :, PH]), t, rd.free)
                    t1 = self.V(lambda e, rd=rd, view=view, n=n: e.tensor_tensor(
                        y.at[:, 2 * n:2 * n + 2, :].rearrange("p c (h m) -> p c h m", h=2), view[:, :, :, 0:PH],
                        rd.at[:, :, :].unsqueeze(3).broadcast_to([P, 2, 2, PH]), ALU.mult), t1, y.free)
                    bank.free, rd.free = [t1], [t1]
                    ready += [t1, t1]
                qT.free = [t]
                outputs[pair] = y, ready

            t_y = []

            def turn_output(pair):
                y, ready = outputs[pair]
                yT = kdd[:, pair, :, :].rearrange("p c m -> p (c m)")
                t = self.to_features(y.at, P, NC, ready, lambda f, n, view, t: self.copy(
                    self.act if n else self.dve, yT[:, n * BANK:(n + 1) * BANK], view, t))
                y.free = list(t)
                t_y.extend(t)

            ahead = head_projection(wk, 0, loads["k"])
            for pair in range(PAIRS):
                now = ahead
                ahead = head_projection(wk, pair + 1, loads["k"]) if pair + 1 < PAIRS else head_projection(wq, 0, loads["q"])
                t_mx = keys(now)
            value_projection(0)
            t = self.V(lambda e: e.tensor_reduce(gm[:, 0:1], kmax[:, :], AX.X, ALU.max), t_mx)
            bank = self.banks.next()
            t = self.pe.do(lambda e, b=bank.at: e.transpose(ps[0:1, b, 0:P], gm[:, 0:1], self.ident[:, :]), t, bank.free)
            t = self.V(lambda e, b=bank.at: e.tensor_reduce(gm[0:1, 1:2], ps[0:1, b, 0:P], AX.X, ALU.max), t)
            t = self.chain(ps[:, bank.at, 0:1], [(self.ones[0:1, :], gm[0:1, 1:2])], t, self.t_ones)
            t_gm = self.V(lambda e, b=bank.at: e.tensor_scalar(gm[:, 2:3], ps[:, b, 0:1], DN, None, ALU.mult), t)
            bank.free = [t_gm]
            key_exp(0)
            now, ahead = ahead, head_projection(wq, 1, loads["q"])
            query_exp(now)
            for pair in range(PAIRS):
                if pair + 1 < PAIRS:
                    key_exp(pair + 1)
                    now = ahead
                    if pair + 2 < PAIRS:
                        ahead = head_projection(wq, pair + 2, loads["q"])
                    query_exp(now)
                blks, t_b = contexts(pair)
                if pair:
                    turn_output(pair - 1)
                qT, t_qT = turn_queries(pair)
                if pair + 1 < PAIRS:
                    value_projection(pair + 1)
                output(pair, blks, t_b, qT, t_qT)
            turn_output(PAIRS - 1)
            self.x_ready = []
            for c in range(NC):
                bank = self.banks.next()
                t = self.chain(ps[:, bank.at, 0:D], [(kdd[:, p, c, :], wo[:, p, :]) for p in range(PAIRS)], bank.free, t_y, t_wo)
                t = self.V(lambda e, c=c, b=bank.at: e.tensor_tensor(self.x[:, c, :], self.x[:, c, :], ps[:, b, 0:D], ALU.add), t, t_xb)
                bank.free = [t]
                self.x_ready.append(t)
            self.fence()

    def columns(self, mem, tag, names):
        sizes = [int(np.prod(self.a[n].shape)) // P for n in names]
        total = sum(sizes)
        rows = self.sb(tag + "_rows", [total, P], F32, mem)
        cols = self.sb(tag + "_cols", [P, total], F32, mem)
        arr = self.arrival(tag + "_cols")
        at, views = 0, {}
        for n, k in zip(names, sizes):
            src = self.a[n] if len(self.a[n].shape) == 1 else self.a[n].rearrange("e n -> (e n)")
            t = arr.dma(self.sp, rows[at:at + k, :], src.rearrange("(k p) -> k p", p=P))
            views[n] = cols[:, at:at + k]
            at += k
        bank = self.banks.next()
        t = self.pe.do(lambda e: e.transpose(self.ps[:, bank.at, 0:total], rows[:, :], self.ident[0:total, 0:total]),
                       t, bank.free, self.t_ident)
        t = self.copy(self.act, cols[:, :], self.ps[:, bank.at, 0:total], t)
        bank.free = [t]
        return views, t

    PARTS16 = [([(0, 0), (0, 1), (1, 0), (0, 2), (2, 0), (1, 1)], 96)]
    PARTS32 = [([(0, 0), (0, 1), (1, 0), (1, 1)], None), ([(0, 2), (2, 0)], 64)]

    def scratch(self, name, feats, tokens):
        return self.nc.dram_tensor("scratch_" + name, (3, feats, tokens), BF16).ap()

    def parts_out(self, mem, tag, shared=True):
        self.sent, self.shared = 0, shared
        return Ring([(self.sb(f"{tag}_t{i}", [P, BANK], F32, mem), self.sb(f"{tag}_p{i}", [P, 3, BANK], BF16, mem),
                      self.arrival(f"{tag}_w{i}")) for i in range(4)])

    def send_parts(self, ring, view, bias, t, dram, f, n):
        slot = ring.next()
        rest, parts, arr = slot.at
        if bias is None:
            t = self.A(lambda e: e.activation(parts[:, 0, :], view, ACT.Copy), t, slot.free)
            t_read = self.V(lambda e: e.tensor_tensor(rest[:, :], view, parts[:, 0, :], ALU.subtract), t)
        else:
            t = self.A(lambda e: e.activation(parts[:, 0, :], view, ACT.Identity, bias=bias), t, slot.free)
            t_read = self.V(lambda e: e.scalar_tensor_tensor(rest[:, :], view, bias, parts[:, 0, :], ALU.add, ALU.subtract), t)
        self.flush_parts()
        sent = []

        def second_half():
            t = self.A(lambda e: e.activation(parts[:, 1, :], rest[:, :], ACT.Copy), t_read)
            lane = self.G if self.shared and self.sent % 2 else self.V
            self.sent += 1
            t = lane(lambda e: e.tensor_tensor(parts[:, 2, :], rest[:, :], parts[:, 1, :], ALU.subtract), t)
            t = arr.dma(self.sp, dram[:, f * P:(f + 1) * P, n * BANK:(n + 1) * BANK].rearrange("s p t -> p s t"), parts[:, :, :], t)
            slot.free = [t]
            sent.append(t)
        self.unsent = second_half
        return sent, t_read

    def flush_parts(self):
        if self.unsent:
            half, self.unsent = self.unsent, None
            half()

    def project_parts(self, ring, w, fs, rhs, t_w, t_in, bias, dram, tokens, feats):
        done = {}
        for n in range(tokens // BANK):
            for m in range(feats // P):
                bank = self.banks.next()
                t = self.chain(self.ps[:, bank.at, :], [(w[:, f, m * P:(m + 1) * P], rhs(f, n)) for f in range(fs)],
                               bank.free, t_w, t_in)
                done[m, n], t_read = self.send_parts(ring, self.ps[:, bank.at, :], None if bias is None else bias[:, m:m + 1], t, dram, m, n)
                bank.free = [t_read]
        return done

    def attend(self, tag, jobs, d, scale, mem, kmax, softmax=True, nbuf=3):
        ps, pe = self.ps, self.pe
        spec = self.PARTS16 if d == 16 else self.PARTS32
        sets = []
        for i in range(nbuf):
            qs = [self.sb(f"{tag}_qs{i}{u}", [P, 4, S], BF16, mem) for u in range(len(spec))]
            ks = [self.sb(f"{tag}_ks{i}{u}", [P, 4, kmax], BF16, mem) for u in range(len(spec))]
            nm = self.sb(f"{tag}_nm{i}", [P, 4, 4], F32, mem)
            nt = self.sb(f"{tag}_nt{i}", [P, 4, 4], F32, mem)
            np_ = self.sb(f"{tag}_np{i}", [P, 4, 4, 3], BF16, mem)
            nmT = self.sb(f"{tag}_nmT{i}", [12, S], BF16, mem)
            st = dict(qs=qs, ks=ks, nm=nm, nt=nt, np=np_, nmT=nmT, arr=self.arrival(f"{tag}_l{i}"), arm=self.arrival(f"{tag}_m{i}"),
                      free=[], t_one=None)
            if softmax:
                for u, (pairs, row) in enumerate(spec):
                    if row is not None:
                        st["t_one"] = self.G(lambda e, k=ks[u], row=row: e.memset(k[row:row + 3, :, :], 1.0))
            sets.append(st)
        def settle(job, t_end):
            r = raws.next()
            acc = job["acc"]
            t_raw = self.A(lambda e: e.activation(r.at[:, :], ps[:, acc.at, :], ACT.Copy), t_end, r.free)
            acc.free = [t_raw]
            if not softmax:
                r.free = [job["done"](job, r.at, t_raw, None, None)]
                return
            dn, t_dn = r, t_raw
            if d == 32:
                dn = dens.next()
                t_dn = self.V(lambda e: e.tensor_copy(dn.at[:, :], ps[:, 7, :]), t_end, dn.free)
                acc.free = [t_raw, t_dn]
            yield
            pr = pairs_ring.next()
            for i in range(SC):
                t = self.chain(ps[:, pr.at, 4 * i:4 * i + 4], [(dn.at[:, i * P:(i + 1) * P], pick[:, :])], t_dn, t_pick, pr.free, tick=i == SC - 1)
            rc = rec.next()
            small, wide = rc.at
            t_rc = self.V(lambda e: e.reciprocal(small[:, :], ps[:, pr.at, 0:4 * SC]), t, rc.free)
            pr.free = [t_rc]
            t_rc = self.V(lambda e: e.tensor_copy(wide[:, :, :], small[:, :].unsqueeze(2).broadcast_to([P, 4 * SC, 32])), t_rc)
            if dn is not r:
                dn.free = [t]
            yield
            pb = pairs_ring.next()
            for i in range(SC):
                t = self.chain(ps[:, pb.at, i * P:(i + 1) * P],
                               [(wide[:, 4 * i:4 * i + 4, :].rearrange("p h r -> p (h r)"), self.ident[:, :])], t_rc, pb.free, tick=i == SC - 1)
            rc.free = [t]
            t = job["done"](job, r.at, t_raw, ps[:, pb.at, :], [t, t_raw])
            pb.free, r.free = [t], [t]

        def load(n):
            job, st = jobs[n], sets[n % nbuf]
            arr = st["arr"]
            self.sp.wait(st["free"], job["ready"])
            for u, (pairs, row) in enumerate(spec):
                for i, (qp, kp) in enumerate(pairs):
                    for (dram, first), part, tile, width in ((job["q"], qp, st["qs"][u], S), (job["k"], kp, st["ks"][u], job["keys"])):
                        src = dram[part, job["rows"]:job["rows"] + 4 * d, first:first + width].rearrange("(h i) t -> i h t", h=4)
                        t = arr.dma(self.sp, tile[i * d:(i + 1) * d, :, 0:width], src)
            st["loaded"] = t

        def pass1(n):
            job, st = jobs[n], sets[n % nbuf]
            pairs = spec[0][0]
            K = len(pairs) * d
            q, k = st["qs"][0], st["ks"][0]
            t_r = None
            for i in range(SC):
                if job["mode"] == "causal":
                    for jj in range(2):
                        pr = pairs_ring.next()
                        N = (i + 1) * P
                        for j in range(2):
                            h = 2 * jj + j
                            pe.do(lambda e, h=h, b=pr.at + j, i=i, N=N: e.matmul(
                                ps[:, b, 0:N], q[0:K, h, i * P:(i + 1) * P], k[0:K, h, 0:N], start=True, stop=False),
                                pr.free, st["loaded"], tick=False)
                            t = pe.do(lambda e, b=pr.at + j, i=i, N=N: e.matmul(
                                ps[:, b, N - P:N], self.identb[:, :], self.mask_qk[:, :], start=False, stop=True),
                                self.t_const, tick=j == 1)
                        t_r = self.V(lambda e, b=pr.at, i=i, jj=jj, N=N: e.tensor_reduce(
                            st["nm"][:, i, 2 * jj:2 * jj + 2], ps[:, b:b + 2, 0:N], AX.X, ALU.max, negate=True), t, st.get("nm_free"))
                        pr.free = [t_r]
                        yield
                elif job["keys"] == S:
                    for jj in range(2):
                        pr = pairs_ring.next()
                        for j in range(2):
                            t = pe.do(lambda e, h=2 * jj + j, b=pr.at + j, i=i: e.matmul(
                                ps[:, b, :], q[0:K, h, i * P:(i + 1) * P], k[0:K, h, 0:S], start=True, stop=True),
                                pr.free, st["loaded"], tick=j == 1)
                        t_r = self.V(lambda e, b=pr.at, i=i, jj=jj: e.tensor_reduce(
                            st["nm"][:, i, 2 * jj:2 * jj + 2], ps[:, b:b + 2, :], AX.X, ALU.max, negate=True), t, st.get("nm_free"))
                        pr.free = [t_r]
                        yield
                else:
                    for h in range(4):
                        pr = pairs_ring.next()
                        for j in range(2):
                            t = pe.do(lambda e, h=h, j=j, b=pr.at + j, i=i: e.matmul(
                                ps[:, b, :], q[0:K, h, i * P:(i + 1) * P], k[0:K, h, j * S:(j + 1) * S], start=True, stop=True),
                                pr.free, st["loaded"], tick=j == 1)
                        t_r = self.V(lambda e, b=pr.at, i=i, h=h: e.tensor_reduce(
                            st["nm"][:, i, h:h + 1], ps[:, b:b + 2, :], AX.XY, ALU.max, negate=True), t, st.get("nm_free"))
                        pr.free = [t_r]
                        yield
            nm, nt, np_, nmT = st["nm"], st["nt"], st["np"], st["nmT"]
            t = self.V(lambda e: e.tensor_copy(np_[:, :, :, 0], nm[:, :, :]), t_r, st.get("np_free"))
            t = self.V(lambda e: e.tensor_tensor(nt[:, :, :], nm[:, :, :], np_[:, :, :, 0], ALU.subtract), t)
            t = self.V(lambda e: e.tensor_copy(np_[:, :, :, 1], nt[:, :, :]), t)
            t = self.V(lambda e: e.tensor_tensor(np_[:, :, :, 2], nt[:, :, :], np_[:, :, :, 1], ALU.subtract), t)
            st["nm_free"] = t
            yield
            pr = pairs_ring.next()
            view = ps[0:12, pr.at, 0:S // 2].bitcast(BF16)
            for i in range(SC):
                t2 = pe.do(lambda e, i=i: e.transpose(view[:, i * P:(i + 1) * P], np_[:, i, :, :].rearrange("p h s -> p (h s)"),
                                                     self.identb[:, :]), t, pr.free, self.t_const, tick=i == SC - 1)
            st["np_free"] = t2
            t = self.V(lambda e: e.tensor_copy(nmT[:, :], view), t2, st.get("nmT_free"))
            pr.free = [t]
            u = len(spec) - 1
            row = spec[u][1]
            for h in range(4):
                t3 = st["arm"].dma(self.sp, st["qs"][u][row:row + 3, h, :], nmT[3 * h:3 * h + 3, :], t)
            st["maxed"] = st["nmT_free"] = t3
            yield

        def pass2(n):
            job, st = jobs[n], sets[n % nbuf]
            acc = job["acc"] = accs.next()
            chunks = job["keys"] // P
            order = list(range(chunks))[::-1] if job["mode"] == "upper" else list(range(chunks))
            late = []
            first = [True]

            def values(c, jj, w, wd, t, t_wd, last):
                start = c == order[0]
                lo, hi = (c * P, S) if job["mode"] == "causal" else (0, c * P) if job["mode"] == "upper" else (0, S)
                heads = [(j, 2 * jj + j) for j in range(2)]
                if hi > lo:
                    for j, h in heads:
                        t1 = pe.do(lambda e, j=j, h=h: e.matmul(
                            ps[32 * h:32 * h + 32, acc.at, lo:hi], job["v"](c, h), w.at[:, j, lo:hi], start=start,
                            stop=last and wd is None), t, acc.free, job["v_ready"], tick=j == 1)
                if softmax and d == 32:
                    for j, h in heads:
                        o = 32 * ((h + 2) % 4)
                        t1 = pe.do(lambda e, j=j, o=o: e.matmul(
                            ps[o:o + 32, 7, :], self.ones[:, 0:32], w.at[:, j, :], start=start, stop=last), t, acc.free, tick=j == 1)
                w.free = [t1]
                if wd is not None:
                    for j, h in heads:
                        t1 = pe.do(lambda e, j=j, h=h: e.matmul(
                            ps[32 * h:32 * h + 32, acc.at, c * P:(c + 1) * P], job["v"](c, h), wd.at[:, j, :], start=False, stop=last),
                            t_wd, job["v_ready"], tick=j == 1)
                    wd.free = [t1]
                return t1

            for c in order:
                lo = c * P if job["mode"] == "causal" else 0
                for jj in range(2):
                    pr = pairs_ring.next()
                    for j in range(2):
                        h = 2 * jj + j
                        out = ps[:, pr.at + j, lo:S]
                        pe.wait(pr.free, st["loaded"], st["maxed"] if softmax else None, st["t_one"])
                        for u, (pairs, row) in enumerate(spec):
                            K = len(pairs) * d + (3 if softmax and row is not None else 0)
                            end = u == len(spec) - 1 and job["mode"] != "causal" or (u == len(spec) - 1 and not softmax)
                            t = pe.do(lambda e, u=u, K=K, h=h, c=c, out=out, lo=lo, end=end: e.matmul(
                                out, st["ks"][u][0:K, h, c * P:(c + 1) * P], st["qs"][u][0:K, h, lo:S], start=u == 0, stop=end),
                                tick=end and j == 1)
                        if job["mode"] == "causal" and softmax:
                            t = pe.do(lambda e, b=pr.at + j, lo=lo: e.matmul(
                                ps[:, b, lo:lo + P], self.identb[:, :], self.mask_kq[:, :], start=False, stop=True), tick=j == 1)
                    w = wts.next()
                    if softmax:
                        t = self.A(lambda e, w=w, b=pr.at, lo=lo: e.activation(w.at[:, :, lo:S], ps[:, b:b + 2, lo:S], ACT.Exp, scale=scale),
                                   t, w.free)
                    else:
                        t = self.V(lambda e, w=w, b=pr.at, lo=lo, jj=jj: e.tensor_tensor(
                            w.at[:, :, lo:S], ps[:, b:b + 2, lo:S], job["decay"](jj, S - lo), ALU.mult), t, w.free, job["decay_ready"])
                    pr.free = [t]
                    wd, t_wd = None, None
                    if job["mode"] == "upper":
                        wd = wds.next()
                        t_wd = self.G(lambda e, wd=wd, w=w, c=c: e.affine_select(
                            out=wd.at[:, :, :], in_=w.at[:, :, c * P:(c + 1) * P], compare_op=ALU.is_gt, fill=0.0, base=0,
                            pattern=[[0, 2], [-1, P]], channel_multiplier=1), t, wd.free)
                    late.append((c, jj, w, wd, t, t_wd, c == order[-1]))
                    if len(late) > (1 if d == 32 else 2):
                        for _ in range(1 if d == 32 else 2):
                            values(*late.pop(0))
                    yield
            while late:
                t_end = values(*late.pop(0))
            st["free"] = [t_end]
            job["end"] = t_end

        yield
        for n in range(min(nbuf - 1, len(jobs))):
            load(n)
        yield
        pairs_ring = Ring([0, 2, 4])
        for i, s in enumerate(pairs_ring.slots):
            s.free = self.banks.slots[2 * i].free + self.banks.slots[2 * i + 1].free
        accs = Ring([6, 7] if d == 16 else [6])
        for s in accs.slots:
            s.free = self.banks.slots[6].free + self.banks.slots[7].free
        items = lambda m: (2 * SC if jobs[m]["keys"] == S else 4 * SC) + 2
        maxima, given = {}, {}

        lead = 0.6 if d == 16 else 0.4

        def give(m, share):
            if not softmax or m >= len(jobs):
                return
            if m not in maxima:
                maxima[m], given[m] = pass1(m), 0
            while given[m] < items(m) and given[m] < items(m) * share:
                next(maxima[m], None)
                given[m] += 1

        give(0, 1)
        if nbuf > 2:
            give(1, lead)
        yield
        wts = Ring([self.sb(f"{tag}_w{i}", [P, 2, S], F32, mem) for i in range(4 if d == 32 else 5)])
        if jobs[0]["mode"] == "upper":
            wds = Ring([self.sb(f"{tag}_wd{i}", [P, 2, P], F32, mem) for i in range(3)])
        raws = Ring([self.sb(f"{tag}_raw{i}", [P, S], F32, mem) for i in range(2)])
        if softmax:
            off, turn = (16, 0) if d == 16 else (0, 2)
            pick = self.sb(f"{tag}_pick", [P, 4], F32, mem)
            t = self.G(lambda e: e.memset(pick[:, :], 0.0))
            t_pick = self.G(lambda e: e.affine_select(out=pick[:, 0:4 - turn], in_=pick[:, 0:4 - turn], compare_op=ALU.not_equal, fill=1.0,
                                                      base=-off - 32 * turn, pattern=[[-32, 4 - turn]], channel_multiplier=1), t)
            if turn:
                t_pick = self.G(lambda e: e.affine_select(out=pick[:, turn:4], in_=pick[:, turn:4], compare_op=ALU.not_equal, fill=1.0,
                                                          base=-off, pattern=[[-32, turn]], channel_multiplier=1), t_pick)
            rec = Ring([(self.sb(f"{tag}_rec{i}", [P, SC * 4], F32, mem), self.sb(f"{tag}_rex{i}", [P, SC * 4, 32], F32, mem)) for i in range(2)])
            dens = raws if d == 16 else Ring([self.sb(f"{tag}_den{i}", [P, S], F32, mem) for i in range(2)])

        settling = iter(())
        for n, job in enumerate(jobs):
            if n + nbuf - 1 < len(jobs):
                load(n + nbuf - 1)
            steps = 2 * job["keys"] // P
            for k, _ in enumerate(pass2(n)):
                if k >= 1:
                    next(settling, None)
                now = (k + 1) / steps
                if nbuf > 2:
                    give(n + 1, now + lead)
                    give(n + 2, now - (1 - lead))
                else:
                    give(n + 1, (k + 1 - 3) / (0.72 * steps - 3))
            for _ in settling:
                pass
            give(n + 1, 1)
            settling = settle(job, job["end"])
            next(settling, None)
        for _ in settling:
            pass
        for i, s in enumerate(pairs_ring.slots):
            self.banks.slots[2 * i].free = list(s.free)
            self.banks.slots[2 * i + 1].free = list(s.free)
        for i in (6, 7):
            self.banks.slots[i].free = [t for s in accs.slots for t in s.free]

    def context(self):
        with ExitStack() as mem:
            ctx = self.sb("ctx", [P, MC, CW], F32, mem)
            src = self.a["ctx_512"].rearrange("b (c p) d -> p (b c) d", p=P)
            t_c = self.arrival("ctx").dma(self.sp, ctx[:, :, :], src)
            self.ctxT_ready = self.to_features(ctx, CW, MC, [t_c] * MC, lambda f, n, view, t: self.copy(
                self.act if n % 2 else self.dve, self.ctxT[:, n * BANK:(n + 1) * BANK], view, t))
            self.fence()

    def cross_attention(self):
        a, ps = self.a, self.ps
        self.context()
        with ExitStack() as mem:
            sb = lambda n, s, dt=F32: self.sb("xa_" + n, s, dt, mem)
            W = {}
            tW = {}
            for n, rows in (("Wq", FC), ("Wk", FC), ("Wcq", FC), ("Wck", 1), ("Wv", FC), ("Wcv", 1)):
                W[n] = sb(n, [P, rows, D])
                tW[n] = self.arrival("xa" + n).dma(self.sp, W[n][:, :, :], a["L0_xattn_" + n].rearrange("(f p) n -> p f n", p=P))
            bcol, t_bc = self.columns(mem, "xab", ["L0_xattn_" + n for n in ("bq", "bk", "bcq", "bck")])
            brow = sb("brow", [P, 3, D])
            abr = self.arrival("xabr")
            for i, n in enumerate(("bv", "bcv", "bp")):
                t_br = abr.dma(self.sp, brow[:, i, :], a["L0_xattn_" + n].partition_broadcast(P))
            dh = D // H
            wp = sb("wp", [P, 4, D])
            t_wz = self.G(lambda e: e.memset(wp[:, :, :], 0.0))
            awp = self.arrival("xawp")
            for h in range(4):
                t_wp = awp.dma(self.sp, wp[32 * h:32 * h + dh, :, :], a["L0_xattn_Wp"].rearrange("(g h i) n -> h i g n", g=4, h=4)[h], t_wz)
            v = sb("v", [P, NC, H, 32])
            vc = sb("vc", [P, MC, H, 32])
            t_vo = self.G(lambda e: e.memset(v[:, :, :, :], 1.0))
            t_vco = self.G(lambda e: e.memset(vc[:, :, :, :], 1.0))
            self.norm_x()
            dq, dk, dcq, dck = (self.scratch("xa" + n, D, w) for n, w in (("q", T), ("k", T), ("cq", T), ("ck", TM)))
            jobs = []
            attention = self.attend("xa", jobs, dh, dh ** -0.5, mem, MEM)
            next(attention)
            with ExitStack() as tmp:
                ring = self.parts_out(tmp, "xap")
                xT = lambda f, n: self.xnT[:, f, n * BANK:(n + 1) * BANK]
                cT = lambda f, n: self.ctxT[:, n * BANK:(n + 1) * BANK]
                r_q = self.project_parts(ring, W["Wq"], FC, xT, [tW["Wq"], t_bc], self.xnT_ready, bcol["L0_xattn_bq"], dq, T, D)
                r_k = self.project_parts(ring, W["Wk"], FC, xT, tW["Wk"], self.xnT_ready, bcol["L0_xattn_bk"], dk, T, D)
                t_v, t_vc = [], []
                t_self = {}
                t_y = []

                def done(job, raw, t_raw, rden, t_rden):
                    b, g = job["b"], job["g"]
                    y = yT[:, g, b * S:(b + 1) * S]
                    if not job["cross"]:
                        t_self[b, g] = self.V(lambda e: e.tensor_tensor(y, raw[:, :], rden, ALU.mult), t_rden)
                        return t_self[b, g]
                    q = yc.next()
                    t2 = self.V(lambda e: e.tensor_tensor(q.at[:, :], raw[:, :], rden, ALU.mult), t_rden, q.free)
                    t3 = self.G(lambda e: e.tensor_tensor(y, y, q.at[:, :], ALU.add), t2, t_self[b, g])
                    q.free = [t3]
                    t_y.append(t3)
                    return t2

                def jobs_of(cross):
                    out = []
                    for b in range(B):
                        for g in range(4):
                            rows = g * 4 * dh
                            m = rows // P
                            kn = [b] if not cross else [2 * b, 2 * b + 1]
                            out.append(dict(q=((dcq if cross else dq), b * S), k=((dck, b * MEM) if cross else (dk, b * S)), rows=rows,
                                            keys=MEM if cross else S, mode="full" if cross else "causal", b=b, g=g, cross=cross,
                                            v=(lambda c, h, b=b, g=g: vc[:, b * MC // B + c, 4 * g + h, :]) if cross else
                                              (lambda c, h, b=b, g=g: v[:, b * SC + c, 4 * g + h, :]),
                                            v_ready=t_vc if cross else t_v,
                                            ready=[(r_cq if cross else r_q)[m, b]] + [(r_ck if cross else r_k)[m, n] for n in kn],
                                            done=done))
                    return out
                r_cq = self.project_parts(ring, W["Wcq"], FC, xT, tW["Wcq"], self.xnT_ready, bcol["L0_xattn_bcq"], dcq, T, D)
                r_ck = self.project_parts(ring, W["Wck"], 1, cT, tW["Wck"], self.ctxT_ready, bcol["L0_xattn_bck"], dck, TM, D)
                self.flush_parts()
                jobs += jobs_of(False) + jobs_of(True)
                next(attention)
                for c in range(NC):
                    bank = self.banks.next()
                    t = self.chain(ps[:, bank.at, 0:D], [(self.xnT[:, f, c * P:(c + 1) * P], W["Wv"][:, f, :]) for f in range(FC)],
                                   bank.free, tW["Wv"])
                    t = self.V(lambda e, c=c, b=bank.at: e.tensor_tensor(
                        v[:, c, :, 0:dh], ps[:, b, 0:D].rearrange("p (h i) -> p h i", h=H), brow[:, 0, :].rearrange("p (h i) -> p h i", h=H),
                        ALU.add), t, t_br, t_vo)
                    bank.free = [t]
                    t_v.append(t)
                for c in range(MC):
                    bank = self.banks.next()
                    t = self.chain(ps[:, bank.at, 0:D], [(self.ctxT[:, c * P:(c + 1) * P], W["Wcv"][:, 0, :])], bank.free, tW["Wcv"])
                    t = self.V(lambda e, c=c, b=bank.at: e.tensor_tensor(
                        vc[:, c, :, 0:dh], ps[:, b, 0:D].rearrange("p (h i) -> p h i", h=H), brow[:, 1, :].rearrange("p (h i) -> p h i", h=H),
                        ALU.add), t, t_br, t_vco)
                    bank.free = [t]
                    t_vc.append(t)
                t_xb = None
                for c in range(NC):
                    t_xb = self.G(lambda e, c=c: e.tensor_tensor(self.x[:, c, :], self.x[:, c, :], brow[:, 2, :], ALU.add),
                                  self.xn_ready[-1], t_br)
                next(attention)
                self.fence(*[s.free for s in ring.slots])
            yT = sb("yT", [P, 4, T])
            yc = Ring([sb(f"yc{i}", [P, S]) for i in range(2)])
            for _ in attention:
                pass
            self.x_ready = []
            for c in range(NC):
                bank = self.banks.next()
                t = self.chain(ps[:, bank.at, 0:D], [(yT[:, g, c * P:(c + 1) * P], wp[:, g, :]) for g in range(4)], bank.free, t_y, t_wp)
                t = self.V(lambda e, c=c, b=bank.at: e.tensor_tensor(self.x[:, c, :], self.x[:, c, :], ps[:, b, 0:D], ALU.add), t, t_xb)
                bank.free = [t]
                self.x_ready.append(t)
            self.fence()

    def route(self, mem, tag, w, n_exp, bias_row, t_w):
        ps = self.ps
        lg = self.sb(tag + "_lg", [P, NC, 8], F32, mem)
        st = self.sb(tag + "_st", [P, NC, 2], F32, mem)
        top = self.sb(tag + "_top", [P, NC, 8], F32, mem)
        idx = self.sb(tag + "_idx", [P, NC, 8], U32, mem)
        who = self.sb(tag + "_who", [P, NC, 2], F32, mem)
        t_pad = self.V(lambda e: e.memset(lg[:, :, :], -1.0))
        bank = self.banks.next()
        for c in range(NC):
            t = self.chain(ps[:, bank.at, 8 * c:8 * c + n_exp], [(self.xnT[:, f, c * P:(c + 1) * P], w[:, f, :]) for f in range(FC)],
                           bank.free, self.xnT_ready, t_w, tick=c == NC - 1)
        live = lg[:, :, 0:n_exp]
        view = ps[:, bank.at, 0:8 * NC].rearrange("p (c e) -> p c e", e=8)[:, :, 0:n_exp]
        if bias_row is not None:
            t = self.V(lambda e: e.tensor_tensor(live, view, bias_row.unsqueeze(1).broadcast_to([P, NC, n_exp]), ALU.add), t, t_w, t_pad)
        else:
            t = self.V(lambda e: e.tensor_copy(live, view), t, t_pad)
        bank.free = [t]
        t = self.V(lambda e: e.tensor_reduce(st[:, :, 0], live, AX.X, ALU.max), t)
        bc = lambda i: st[:, :, i].unsqueeze(2).broadcast_to([P, NC, n_exp])
        t = self.V(lambda e: e.tensor_tensor(live, live, bc(0), ALU.subtract), t)
        t = self.A(lambda e: e.activation(live, live, ACT.Exp), t)
        t = self.V(lambda e: e.tensor_reduce(st[:, :, 0], live, AX.X, ALU.add), t)
        t = self.V(lambda e: e.reciprocal(st[:, :, 1], st[:, :, 0]), t)
        t = self.V(lambda e: e.tensor_tensor(live, live, bc(1), ALU.mult), t)
        for c in range(NC):
            t1 = self.V(lambda e, c=c: e.max(top[:, c, :], lg[:, c, :]), t if c == 0 else None)
        for c in range(NC):
            t = self.V(lambda e, c=c: e.max_index(idx[:, c, :], top[:, c, :], lg[:, c, :]), t1 if c == 0 else None)
        t = self.V(lambda e: e.tensor_copy(who[:, :, :], idx[:, :, 0:2]), t)
        return top, who, t

    def moe(self):
        a, ps = self.a, self.ps
        SLOTS = E0 * CAP
        NR = -(-SLOTS // P)
        with ExitStack() as mem:
            sb = lambda n, s, dt=F32: self.sb("mo_" + n, s, dt, mem)
            wr = sb("wr", [P, FC, E0])
            br = sb("br", [P, E0])
            t_wr = self.arrival("mowr").dma(self.sp, wr[:, :, :], a["L0_ffn_Wr"].rearrange("(f p) e -> p f e", p=P))
            t_br = self.arrival("mobr").dma(self.sp, br[:, :], a["L0_ffn_br"].partition_broadcast(P))
            b1, t_b1 = self.columns(mem, "mob1", ["L0_ffn_b1"])
            b1 = b1["L0_ffn_b1"]
            b2 = sb("b2", [1, E0 * D])
            t_b2 = self.arrival("mob2").dma(self.sp, b2[:, :], a["L0_ffn_b2"].rearrange("e d -> (e d)").unsqueeze(0))
            wring = Ring([(sb(f"w1_{i}", [P, FC, HID]), sb(f"w2_{i}", [P, HC, D]), self.arrival(f"mow{i}")) for i in range(4)])
            zero = sb("zero", [P, D])
            t_zero = self.G(lambda e: e.memset(zero[:, :], 0.0))
            xg = self.nc.dram_tensor("scratch_xg", (SLOTS + 2 * T, D), F32).ap()
            yo = self.nc.dram_tensor("scratch_yo", (SLOTS + 1, D), F32).ap()
            zrows = SLOTS // E0 // 2
            az = self.arrival("moz")
            az.dma(self.sp, xg[0:SLOTS, :].rearrange("(p k) d -> p k d", p=zrows), zero[0:zrows, :].unsqueeze(1).broadcast_to([zrows, SLOTS // zrows, D]), t_zero)
            t_z = az.dma(self.sp, yo[SLOTS:SLOTS + 1, :], zero[0:1, :], t_zero)
            weights = {}

            context_operands = self.context_operands(mem)

            def load(e):
                slot = wring.next()
                w1, w2, arr = slot.at
                arr.dma(self.sp, w1[:, :, :], a["L0_ffn_W1"][e].rearrange("(f p) n -> p f n", p=P), slot.free)
                t = arr.dma(self.sp, w2[:, :, :], a["L0_ffn_W2"][e].rearrange("(f p) n -> p f n", p=P))
                weights[e] = (slot, w1, w2, t)
            for e in range(4):
                load(e)
            self.norm_x()
            next(context_operands)
            top, who, t_top = self.route(mem, "mor", wr, E0, br[:, :], [t_wr, t_br])
            iota_e = sb("iota_e", [P, E0])
            t_i = self.G(lambda e: e.iota(iota_e[:, :], pattern=[[1, E0]], base=0, channel_multiplier=0, allow_small_or_imprecise_dtypes=True))
            dump = sb("dump", [P, 2, NC])
            t_i = self.G(lambda e: e.iota(dump[:, :, :], pattern=[[T, 2], [P, NC]], base=SLOTS, channel_multiplier=1, allow_small_or_imprecise_dtypes=True))
            before = sb("before", [P, P])
            t_b = self.G(lambda e: e.memset(before[:, :], 1.0))
            t_b = self.G(lambda e: e.affine_select(out=before[:, :], in_=before[:, :], compare_op=ALU.is_gt, fill=0.0, base=0,
                                                   pattern=[[1, P]], channel_multiplier=-1), t_b)
            chosen = sb("chosen", [P, 2, NC, E0])
            G = sb("G", [P, NC, E0])
            G2 = sb("G2", [P, NC, E0])
            ib = iota_e[:, :].unsqueeze(1).broadcast_to([P, NC, E0])
            for k in range(2):
                t = self.V(lambda e, k=k: e.tensor_tensor(chosen[:, k, :, :], ib, who[:, :, k:k + 1].broadcast_to([P, NC, E0]), ALU.is_equal), t_top, t_i)
            t = self.V(lambda e: e.tensor_tensor(G[:, :, :], chosen[:, 0, :, :], top[:, :, 0:1].broadcast_to([P, NC, E0]), ALU.mult), t)
            t = self.V(lambda e: e.tensor_tensor(G2[:, :, :], chosen[:, 1, :, :], top[:, :, 1:2].broadcast_to([P, NC, E0]), ALU.mult), t)
            t = self.V(lambda e: e.tensor_tensor(G[:, :, :], G[:, :, :], G2[:, :, :], ALU.add), t)
            t = self.V(lambda e: e.tensor_tensor(G2[:, :, :], chosen[:, 0, :, :], chosen[:, 1, :, :], ALU.add), t)
            t_G = self.V(lambda e: e.scalar_tensor_tensor(G[:, :, :], G2[:, :, :], -1.0, G[:, :, :], ALU.add, ALU.add), t)
            K = 7
            digit = sb("digit", [P, K], I32)
            t_i = self.G(lambda e: e.iota(digit[:, :], pattern=[[1, K]], base=1, channel_multiplier=0), t_i)
            level = sb("level", [P, E0], I32)
            cand = sb("cand", [P, K, E0], I32)
            step = sb("step", [P, K], I32)
            hit = sb("hit", [P, K, E0, NC])
            many = sb("many", [P, K, E0])
            found = sb("found", [P, E0])
            found_i = sb("found_i", [P, E0], I32)
            t = self.V(lambda e: e.memset(level[:, :], 0))
            for shift in range(27, -1, -3):
                t1 = self.V(lambda e, shift=shift: e.tensor_scalar(step[:, :], digit[:, :], shift, None, ALU.logical_shift_left), t, t_i)
                t = self.V(lambda e: e.tensor_tensor(cand[:, :, :], level[:, :].unsqueeze(1).broadcast_to([P, K, E0]),
                                                     step[:, :].unsqueeze(2).broadcast_to([P, K, E0]), ALU.bitwise_or), t1)
                t = self.V(lambda e: e.tensor_tensor(hit[:, :, :, :], G[:, :, :].rearrange("p c e -> p e c").unsqueeze(1).broadcast_to([P, K, E0, NC]),
                                                     cand[:, :, :].bitcast(F32).unsqueeze(3).broadcast_to([P, K, E0, NC]), ALU.is_ge), t, t_G)
                t = self.V(lambda e: e.tensor_reduce(many[:, :, :], hit[:, :, :, :], AX.X, ALU.add), t)
                if 3 <= shift <= 24:
                    next(context_operands)
                bank = self.banks.next()
                t = self.chain(ps[:, bank.at, 0:K * E0], [(self.ones[:, :], many[:, :, :].rearrange("p k e -> p (k e)"))], t, bank.free, self.t_ones)
                t = self.V(lambda e, b=bank.at: e.tensor_scalar(many[:, :, :].rearrange("p k e -> p (k e)"), ps[:, b, 0:K * E0], float(CAP), None, ALU.is_ge), t)
                bank.free = [t]
                t = self.V(lambda e: e.tensor_reduce(found[:, :], many[:, :, :].rearrange("p k e -> p e k"), AX.X, ALU.add), t)
                t = self.V(lambda e: e.tensor_copy(found_i[:, :], found[:, :]), t)
                t = self.V(lambda e, shift=shift: e.tensor_scalar(found_i[:, :], found_i[:, :], shift, None, ALU.logical_shift_left), t)
                t = self.V(lambda e: e.tensor_tensor(level[:, :], level[:, :], found_i[:, :], ALU.bitwise_or), t)
            kind = sb("kind", [P, NC, 2, E0])
            lv = level[:, :].bitcast(F32).unsqueeze(1).broadcast_to([P, NC, E0])
            t = self.V(lambda e: e.tensor_tensor(kind[:, :, 0, :], G[:, :, :], lv, ALU.is_gt), t)
            t = self.V(lambda e: e.tensor_tensor(kind[:, :, 1, :], G[:, :, :], lv, ALU.is_equal), t)
            bank = self.banks.next()
            flat = kind[:, :, :, :].rearrange("p c k e -> p (c k e)")
            W = 2 * E0
            self.pe.wait(bank.free, t, t_b)
            for back in range(NC):
                t = self.pe.do(lambda e, back=back, b=bank.at: e.matmul(
                    ps[:, b, back * W:NC * W], (self.ones if back else before)[:, :], flat[:, 0:(NC - back) * W],
                    start=back == 0, stop=back == NC - 1), tick=back == NC - 1)
            t = self.chain(ps[:, bank.at, NC * W:NC * W + E0], [(self.ones[:, :], kind[:, c, 0, :]) for c in range(NC)])
            place = sb("place", [P, NC, 2, E0])
            above = sb("above", [P, E0])
            t1 = self.V(lambda e, b=bank.at: e.tensor_scalar(place[:, :, :, :].rearrange("p c k e -> p (c k e)"), ps[:, b, 0:NC * W],
                                                             -float(CAP), None, ALU.add), t)
            t = self.V(lambda e, b=bank.at: e.tensor_copy(above[:, :], ps[:, b, NC * W:NC * W + E0]), t)
            bank.free = [t]
            t = self.V(lambda e: e.tensor_tensor(place[:, :, 1, :], place[:, :, 1, :], above[:, :].unsqueeze(1).broadcast_to([P, NC, E0]), ALU.add), t, t1)
            t = self.V(lambda e: e.tensor_tensor(place[:, :, :, :], place[:, :, :, :], kind[:, :, :, :], ALU.mult), t)
            rank = sb("rank", [P, NC, E0])
            t_rank = self.V(lambda e: e.scalar_tensor_tensor(rank[:, :, :], place[:, :, 0, :], float(CAP), place[:, :, 1, :], ALU.add, ALU.add), t)
            slot = sb("slot", [P, 2, NC])
            rk = sb("rk", [P, 2, NC])
            ok = sb("ok", [P, 2, NC])
            to = sb("to", [P, 2, NC], U32)
            fro = sb("fro", [P, 2, NC], U32)
            for k in range(2):
                t = self.V(lambda e, k=k: e.tensor_tensor(chosen[:, k, :, :], chosen[:, k, :, :], rank[:, :, :], ALU.mult), t_rank)
                t = self.V(lambda e, k=k: e.tensor_reduce(rk[:, k, :], chosen[:, k, :, :], AX.X, ALU.add), t)
                t = self.V(lambda e, k=k: e.scalar_tensor_tensor(slot[:, k, :], who[:, :, k], float(CAP), rk[:, k, :], ALU.mult, ALU.add), t)
                t = self.V(lambda e, k=k: e.tensor_scalar(ok[:, k, :], rk[:, k, :], float(CAP), None, ALU.is_lt), t)
            t = self.V(lambda e: e.tensor_tensor(rk[:, :, :], slot[:, :, :], dump[:, :, :], ALU.subtract), t)
            t = self.V(lambda e: e.tensor_tensor(rk[:, :, :], rk[:, :, :], ok[:, :, :], ALU.mult), t)
            t_to = self.V(lambda e: e.tensor_tensor(to[:, :, :], rk[:, :, :], dump[:, :, :], ALU.add), t)
            t = self.V(lambda e: e.scalar_tensor_tensor(rk[:, :, :], slot[:, :, :], -float(SLOTS), ok[:, :, :], ALU.add, ALU.mult), t_to)
            t_fro = self.V(lambda e: e.tensor_scalar(fro[:, :, :], rk[:, :, :], float(SLOTS), None, ALU.add), t)
            sc = self.arrival("mosc")
            self.pool.wait(t_to, t_z)
            for c in range(NC):
                for k in range(2):
                    sc.count += 16
                    self.pool.items.append(lambda e, c=c, k=k: e.indirect_dma_start(
                        xg, bass.IndirectOffsetOnAxis(ap=to[:, k, c:c + 1], axis=0), self.xn[:, c, :], None).then_inc(sc.sem, 16))
            t_sc = (sc.sem, sc.count)
            next(context_operands)
            xs = sb("xs", [P, NR, D])
            xgT = sb("xgT", [P, FC, NR * P])
            ax = self.arrival("moxg")
            full = SLOTS // P
            t = ax.dma(self.pool, xs[:, 0:full, :], xg[0:full * P, :].rearrange("(r p) d -> p r d", p=P), t_sc)
            rest = SLOTS - full * P
            if rest:
                t = ax.dma(self.pool, xs[0:rest, full, :], xg[full * P:SLOTS, :])
            t_g = []
            for f in range(FC):
                for r0 in range(0, NR, 4):
                    bank = self.banks.next()
                    rs = list(range(r0, min(NR, r0 + 4)))
                    for r in rs:
                        m = P if r < full else rest
                        t1 = self.pe.do(lambda e, r=r, m=m, b=bank.at, r0=r0, f=f: e.transpose(
                            ps[:, b, (r - r0) * P:(r - r0) * P + m], xs[0:m, r, f * P:(f + 1) * P], self.ident[0:m, 0:m]),
                            t, bank.free, tick=r == rs[-1])
                    n = (len(rs) - 1) * P + m
                    t1 = self.copy(self.act if f else self.dve, xgT[:, f, r0 * P:r0 * P + n], ps[:, bank.at, 0:n], t1)
                    bank.free = [t1]
                    t_g.append(t1)
            hT = Ring([sb(f"hT{i}", [P, HC, CAP]) for i in range(2)])
            os_ = Ring([(sb(f"o{i}", [P, 2, D]), self.arrival(f"moo{i}")) for i in range(2)])
            t_done = []
            for x in range(E0):
                wslot, w1, w2, t_w = weights[x]
                h = hT.next()
                t_h = []
                for m0 in range(0, HC, 2):
                    bank = self.banks.next()
                    for m in (m0, m0 + 1):
                        t = self.chain(ps[:, bank.at, (m - m0) * 256:(m - m0) * 256 + CAP],
                                       [(w1[:, f, m * P:(m + 1) * P], xgT[:, f, x * CAP:(x + 1) * CAP]) for f in range(FC)],
                                       bank.free, t_w, t_g, tick=m != m0)
                    for m in (m0, m0 + 1):
                        t1 = self.A(lambda e, m=m, m0=m0, b=bank.at, h=h, x=x: e.activation(
                            h.at[:, m, :], ps[:, b, (m - m0) * 256:(m - m0) * 256 + CAP], ACT.Silu,
                            bias=b1[:, x * HC + m:x * HC + m + 1]), t, h.free, t_b1)
                    bank.free = [t1]
                    t_h.append(t1)
                o = os_.next()
                ot, oarr = o.at
                for r, (lo, n) in enumerate(((0, P), (P, CAP - P))):
                    bank = self.banks.next()
                    t = self.chain(ps[0:n, bank.at, 0:D], [(h.at[:, m, lo:lo + n], w2[:, m, :]) for m in range(HC)] +
                                   [(self.ones[0:1, 0:n], b2[0:1, x * D:(x + 1) * D])], bank.free, t_h, t_b2, self.t_ones)
                    t1 = self.V(lambda e, n=n, r=r, b=bank.at, ot=ot: e.tensor_copy(ot[0:n, r, :], ps[0:n, b, 0:D]), t, o.free)
                    bank.free = [t1]
                    t2 = oarr.dma(self.sp, yo[x * CAP + lo:x * CAP + lo + n, :], ot[0:n, r, :], t1)
                    if r == 0:
                        first = t2
                h.free, wslot.free = [t], [t]
                o.free = [t2]
                t_done.append(t2)
                if x + 4 < E0:
                    load(x + 4)
            ga = [self.arrival(f"moga{i}") for i in range(8)]
            gb = Ring([(sb(f"g{i}", [P, D]), ga[i]) for i in range(8)])
            self.pool.wait(t_done, t_fro)
            self.x_ready = []
            for c in range(NC):
                for k in range(2):
                    g = gb.next()
                    gt, arr = g.at
                    self.pool.wait(g.free)
                    arr.count += 16
                    self.pool.items.append(lambda e, c=c, k=k, gt=gt, arr=arr: e.indirect_dma_start(
                        gt[:, :], None, yo, bass.IndirectOffsetOnAxis(ap=fro[:, k, c:c + 1], axis=0)).then_inc(arr.sem, 16))
                    t = self.V(lambda e, c=c, k=k, gt=gt: e.scalar_tensor_tensor(
                        self.x[:, c, :], gt[:, :], top[:, c, k:k + 1], self.x[:, c, :], ALU.mult, ALU.add),
                        (arr.sem, arr.count), self.dve.last())
                    g.free = [t]
                self.x_ready.append(t)
            self.fence()

    def retention(self):
        a, ps = self.a, self.ps
        dk = D // H
        with ExitStack() as mem:
            sb = lambda n, s, dt=F32: self.sb("re_" + n, s, dt, mem)
            wT = sb("wT", [P, FC, 3 * D])
            woT = sb("woT", [P, 4, D])
            v = sb("v", [P, NC, H, 32])
            jobs = []
            attention = self.attend("re", jobs, dk, 1.0, mem, S, softmax=False)
            next(attention)
            decay = sb("decay", [P, H, S])
            lg = sb("lg", [P, 4, H])
            dq, dkk = self.scratch("req", D, T), self.scratch("rek", D, T)
            t_v0 = self.G(lambda e: e.memset(v[:, :, :, :], 0.0))
            t_lg = self.arrival("relg").dma(self.sp, lg[:, 0, :], a["L1_attn_log_gamma"].partition_broadcast(P))
            self.norm_x()
            with ExitStack() as tmp:
                tb = lambda n, s, dt=F32: self.sb("ret_" + n, s, dt, tmp)
                raw = tb("raw", [P, 3 * FC, D])
                rawo = tb("rawo", [P, FC, H, 32])
                dist = tb("dist", [P, S])
                kt = tb("kt", [P, NC, D])
                kst = tb("kst", [P, 4, NC, H])
                ksq = tb("ksq", [P, NC, D])
                t_r = self.arrival("rew").dma(self.sp, raw[:, :, :], a["L1_attn_W_qkv"].rearrange("(o p) i -> p o i", p=P))
                t_z = self.G(lambda e: e.memset(rawo[:, :, :, :], 0.0))
                aw = self.arrival("rewo")
                for f in range(FC):
                    t_ro = aw.dma(self.sp, rawo[:, f, :, 0:dk], a["L1_attn_W_o"][f * P:(f + 1) * P, :].rearrange("p (h i) -> p h i", h=H), t_z)
                t = self.V(lambda e: e.tensor_scalar(lg[:, 1, :], lg[:, 0, :], -1.0, None, ALU.mult), t_lg)
                t = self.V(lambda e: e.tensor_tensor(lg[:, 1, :], lg[:, 1, :], lg[:, 0, :], ALU.min), t)
                t = self.A(lambda e: e.activation(lg[:, 2, :], lg[:, 1, :], ACT.Exp), t)
                t = self.A(lambda e: e.activation(lg[:, 3, :], lg[:, 2, :], ACT.Ln, bias=1.0), t)
                t = self.V(lambda e: e.tensor_scalar(lg[:, 0, :], lg[:, 0, :], 0.0, None, ALU.min), t)
                t_gamma = self.V(lambda e: e.tensor_tensor(lg[:, 0, :], lg[:, 0, :], lg[:, 3, :], ALU.subtract), t)
                t = self.G(lambda e: e.iota(dist[:, :], pattern=[[1, S]], base=0, channel_multiplier=-1, allow_small_or_imprecise_dtypes=True))
                t_di = self.G(lambda e: e.tensor_scalar(dist[:, :], dist[:, :], 0.0, None, ALU.max), t)
                self.norm_x()
                t_wT = []
                for f in range(FC):
                    for o0 in (0, 3):
                        bank = self.banks.next()
                        for o in range(3):
                            t = self.pe.do(lambda e, o=o, o0=o0, f=f, b=bank.at: e.transpose(
                                ps[:, b, o * P:(o + 1) * P], raw[:, o0 + o, f * P:(f + 1) * P], self.ident[:, :]), t_r, bank.free, tick=o == 2)
                        t = self.copy(self.act, wT[:, f, o0 * P:(o0 + 3) * P], ps[:, bank.at, 0:3 * P], t)
                        bank.free = [t]
                        t_wT.append(t)
                for g in range(4):
                    bank = self.banks.next()
                    for f in range(FC):
                        t = self.pe.do(lambda e, f=f, g=g, b=bank.at: e.transpose(
                            ps[:, b, f * P:(f + 1) * P], rawo[:, f, 4 * g:4 * g + 4, :].rearrange("p h i -> p (h i)"), self.ident[:, :]),
                            t_ro, bank.free, tick=f == 1)
                    t_wo = self.copy(self.act, woT[:, g, :], ps[:, bank.at, 0:D], t)
                    bank.free = [t_wo]
                t_v, t_k = [], []
                for c in range(NC):
                    bank = self.banks.next()
                    t = self.chain(ps[:, bank.at, :], [(self.xnT[:, f, c * P:(c + 1) * P], wT[:, f, D:3 * D]) for f in range(FC)],
                                   bank.free, t_wT, self.xnT_ready)
                    t1 = self.A(lambda e, c=c, b=bank.at: e.activation(kt[:, c, :], ps[:, b, 0:D], ACT.Copy), t)
                    t2 = self.A(lambda e, c=c, b=bank.at: e.activation(
                        v[:, c, :, 0:dk], ps[:, b, D:2 * D].rearrange("p (h i) -> p h i", h=H), ACT.Copy), t, t_v0)
                    bank.free = [t2]
                    t_k.append(t1)
                    t_v.append(t2)
                    for h in (2 * c, 2 * c + 1):
                        t_dc = self.A(lambda e, h=h: e.activation(decay[:, h, :], dist[:, :], ACT.Exp, scale=lg[:, 0, h:h + 1]), t_di, t_gamma)
                t_dec = [self.G(lambda e: e.affine_select(out=decay[:, :, 0:P], in_=decay[:, :, 0:P], compare_op=ALU.is_ge, fill=0.0, base=0,
                                                          pattern=[[0, H], [1, P]], channel_multiplier=-1), t_dc)]
                t_kn = []
                for b in range(B):
                    half = slice(b * SC, (b + 1) * SC)
                    k4 = kt[:, half, :].rearrange("p c (h i) -> p (c h) i", h=H)
                    q4 = ksq[:, half, :].rearrange("p c (h i) -> p (c h) i", h=H)
                    s4 = lambda i, half=half: kst[:, i, half, :].rearrange("p c h -> p (c h)")
                    wide = lambda i, s4=s4: s4(i).unsqueeze(2).broadcast_to([P, SC * H, dk])
                    t = self.V(lambda e, k4=k4, s4=s4: e.tensor_reduce(s4(0), k4, AX.X, ALU.add), t_k[half])
                    t = self.V(lambda e, s4=s4: e.tensor_scalar(s4(0), s4(0), 1.0 / dk, None, ALU.mult), t)
                    t = self.V(lambda e, k4=k4, wide=wide: e.tensor_tensor(k4, k4, wide(0), ALU.subtract), t)
                    t = self.A(lambda e, k4=k4, q4=q4: e.activation(q4, k4, ACT.Square), t)
                    t = self.V(lambda e, q4=q4, s4=s4: e.tensor_reduce(s4(1), q4, AX.X, ALU.add), t)
                    t = self.V(lambda e, s4=s4: e.tensor_scalar(s4(1), s4(1), 1.0 / dk, LN_EPS, ALU.mult, ALU.add), t)
                    t = self.A(lambda e, s4=s4: e.activation(s4(2), s4(1), ACT.Sqrt), t)
                    t = self.V(lambda e, s4=s4: e.reciprocal(s4(3), s4(2)), t)
                    t = self.V(lambda e, k4=k4, wide=wide: e.tensor_tensor(k4, k4, wide(3), ALU.mult), t)
                    t_kn += [t] * SC
                ring = self.parts_out(tmp, "rep")
                r_q = self.project_parts(ring, wT, FC, lambda f, n: self.xnT[:, f, n * BANK:(n + 1) * BANK], t_wT, None, None, dq, T, D)
                r_k = {}

                def send(f, n, view, t):
                    r_k[f, n], t_read = self.send_parts(ring, view, None, t, dkk, f, n)
                    return t_read
                self.to_features(kt, D, NC, t_kn, send)
                self.flush_parts()
                t_y = []

                def done(job, raw, t_raw, rden, t_rden):
                    b, g = job["b"], job["g"]
                    t_y.append(self.G(lambda e: e.tensor_copy(yT[:, g, b * S:(b + 1) * S], raw[:, :]), t_raw))
                    return t_y[-1]

                for b in range(B):
                    for g in range(4):
                        rows = g * 4 * dk
                        jobs.append(dict(q=(dq, b * S), k=(dkk, b * S), rows=rows, keys=S, mode="causal", b=b, g=g,
                                         v=lambda c, h, b=b, g=g: v[:, b * SC + c, 4 * g + h, :], v_ready=t_v[-1],
                                         decay=lambda jj, n, g=g: decay[:, 4 * g + 2 * jj:4 * g + 2 * jj + 2, 0:n], decay_ready=t_dec,
                                         ready=[r_q[rows // P, b], r_k[rows // P, b]], done=done))
                next(attention)
                next(attention)
                self.fence(*[s.free for s in ring.slots])

            yT = sb("yT", [P, 4, T])
            for _ in attention:
                pass
            self.x_ready = []
            for c in range(NC):
                bank = self.banks.next()
                t = self.chain(ps[:, bank.at, 0:D], [(yT[:, g, c * P:(c + 1) * P], woT[:, g, :]) for g in range(4)], bank.free, t_y, t_wo)
                t = self.V(lambda e, c=c, b=bank.at: e.tensor_tensor(self.x[:, c, :], self.x[:, c, :], ps[:, b, 0:D], ALU.add), t)
                bank.free = [t]
                self.x_ready.append(t)
            self.fence()

    def affine_copy(self, gain, shift, t_gb, dst):
        def emit(f, n, view, t):
            return self.A(lambda e: e.activation(dst[:, f, n * BANK:(n + 1) * BANK], view, ACT.Identity,
                                                 bias=shift[:, f:f + 1], scale=gain[:, f:f + 1]), t, t_gb)
        return emit

    def context_operands(self, mem):
        a, ps = self.a, self.ps
        HD = H * 32
        names = ["L1_xattn_a2_lny_g", "L1_xattn_a2_lny_b"]
        vecs, t_c = self.columns(mem, "co", names)
        ctx = self.sb("co_ctx", [P, MC, CW], F32, mem)
        t_ctx = self.arrival("coctx").dma(self.sp, ctx[:, :, :], a["ctx_512"].rearrange("b (c p) d -> p (b c) d", p=P))
        w = {}
        for n in ("wk", "wv"):
            tile = self.sb("co_" + n, [P, HD], F32, mem)
            w[n] = tile, self.arrival("co" + n).dma(self.sp, tile[:, :].rearrange("p (h d) -> p h d", h=H),
                                                    a["L1_xattn_a2_" + n].rearrange("h p d -> p h d"))
        ring = self.parts_out(mem, "co", shared=False)
        stage = Ring([(self.sb(f"co_v{i}", [P, HD], F32, mem), self.arrival(f"cov{i}")) for i in range(2)])
        self.ctx_k, self.ctx_v = self.scratch("a2k", HD, TM), self.nc.dram_tensor("scratch_a2v", (TM, HD), F32).ap()

        def steps():
            done = self.normalize(ctx, ctx, MC, [t_ctx] * MC)
            t_T = self.to_features(ctx, CW, MC, done, self.affine_copy(*(vecs[n] for n in names), t_c, self.ctxT[:, :].unsqueeze(1)))
            yield
            self.ctx_v_ready = []
            for c in range(MC):
                if c and c % 2 == 0:
                    yield
                bank, slot = self.banks.next(), stage.next()
                v, arr = slot.at
                t = self.chain(ps[:, bank.at, :], [(self.ctxT[:, c * P:(c + 1) * P], w["wv"][0][:, :])], bank.free, w["wv"][1], t_T)
                t = self.copy(self.act, v[:, :], ps[:, bank.at, :], t, slot.free)
                bank.free = [t]
                t = arr.dma(self.sp, self.ctx_v[c * P:(c + 1) * P, :], v[:, :], t)
                slot.free = [t]
                self.ctx_v_ready.append(t)
            yield
            self.ctx_k_ready = self.project_parts(ring, w["wk"][0][:, :].unsqueeze(1), 1, lambda f, n: self.ctxT[:, n * BANK:(n + 1) * BANK],
                                                  w["wk"][1], t_T, None, self.ctx_k, TM, HD)
            self.flush_parts()
            yield
        return steps()

    def mha(self, pre, xb, xb_ready, cross):
        a, ps = self.a, self.ps
        A = "L1_xattn_" + pre + "_"
        dh = 32
        HD = H * dh
        cy = CW if cross else D
        fy = cy // P
        ty = TM if cross else T
        ny = ty // P
        with ExitStack() as mem:
            sb = lambda n, s, dt=F32: self.sb(pre + n, s, dt, mem)
            vecs, t_c = self.columns(mem, pre + "c", [A + n for n in ("lnx_g", "lnx_b", "ln3_g", "ln3_b", "li2_b") + (() if cross else ("lny_g", "lny_b"))])
            rows = sb("rows", [P, 2, D])
            ar = self.arrival(pre + "rows")
            for i, n in enumerate(("li1_b", "li3_b")):
                t_rows = ar.dma(self.sp, rows[:, i, :], a[A + n].partition_broadcast(P))
            li1 = sb("li1", [P, HD // P, D])
            t_li1 = self.arrival(pre + "li1").dma(self.sp, li1[:, :, :], a[A + "li1_w"].rearrange("(f p) n -> p f n", p=P))
            core = sb("core", [P, NC, D])
            y = sb("y", [P, NC, D])

            affine = lambda g, b, dst: self.affine_copy(vecs[A + g], vecs[A + b], t_c, dst)
            with ExitStack() as att:
                ab = lambda n, s, dt=F32: self.sb(pre + n, s, dt, att)
                v = ab("v", [P, ny, HD])
                jobs = []
                attention = self.attend(pre, jobs, dh, dh ** -0.5, att, ty // B, nbuf=2 if cross else 3)
                next(attention)
                dq, dk = self.scratch(pre + "q", HD, T), self.ctx_k if cross else self.scratch(pre + "k", HD, ty)
                with ExitStack() as tmp:
                    tb = lambda n, s, dt=F32: self.sb(pre + n, s, dt, tmp)
                    w, tw = {}, {}
                    for n in ("wq",) if cross else ("wq", "wk", "wv"):
                        w[n] = tb(n, [P, FC, HD])
                        arr = self.arrival(pre + n)
                        for f in range(FC):
                            tw[n] = arr.dma(self.sp, w[n][:, f, :].rearrange("p (h d) -> p h d", h=H),
                                            a[A + n][:, f * P:(f + 1) * P, :].rearrange("h p d -> p h d"))
                    ring = self.parts_out(tmp, pre + "p")
                    done = self.normalize(xb, core, NC, xb_ready)
                    xcols = lambda f, n: self.xnT[:, f, n * BANK:(n + 1) * BANK]
                    if cross:
                        t_x = self.to_features(core, D, NC, done, affine("lnx_g", "lnx_b", self.xnT))
                        r_k = self.ctx_k_ready
                        arr = self.arrival(pre + "v")
                        t_v = [arr.dma(self.sp, v[:, c:c + 4, :], self.ctx_v[c * P:(c + 4) * P, :].rearrange("(c p) n -> p c n", p=P), self.ctx_v_ready)
                               for c in range(0, MC, 4)]
                    else:
                        yT = tb("ynT", [P, FC, T])

                        def both(f, n, view, t):
                            affine("lnx_g", "lnx_b", self.xnT)(f, n, view, t)
                            return affine("lny_g", "lny_b", yT)(f, n, view, t)
                        t_x = self.to_features(core, D, NC, done, both)
                        r_k = self.project_parts(ring, w["wk"], FC, lambda f, n: yT[:, f, n * BANK:(n + 1) * BANK], tw["wk"], t_x, None, dk, T, HD)
                        t_v = []
                    r_q = self.project_parts(ring, w["wq"], FC, xcols, tw["wq"], t_x, None, dq, T, HD)
                    self.flush_parts()
                    t_o = []

                    def settled(job, raw, t_raw, rden, t_rden):
                        b, g = job["b"], job["g"]
                        t_o.append(self.V(lambda e: e.tensor_tensor(oT[:, g, b * S:(b + 1) * S], raw[:, :], rden, ALU.mult), t_rden))
                        return t_o[-1]
                    for b in range(B):
                        for g in range(4):
                            kn = [2 * b, 2 * b + 1] if cross else [b]
                            jobs.append(dict(q=(dq, b * S), k=(dk, b * (ty // B)), rows=g * P, keys=ty // B, mode="full" if cross else "upper",
                                             b=b, g=g, v=lambda c, h, b=b, g=g: v[:, b * (ny // B) + c, (4 * g + h) * dh:(4 * g + h + 1) * dh],
                                             v_ready=t_v, ready=[r_q[g, b]] + [r_k[g, n] for n in kn], done=settled))
                    next(attention)
                    for c in range(0 if cross else NC):
                        bank = self.banks.next()
                        t = self.chain(ps[:, bank.at, :], [(yT[:, f, c * P:(c + 1) * P], w["wv"][:, f, :]) for f in range(FC)], bank.free, tw["wv"], t_x)
                        t = self.copy(self.act, v[:, c, :], ps[:, bank.at, :], t)
                        bank.free = [t]
                        t_v.append(t)
                    for c in range(NC):
                        t_yb = self.G(lambda e, c=c: e.tensor_tensor(y[:, c, :], xb[:, c, :], rows[:, 0, :], ALU.add), xb_ready[c], t_rows)
                    next(attention)
                    self.fence(*[s.free for s in ring.slots])
                oT = ab("oT", [P, 4, T])
                for _ in attention:
                    pass
                t_y = []
                for c in range(NC):
                    bank = self.banks.next()
                    t = self.chain(ps[:, bank.at, 0:D], [(oT[:, g, c * P:(c + 1) * P], li1[:, g, :]) for g in range(4)], bank.free, t_o, t_li1)
                    t = self.V(lambda e, c=c, b=bank.at: e.tensor_tensor(y[:, c, :], y[:, c, :], ps[:, b, 0:D], ALU.add), t, t_yb)
                    bank.free = [t]
                    t_y.append(t)
                self.fence()
            li2, li3 = sb("li2", [P, FC, HID]), sb("li3", [P, HC, D])
            t_li2 = self.arrival(pre + "li2").dma(self.sp, li2[:, :, :], a[A + "li2_w"].rearrange("(f p) n -> p f n", p=P))
            t_li3 = self.arrival(pre + "li3").dma(self.sp, li3[:, :, :], a[A + "li3_w"].rearrange("(f p) n -> p f n", p=P))
            hT = sb("hT", [P, HC, T])
            done = self.normalize(y, core, NC, t_y)
            t_m = self.to_features(core, D, NC, done, affine("ln3_g", "ln3_b", self.xnT))
            for c in range(NC):
                t_1 = self.G(lambda e, c=c: e.tensor_tensor(y[:, c, :], y[:, c, :], xb[:, c, :], ALU.add), done[c])
                t_1 = self.G(lambda e, c=c: e.tensor_tensor(y[:, c, :], y[:, c, :], rows[:, 1, :], ALU.add), t_1)
            t_h = []
            for n in range(T // BANK):
                for m in range(HC):
                    bank = self.banks.next()
                    t = self.chain(ps[:, bank.at, :], [(li2[:, f, m * P:(m + 1) * P], self.xnT[:, f, n * BANK:(n + 1) * BANK]) for f in range(FC)],
                                   bank.free, t_li2, t_m)
                    t = self.A(lambda e, m=m, n=n, b=bank.at: e.activation(hT[:, m, n * BANK:(n + 1) * BANK], ps[:, b, :], ACT.Gelu,
                                                                          bias=vecs[A + "li2_b"][:, m:m + 1]), t, t_c)
                    bank.free = [t]
                t_h.append(t)
            out = []
            for c in range(NC):
                bank = self.banks.next()
                t = self.chain(ps[:, bank.at, 0:D], [(hT[:, m, c * P:(c + 1) * P], li3[:, m, :]) for m in range(HC)], bank.free, t_h[c // SC], t_li3)
                t = self.V(lambda e, c=c, b=bank.at: e.tensor_tensor(xb[:, c, :], y[:, c, :], ps[:, b, 0:D], ALU.add), t, t_1)
                bank.free = [t]
                out.append(t)
            self.fence()
        return out

    def double_attention(self):
        a = self.a
        with ExitStack() as mem:
            gb = self.sb("da_gb", [P, 4, D], F32, mem)
            arr = self.arrival("dagb")
            for i, n in enumerate(("ln1_g", "ln1_b", "ln2_g", "ln2_b")):
                t_gb = arr.dma(self.sp, gb[:, i, :], a["L1_xattn_" + n].partition_broadcast(P))
            xb = self.xn
            done = self.normalize(self.x, xb, NC, self.x_ready)
            done = self.normalize(xb, xb, NC, done, gb[:, 0, :], gb[:, 1, :], t_gb)
            done = self.mha("a1", xb, done, False)
            done = self.normalize(xb, xb, NC, done, gb[:, 2, :], gb[:, 3, :], t_gb)
            done = self.mha("a2", xb, done, True)
            self.x_ready = [self.G(lambda e, c=c: e.tensor_tensor(self.x[:, c, :], self.x[:, c, :], xb[:, c, :], ALU.add), done[c])
                            for c in range(NC)]
            self.fence()

    def swiglu(self):
        a, ps = self.a, self.ps
        NT = NC + E1 - 1
        with ExitStack() as mem:
            sb = lambda n, s, dt=F32: self.sb("sw_" + n, s, dt, mem)
            wr = sb("wr", [P, FC, E1])
            t_wr = self.arrival("swwr").dma(self.sp, wr[:, :, :], a["L1_ffn_w_router"].rearrange("(f p) e -> p f e", p=P))
            zero = sb("zero", [P, D])
            t_zero = self.G(lambda e: e.memset(zero[:, :], 0.0))
            xg = self.nc.dram_tensor("scratch_swx", (NT * P, D), F32).ap()
            yo = self.nc.dram_tensor("scratch_swy", (NT * P, D), F32).ap()
            t_z = self.arrival("swz").dma(self.sp, xg.rearrange("(i p) d -> p i d", p=P),
                                          zero[:, :].unsqueeze(1).broadcast_to([P, NT, D]), t_zero)
            wv = sb("wv", [P, E1, FC, 2 * HID])
            wp = sb("wp", [P, E1, HC, D])
            t_w = []
            for x in range(E1):
                arr = self.arrival(f"sww{x}")
                arr.dma(self.sp, wv[:, x, :, :], a["L1_ffn_w_v"][x].rearrange("(f p) n -> p f n", p=P))
                t_w.append(arr.dma(self.sp, wp[:, x, :, :], a["L1_ffn_w_proj"][x].rearrange("(f p) n -> p f n", p=P)))
            iota_e = sb("iota_e", [P, E1])
            t_i = self.G(lambda e: e.iota(iota_e[:, :], pattern=[[1, E1]], base=0, channel_multiplier=0, allow_small_or_imprecise_dtypes=True))
            full = sb("full", [P, NC])
            t_i = self.G(lambda e: e.iota(full[:, :], pattern=[[P, NC]], base=0, channel_multiplier=0, allow_small_or_imprecise_dtypes=True))
            tile_no = sb("tile_no", [1, NT])
            t_i = self.G(lambda e: e.iota(tile_no[:, :], pattern=[[1, NT]], base=0, channel_multiplier=0, allow_small_or_imprecise_dtypes=True))
            before = sb("before", [P, P])
            t_b = self.G(lambda e: e.memset(before[:, :], 1.0))
            t_b = self.G(lambda e: e.affine_select(out=before[:, :], in_=before[:, :], compare_op=ALU.is_gt, fill=0.0, base=0,
                                                   pattern=[[1, P]], channel_multiplier=-1), t_b)
            self.norm_x()
            top, who, t = self.route(mem, "swr", wr, E1, None, t_wr)
            pick = sb("pick", [P, NC, E1])
            t_pick = self.V(lambda e: e.tensor_tensor(pick[:, :, :], iota_e[:, :].unsqueeze(1).broadcast_to([P, NC, E1]),
                                                      who[:, :, 0:1].broadcast_to([P, NC, E1]), ALU.is_equal), t, t_i)
            bank = self.banks.next()
            flat = pick[:, :, :].rearrange("p c e -> p (c e)")
            self.pe.wait(bank.free, t_pick, t_b, self.t_ones)
            for back in range(NC):
                self.pe.do(lambda e, back=back, b=bank.at: e.matmul(
                    ps[:, b, back * E1:NC * E1], (self.ones if back else before)[:, :], flat[:, 0:(NC - back) * E1],
                    start=back == 0, stop=back == NC - 1), tick=False)
            t = self.chain(ps[:, bank.at, NC * E1:(NC + 1) * E1], [(self.ones[:, :], pick[:, c, :]) for c in range(NC)])
            place = sb("place", [P, NC + 1, E1])
            t = self.V(lambda e, b=bank.at: e.tensor_copy(place[:, :, :].rearrange("p c e -> p (c e)"), ps[:, b, 0:(NC + 1) * E1]), t)
            bank.free = [t]
            some = sb("some", [P, E1, NC])
            ends = sb("ends", [P, 2, E1])
            t = self.V(lambda e: e.tensor_tensor(some[:, :, :], full[:, :].unsqueeze(1).broadcast_to([P, E1, NC]),
                                                 place[:, NC, :].unsqueeze(2).broadcast_to([P, E1, NC]), ALU.is_lt), t, t_i)
            t = self.V(lambda e: e.tensor_reduce(ends[:, 0, :], some[:, :, :], AX.X, ALU.add), t)
            t = self.V(lambda e: e.tensor_copy(ends[:, 1, :], ends[:, 0, :]), t)
            for x in range(1, E1):
                t = self.V(lambda e, x=x: e.tensor_tensor(ends[:, 1, x:x + 1], ends[:, 1, x:x + 1], ends[:, 1, x - 1:x], ALU.add), t)
            t_ends = t
            slot = sb("slot", [P, NC])
            to = sb("to", [P, NC], U32)
            t = self.V(lambda e: e.tensor_tensor(ends[:, 0, :], ends[:, 1, :], ends[:, 0, :], ALU.subtract), t_ends)
            t = self.V(lambda e: e.scalar_tensor_tensor(place[:, 0:NC, :], ends[:, 0, :].unsqueeze(1).broadcast_to([P, NC, E1]), float(P),
                                                        place[:, 0:NC, :], ALU.mult, ALU.add), t)
            t = self.V(lambda e: e.tensor_tensor(place[:, 0:NC, :], place[:, 0:NC, :], pick[:, :, :], ALU.mult), t)
            t = self.V(lambda e: e.tensor_reduce(slot[:, :], place[:, 0:NC, :], AX.X, ALU.add), t)
            t_to = self.V(lambda e: e.tensor_copy(to[:, :], slot[:, :]), t)
            past = sb("past", [1, NT, E1 - 1])
            owner = sb("owner", [1, NT])
            owner_i = sb("owner_i", [1, NT], I32)
            t = self.V(lambda e: e.tensor_tensor(past[:, :, :], tile_no[:, :].unsqueeze(2).broadcast_to([1, NT, E1 - 1]),
                                                 ends[0:1, 1, 0:E1 - 1].unsqueeze(1).broadcast_to([1, NT, E1 - 1]), ALU.is_ge), t_ends)
            t = self.V(lambda e: e.tensor_reduce(owner[:, :], past[:, :, :], AX.X, ALU.add), t)
            t_owner = self.V(lambda e: e.tensor_copy(owner_i[:, :], owner[:, :]), t)
            sc = self.arrival("swsc")
            self.pool.wait(t_to, t_z, self.xn_ready)
            for c in range(NC):
                sc.count += 16
                self.pool.items.append(lambda e, c=c: e.indirect_dma_start(
                    xg, bass.IndirectOffsetOnAxis(ap=to[:, c:c + 1], axis=0), self.xn[:, c, :], None).then_inc(sc.sem, 16))
            t_sc = (sc.sem, sc.count)
            xs = sb("xs", [P, NT, D])
            xgT = sb("xgT", [P, NT, D])
            t_xs = []
            for i in range(NT):
                if i % 3 == 0:
                    n = min(3, NT - i)
                    t = self.arrival(f"swxs{i}").dma(self.sp, xs[:, i:i + n, :], xg[i * P:(i + n) * P, :].rearrange("(r p) d -> p r d", p=P), t_sc)
                t_xs.append(t)
            hs = Ring([sb(f"h{i}", [P, HID]) for i in range(2)])
            hTs = Ring([sb(f"hT{i}", [P, HID]) for i in range(2)])
            gates = Ring([sb(f"gt{i}", [P, BANK]) for i in range(2)])
            os_ = Ring([(sb(f"o{i}", [P, D]), self.arrival(f"swo{i}")) for i in range(2)])
            expert = {}
            t_T, t_h, t_done = {}, {}, []

            def turn(i):
                bank = self.banks.next()
                for f in range(FC):
                    t = self.pe.do(lambda e, f=f, i=i, b=bank.at: e.transpose(
                        ps[:, b, f * P:(f + 1) * P], xs[:, i, f * P:(f + 1) * P], self.ident[:, :]), t_xs[i], bank.free, tick=f == FC - 1)
                t_T[i] = self.copy(self.act, xgT[:, i, :], ps[:, bank.at, 0:D], t)
                bank.free = [t_T[i]]

            def up(i):
                self.pe.wait(t_owner)
                self.pe.items.append(lambda e: expert.update({i: e.value_load(owner_i[0:1, i:i + 1], min_val=0, max_val=E1 - 1)}))
                h = hs.next()
                for n in range(HID // BANK):
                    gate, val = self.banks.next(), self.banks.next()
                    for bank, off in ((gate, n * BANK), (val, HID + n * BANK)):
                        self.pe.wait(bank.free, t_w, t_T[i])
                        for f in range(FC):
                            t = self.pe.do(lambda e, f=f, off=off, b=bank.at: e.matmul(
                                ps[:, b, :], xgT[:, i, f * P:(f + 1) * P],
                                wv[:, bass.ds(expert[i], 1), f, off:off + BANK].rearrange("p o n -> p (o n)"), start=f == 0, stop=f == FC - 1),
                                tick=f == FC - 1)
                        if bank is gate:
                            g = gates.next()
                            t_g = self.A(lambda e, g=g, b=bank.at: e.activation(g.at[:, :], ps[:, b, :], ACT.Silu), t, g.free)
                            gate.free = [t_g]
                    t1 = self.V(lambda e, g=g, n=n, b=val.at: e.tensor_tensor(
                        h.at[:, n * BANK:(n + 1) * BANK], g.at[:, :], ps[:, b, :], ALU.mult), t, t_g, h.free)
                    val.free, g.free = [t1], [t1]
                    t_h[i, n] = t1
                t_h[i] = h

            def down(i):
                h, hT = t_h[i], hTs.next()
                t_hT = []
                for n in range(HID // BANK):
                    bank = self.banks.next()
                    for k in range(4):
                        t = self.pe.do(lambda e, k=k, n=n, b=bank.at: e.transpose(
                            ps[:, b, k * P:(k + 1) * P], h.at[:, (4 * n + k) * P:(4 * n + k + 1) * P], self.ident[:, :]),
                            t_h[i, n], bank.free, tick=k == 3)
                    t1 = self.copy(self.act if n else self.dve, hT.at[:, n * BANK:(n + 1) * BANK], ps[:, bank.at, :], t, hT.free)
                    bank.free = [t1]
                    t_hT.append(t1)
                h.free = [t]
                return hT, t_hT

            def project(i, hT, t_hT):
                bank = self.banks.next()
                self.pe.wait(bank.free)
                for m in range(HC):
                    t = self.pe.do(lambda e, m=m, b=bank.at: e.matmul(
                        ps[:, b, 0:D], hT.at[:, m * P:(m + 1) * P],
                        wp[:, bass.ds(expert[i], 1), m, :].rearrange("p o n -> p (o n)"), start=m == 0, stop=m == HC - 1),
                        t_hT[m // 4], tick=m == HC - 1)
                hT.free = [t]
                o = os_.next()
                ot, oarr = o.at
                t1 = self.V(lambda e, b=bank.at, ot=ot: e.tensor_copy(ot[:, :], ps[:, b, 0:D]), t, o.free)
                bank.free = [t1]
                t2 = oarr.dma(self.sp, yo[i * P:(i + 1) * P, :], ot[:, :], t1)
                o.free = [t2]
                t_done.append(t2)

            turn(0)
            turned = None
            for i in range(NT):
                if i + 1 < NT:
                    turn(i + 1)
                if i:
                    turned = down(i - 1)
                up(i)
                if i:
                    project(i - 1, *turned)
            project(NT - 1, *down(NT - 1))
            gb = Ring([(sb(f"g{i}", [P, D]), self.arrival(f"swga{i}")) for i in range(NC)])
            self.pool.wait(t_done)
            ready = []
            for c in range(NC):
                gt, arr = gb.next().at
                arr.count += 16
                self.pool.items.append(lambda e, c=c, gt=gt, arr=arr: e.indirect_dma_start(
                    gt[:, :], None, yo, bass.IndirectOffsetOnAxis(ap=to[:, c:c + 1], axis=0)).then_inc(arr.sem, 16))
                ready.append(self.V(lambda e, c=c, gt=gt: e.tensor_tensor(self.x[:, c, :], self.x[:, c, :], gt[:, :], ALU.add),
                                    (arr.sem, arr.count), self.x_ready[c]))
            self.x_ready = ready


STAGE_FUNCTIONS = {0: Program.performer, 1: Program.cross_attention, 2: Program.moe, 3: Program.retention,
                   4: Program.double_attention, 5: Program.swiglu}


def build(nc, names, aps, out, stages):
    with ExitStack() as ctx:
        p = Program(nc, ctx, dict(zip(names, aps)), out, stages)
        block = ctx.enter_context(nc.Block())

        @block.sync
        def _(e):
            for f in p.sp.items:
                f(e)

        @block.tensor
        def _(e):
            for f in p.pe.items:
                f(e)

        @block.scalar
        def _(e):
            for f in p.act.items:
                f(e)

        @block.vector
        def _(e):
            for f in p.dve.items:
                f(e)

        @block.gpsimd
        def _(e):
            for f in p.pool.items:
                f(e)
    return p


NAMES = ["x", "ctx_512"] + ["L0_attn_" + n for n in ("Wq", "Wk", "Wv", "Wo", "bo", "P")] \
    + ["L0_xattn_" + n for n in ("Wk", "bk", "Wq", "bq", "Wv", "bv", "Wck", "bck", "Wcq", "bcq", "Wcv", "bcv", "Wp", "bp")] \
    + ["L0_ffn_" + n for n in ("Wr", "br", "W1", "b1", "W2", "b2")] \
    + ["L1_attn_" + n for n in ("W_qkv", "W_o", "log_gamma")] \
    + ["L1_xattn_" + n for n in ("ln1_g", "ln1_b", "ln2_g", "ln2_b")] \
    + [f"L1_xattn_{a}_{n}" for a in ("a1", "a2") for n in (
        "wq", "wk", "wv", "li1_w", "li1_b", "lnx_g", "lnx_b", "lny_g", "lny_b", "ln3_g", "ln3_b",
        "li2_w", "li2_b", "li3_w", "li3_b")] \
    + ["L1_ffn_" + n for n in ("w_router", "w_v", "w_proj")]

STAGES = (0, 1, 2, 3, 4, 5)


def kernel(**inputs):
    import concourse.bacc as bacc
    from concourse.bass_utils import run_bass_kernel_spmd as run

    nc = bacc.Bacc("TRN2", target_bir_lowering=False, num_devices=1)
    arrays, aps = {}, []
    for name in NAMES:
        v = np.ascontiguousarray(inputs[name])
        arrays["in_" + name] = v
        aps.append(nc.dram_tensor("in_" + name, v.shape, mybir.dt.from_np(v.dtype), kind="ExternalInput").ap())
    out = nc.dram_tensor("out_0", (B, S, D), F32, kind="ExternalOutput").ap()
    build(nc, NAMES, aps, out, STAGES)
    r = run(nc, [arrays], core_ids=[0])
    return np.asarray(r.results[0]["out_0"])
```

```python
from contextlib import ExitStack

import numpy as np

import concourse.bass as bass
from concourse import mybir

F32 = mybir.dt.float32
BF16 = mybir.dt.bfloat16
U32 = mybir.dt.uint32
I32 = mybir.dt.int32
ALU = mybir.AluOpType
ACT = mybir.ActivationFunctionType
AX = mybir.AxisListType

P = 128
B, S, D = 2, 512, 256
T = B * S
NC = T // P
SC = S // P
FC = D // P
MEM, CW = 1024, 128
TM = B * MEM
MC = TM // P
H = 16
LN_EPS = 1e-5
PH, PM = 64, 64
PAIRS = H * PH // P
DN = PH ** -0.25
KEPS = 1e-4
E0, HID = 8, 1024
CAP = -(-12 * T // (10 * E0))
E1 = 4
HC = HID // P
NEG = -1e30
BANK = 512


class Lane:

    def __init__(self, name, sem):
        self.name, self.sem, self.count, self.items, self.seen = name, sem, 0, [], {}

    def wait(self, *tickets):
        for t in tickets:
            if t is None:
                continue
            if isinstance(t, list):
                self.wait(*t)
                continue
            sem, value = t
            if self.seen.get(id(sem), 0) < value:
                self.seen[id(sem)] = value
                self.items.append(lambda e, s=sem, v=value: e.wait_ge(s, v))

    def do(self, make, *tickets, tick=True):
        self.wait(*tickets)
        if not tick:
            self.items.append(lambda e: make(e))
            return None
        self.count += 1
        self.items.append(lambda e: make(e).then_inc(self.sem, 1))
        return (self.sem, self.count)

    def last(self):
        return (self.sem, self.count) if self.count else None


class Arrival:

    def __init__(self, sem):
        self.sem, self.count = sem, 0

    def dma(self, lane, out, in_, *tickets):
        lane.wait(*tickets)
        self.count += 16
        lane.items.append(lambda e: e.dma_start(out, in_).then_inc(self.sem, 16))
        return (self.sem, self.count)


class Slot:

    def __init__(self, at):
        self.at, self.free = at, []


class Ring:
    def __init__(self, slots):
        self.slots, self.n = [Slot(s) for s in slots], 0

    def next(self):
        s = self.slots[self.n % len(self.slots)]
        self.n += 1
        return s


class Program:
    def __init__(self, nc, ctx, a, out):
        self.nc, self.ctx, self.a, self.out = nc, ctx, a, out
        self.pe, self.act, self.dve, self.pool, self.sp = (
            Lane(n, self.sem("s_" + n)) for n in ("pe", "act", "dve", "pool", "sp"))
        self.lanes = [self.pe, self.act, self.dve, self.pool]
        self.arrivals = []
        self.ps = ctx.enter_context(nc.psum_tensor("psum", [P, 8, BANK], F32))
        self.banks = Ring(range(8))
        self.build()

    def sem(self, name):
        return self.ctx.enter_context(self.nc.semaphore(name))

    def arrival(self, name):
        s = Arrival(self.sem("d_" + name))
        self.arrivals.append(s)
        return s

    def sb(self, name, shape, dt=F32, ctx=None):
        return (ctx or self.ctx).enter_context(self.nc.sbuf_tensor(name, shape, dt))

    def fence(self, *tickets):
        last = [l.last() for l in self.lanes]
        for l in self.lanes + [self.sp]:
            l.wait(*last, *tickets)

    def chain(self, out, terms, *tickets, tick=True):
        self.pe.wait(*tickets)
        for i, (l, r) in enumerate(terms):
            end = i == len(terms) - 1
            t = self.pe.do(lambda e, l=l, r=r, i=i, end=end: e.matmul(out, l, r, start=i == 0, stop=end),
                           tick=tick and end)
        return t

    def V(self, make, *tickets):
        return self.dve.do(make, *tickets)

    def A(self, make, *tickets):
        return self.act.do(make, *tickets)

    def G(self, make, *tickets):
        return self.pool.do(make, self.pool.last(), *tickets)

    def copy(self, lane, out, in_, *tickets):
        if lane is self.act:
            return lane.do(lambda e: e.activation(out, in_, ACT.Copy), *tickets)
        return lane.do(lambda e: e.tensor_copy(out, in_), *tickets)

    def constants(self):
        z = self.sb("ident", [P, P])
        self.ident = z
        t = self.G(lambda e: e.memset(z[:, :], 0.0))
        t = self.G(lambda e: e.affine_select(out=z[:, :], in_=z[:, :], compare_op=ALU.not_equal, fill=1.0, base=0,
                                             pattern=[[-1, P]], channel_multiplier=1), t)
        self.t_ident = t
        self.ones = self.sb("ones", [P, P])
        self.t_ones = self.G(lambda e: e.memset(self.ones[:, :], 1.0))
        self.identb = self.sb("identb", [P, P], BF16)
        self.G(lambda e: e.tensor_copy(self.identb[:, :], z[:, :]), t)
        mf = self.sb("maskf", [P, 2, P])
        self.mask_qk = self.sb("mask_qk", [P, P], BF16)
        self.mask_kq = self.sb("mask_kq", [P, P], BF16)
        t = self.G(lambda e: e.memset(mf[:, :, :], 0.0))
        t1 = self.G(lambda e: e.affine_select(out=mf[:, 0, :], in_=mf[:, 0, :], compare_op=ALU.is_ge, fill=NEG,
                                              base=0, pattern=[[-1, P]], channel_multiplier=1), t)
        t2 = self.G(lambda e: e.affine_select(out=mf[:, 1, :], in_=mf[:, 1, :], compare_op=ALU.is_ge, fill=NEG,
                                              base=0, pattern=[[1, P]], channel_multiplier=-1), t)
        self.G(lambda e: e.tensor_copy(self.mask_qk[:, :], mf[:, 0, :]), t1)
        self.t_const = self.G(lambda e: e.tensor_copy(self.mask_kq[:, :], mf[:, 1, :]), t2)

    def normalize(self, src, dst, chunks, after, gain=None, shift=None, t_gb=None, alike=False):
        self.dve.wait(*self.ln_free)
        groups = range(0, chunks, 4)
        roots = []
        for g in groups:
            for c in range(g, g + 4):
                t = self.V(lambda e, c=c: e.bn_stats(self.ln_raw[:, c, :], src[:, c, :]), after[c])
            roots.append(self.deviation(g, t))
        done = []
        for g, root in zip(groups, roots):
            done += self.apply_norm(src, dst, g, root, gain, shift, t_gb, alike)
        self.ln_free = list(done)
        return done

    def deviation(self, g, t):
        raw, agg, std, four = self.ln_raw, self.ln_agg, self.ln_std, slice(g, g + 4)
        for c in range(g, g + 4):
            t = self.V(lambda e, c=c: e.bn_aggr(agg[:, c, :], raw[:, c, :]), t if c == g else None)
        t = self.V(lambda e: e.tensor_scalar(std[:, four, 0], agg[:, four, 1], LN_EPS, None, ALU.add), t)
        return self.A(lambda e: e.activation(std[:, four, 1], std[:, four, 0], ACT.Sqrt), t)

    def apply_norm(self, src, dst, g, root, gain, shift, t_gb, alike):
        agg, std, four = self.ln_agg, self.ln_std, slice(g, g + 4)
        t = self.V(lambda e: e.reciprocal(std[:, four, 0], std[:, four, 1]), root)
        if gain is None:
            t = self.V(lambda e: e.scalar_tensor_tensor(std[:, four, 1], agg[:, four, 0], -1.0, std[:, four, 0], ALU.mult, ALU.mult), t)
        done = []
        for c in range(g, g + 4):
            if gain is None and c % 2 and not alike:
                done.append(self.A(lambda e, c=c: e.activation(dst[:, c, :], src[:, c, :], ACT.Identity, bias=std[:, c, 1:2], scale=std[:, c, 0:1]), t))
            elif gain is None:
                done.append(self.V(lambda e, c=c: e.tensor_scalar(dst[:, c, :], src[:, c, :], agg[:, c, 0:1], std[:, c, 0:1],
                                                                  ALU.subtract, ALU.mult), t))
            elif c == g + 3:
                t1 = self.G(lambda e, c=c: e.tensor_scalar(dst[:, c, :], src[:, c, :], agg[:, c, 0:1], std[:, c, 0:1], ALU.subtract, ALU.mult), t)
                t1 = self.G(lambda e, c=c: e.tensor_tensor(dst[:, c, :], dst[:, c, :], gain, ALU.mult), t1, t_gb)
                done.append(self.G(lambda e, c=c: e.tensor_tensor(dst[:, c, :], dst[:, c, :], shift, ALU.add), t1))
            else:
                t1 = self.V(lambda e, c=c: e.scalar_tensor_tensor(dst[:, c, :], src[:, c, :], agg[:, c, 0:1], gain, ALU.subtract, ALU.mult), t, t_gb)
                done.append(self.V(lambda e, c=c: e.scalar_tensor_tensor(dst[:, c, :], dst[:, c, :], std[:, c, 0:1], shift, ALU.mult, ALU.add), t1))
        return done

    def norm_as_it_comes(self, src, dst, gain=None, shift=None, t_gb=None, emit=None, alike=False):
        done, turned = [], []
        self.dve.wait(*self.ln_free)

        def turn(n):
            turned.extend(self.to_features(dst, D, NC, done, emit, [n]))

        def push(c, t):
            t = self.V(lambda e: e.bn_stats(self.ln_raw[:, c, :], src[:, c, :]), t)
            if c % 4 == 3:
                done.extend(self.apply_norm(src, dst, c - 3, self.deviation(c - 3, t), gain, shift, t_gb, alike))
                self.ln_free = done[-4:]
            if emit and c == NC - 2:
                turn(0)
            if emit and c == NC - 1:
                turn(1)
        return push, done, turned

    def to_features(self, src, width, chunks, ready, emit, groups=None):
        out = []
        for n in groups or range(chunks // 4):
            for f in range(width // P):
                bank = self.banks.next()
                self.pe.wait(*bank.free, self.t_ident)
                for k in range(4):
                    c = 4 * n + k
                    t = self.pe.do(lambda e, k=k, c=c, f=f, b=bank.at: e.transpose(
                        self.ps[:, b, k * P:(k + 1) * P], src[:, c, f * P:(f + 1) * P], self.ident[:, :]),
                        ready[c], tick=k == 3)
                t = emit(f, n, self.ps[:, bank.at, :], t)
                bank.free = [t]
                out.append(t)
        return out

    def feature_copy(self, dst):
        def emit(f, n, view, t):
            lane = self.act if (f + n) % 2 == 0 else self.dve
            return self.copy(lane, dst[:, f, n * BANK:(n + 1) * BANK], view, t)
        return emit

    def build(self):
        a = self.a
        self.ln_free, self.unsent, self.normed = [], None, None
        self.ln_raw = self.sb("ln_raw", [P, MC, 6])
        self.ln_agg = self.sb("ln_agg", [P, MC, 2])
        self.ln_std = self.sb("ln_std", [P, MC, 2])
        self.constants()
        self.x = self.sb("x", [P, NC, D])
        self.xn = self.sb("xn", [P, NC, D])
        self.xnT = self.sb("xnT", [P, FC, T])
        self.ctxT = self.sb("ctxT", [P, TM])
        xin = a["x"].rearrange("b (c p) d -> p (b c) d", p=P)
        d_xs = [self.arrival(f"x{i}") for i in range(2)]
        t_x = [d_xs[i].dma(self.sp, self.x[:, 4 * i:4 * i + 4, :], xin[:, 4 * i:4 * i + 4, :]) for i in range(2)]
        self.x_ready = [t_x[c // 4] for c in range(NC)]
        self.wr = {}
        for n, e in (("L0_ffn_Wr", E0), ("L1_ffn_w_router", E1)):
            tile = self.sb(n, [P, FC, e])
            self.wr[n] = tile, self.arrival(n).dma(self.sp, tile[:, :, :], a[n].rearrange("(f p) e -> p f e", p=P))
        self.da_rows = self.sb("da_rows", [P, 4, D])
        load_columns, turn_columns = self.columns()

        def load_rows():
            arr = self.arrival("darows")
            for i, n in enumerate(("ln1_g", "ln1_b", "ln2_g", "ln2_b")):
                self.t_da_rows = arr.dma(self.sp, self.da_rows[:, i, :], a["L1_xattn_" + n].partition_broadcast(P))
        with ExitStack() as early:
            load_weights = self.cross_attention_weights(early)
            self.performer([load_columns, load_weights, load_rows], [turn_columns])
            self.cross_attention()
        with ExitStack() as middle:
            load_weights, turn_weights = self.retention_weights(middle)
            self.moe(load_weights, turn_weights)
            self.retention()
        self.double_attention()
        self.swiglu()
        for b in range(B):
            half = slice(b * SC, (b + 1) * SC)
            self.arrival(f"out{b}").dma(self.sp, self.out[b].rearrange("(c p) d -> p c d", p=P), self.x[:, half, :], *self.x_ready[half])
        for d in self.arrivals:
            if d.count:
                self.sp.wait((d.sem, d.count))

    def norm_x(self):
        if self.normed:
            self.xn_ready, self.xnT_ready = self.normed
            return
        self.xn_ready = self.normalize(self.x, self.xn, NC, self.x_ready, alike=True)
        self.xnT_ready = self.to_features(self.xn, D, NC, self.xn_ready, self.feature_copy(self.xnT))

    def new_x(self, turn=True, alike=False):
        push, done, turned = self.norm_as_it_comes(self.x, self.xn, emit=self.feature_copy(self.xnT) if turn else None, alike=alike)
        self.normed = done, turned
        self.x_ready = []

        def final(c, t):
            self.x_ready.append(t)
            push(c, t)
        return final

    def performer(self, loads_beside, turns_beside):
        a, ps = self.a, self.ps
        with ExitStack() as mem:
            sb = lambda n, s, dt=F32: self.sb("pf_" + n, s, dt, mem)
            wq, wk, wv = (sb(n, [P, FC, H * PH]) for n in ("wq", "wk", "wv"))
            wo = sb("wo", [P, PAIRS, D])
            praw = sb("praw", [P, P])
            pbd = sb("pbd", [P, P])
            half = sb("half", [P, 2])
            bo = sb("bo", [P, D])
            kdd = sb("kdd", [P, PAIRS, NC, P])
            diag = sb("diag", [P, 2, PAIRS, NC, 2])
            kmax = sb("kmax", [P, 2 * PAIRS])
            gm = sb("gm", [P, 4])
            headT = Ring([sb(f"hT{i}", [P, T]) for i in range(2)])
            sq = Ring([sb(f"sq{i}", [P, T]) for i in range(2)])
            qp = Ring([sb(f"qp{i}", [P, NC, P]) for i in range(3)])
            qpT = Ring([sb(f"qpT{i}", [P, T]) for i in range(2)])
            vv = Ring([sb(f"v{i}", [P, NC, 2, PH + 1]) for i in range(2)])
            rden = Ring([sb(f"rd{i}", [P, 2, 2]) for i in range(4)])
            qmx = Ring([sb(f"qmx{i}", [P, NC, 2]) for i in range(2)])
            bd = Ring([sb(f"bd{i}", [P, 2, PH + 1]) for i in range(4)])
            loads = {}
            for n, tile, src in (("k", wk, "L0_attn_Wk"), ("q", wq, "L0_attn_Wq"), ("v", wv, "L0_attn_Wv")):
                loads[n] = self.arrival("pf" + n).dma(self.sp, tile[:, :, :], a[src].rearrange("(f p) n -> p f n", p=P))
            t_z = self.G(lambda e: e.memset(praw[:, :], 0.0))
            d_p = self.arrival("pfp")
            for j in range(2):
                t_p = d_p.dma(self.sp, praw[64 * j:64 * j + 64, 64 * j:64 * j + 64], a["L0_attn_P"], t_z)
            t_bo = self.arrival("pfbo").dma(self.sp, bo[:, :], a["L0_attn_bo"].partition_broadcast(P))
            t_wo = self.arrival("pfwo").dma(self.sp, wo[:, :, :], a["L0_attn_Wo"].rearrange("(f p) n -> p f n", p=P))
            t_h = self.G(lambda e: e.memset(half[:, :], 0.0))
            for j in range(2):
                t_h = self.G(lambda e, j=j: e.memset(half[64 * j:64 * j + 64, j:j + 1], 0.5 * DN * DN), t_h)
            for s in bd.slots:
                s.free = [self.G(lambda e, s=s: e.memset(s.at[:, :, :], 0.0))]
            for s in vv.slots:
                s.free = [self.G(lambda e, s=s: e.memset(s.at[:, :, :, PH:PH + 1], 1.0))]
            bank = self.banks.next()
            t = self.pe.do(lambda e, b=bank.at: e.transpose(ps[:, b, 0:P], praw[:, :], self.ident[:, :]), t_p, self.t_ident)
            t_pbd = self.copy(self.act, pbd[:, :], ps[:, bank.at, 0:P], t)
            bank.free = [t_pbd]

            load_context, turn_context = self.context(mem)
            for load in [load_context] + loads_beside:
                load()
            self.norm_x()
            t_xb = None
            for c in range(NC):
                t_xb = self.G(lambda e, c=c: e.tensor_tensor(self.x[:, c, :], self.x[:, c, :], bo[:, :], ALU.add),
                              self.xn_ready, t_bo)

            def head_projection(w, pair, t_w):
                hT, s2 = headT.next(), sq.next()
                t_hT, t_sq = [], []
                for n in range(T // BANK):
                    bank = self.banks.next()
                    t = self.chain(ps[:, bank.at, :], [(w[:, f, pair * P:(pair + 1) * P], self.xnT[:, f, n * BANK:(n + 1) * BANK])
                                                       for f in range(FC)], bank.free, t_w, self.xnT_ready)
                    cols = slice(n * BANK, (n + 1) * BANK)
                    t1 = self.A(lambda e, b=bank.at, cols=cols: e.activation(hT.at[:, cols], ps[:, b, :], ACT.Copy), t, hT.free)
                    t2 = self.A(lambda e, b=bank.at, cols=cols: e.activation(s2.at[:, cols], ps[:, b, :], ACT.Square), t, s2.free)
                    bank.free = [t2]
                    t_hT.append(t1)
                    t_sq.append(t2)
                return pair, hT, s2, t_hT, t_sq

            def head_features(projection, which):
                pair, hT, s2, t_hT, t_sq = projection
                res = []
                for n in range(2):
                    bank = self.banks.next()
                    for k in range(4):
                        c = 4 * n + k
                        t = self.chain(ps[:, bank.at, k * P:(k + 1) * P], [(hT.at[:, c * P:(c + 1) * P], pbd[:, :])],
                                       bank.free, t_hT[n], t_pbd, tick=k == 3)
                    res.append((bank, t))
                hT.free = [t]
                bank = self.banks.next()
                for c in range(NC):
                    t = self.chain(ps[:, bank.at, 2 * c:2 * c + 2], [(s2.at[:, c * P:(c + 1) * P], half[:, :])],
                                   bank.free, t_sq[c // 4], t_h, tick=c == NC - 1)
                s2.free = [t]
                t_d = self.V(lambda e, b=bank.at: e.tensor_copy(diag[:, which, pair, :, :],
                                                                ps[:, b, 0:2 * NC].rearrange("p (c h) -> p c h", h=2)), t)
                bank.free = [t_d]
                return res, t_d

            heads_of = lambda v: v.rearrange("p c (h m) -> p (c h) m", h=2)
            t_kd, t_kp, queries, values, outputs = [], {}, {}, {}, {}

            def keys(projection):
                pair = projection[0]
                res, t_d = head_features(projection, 1)
                for n, (bank, t) in enumerate(res):
                    t1 = self.V(lambda e, b=bank.at, i=2 * pair + n: e.tensor_reduce(kmax[:, i:i + 1], ps[:, b, :], AX.X, ALU.max), t)
                    t2 = self.A(lambda e, b=bank.at, n=n: e.activation(
                        kdd[:, pair, 4 * n:4 * n + 4, :], ps[:, b, :].rearrange("p (c m) -> p c m", c=4), ACT.Copy), t, t1)
                    bank.free = [t2]
                t_kd.append([t2, t_d])
                return t1

            def key_exp(pair):
                kv = heads_of(kdd[:, pair, :, :])
                kb = diag[:, 1, pair, :, :].rearrange("p c h -> p (c h)")
                t = self.V(lambda e: e.tensor_scalar(kb, kb, gm[:, 2:3], None, ALU.add), t_gm, t_kd[pair])
                t = self.V(lambda e: e.scalar_tensor_tensor(
                    kv, kv, DN, kb.unsqueeze(2).broadcast_to([P, 2 * NC, PM]), ALU.mult, ALU.subtract), t)
                t = self.A(lambda e: e.activation(kdd[:, pair, :, :], kdd[:, pair, :, :], ACT.Exp), t)
                t_kp[pair] = self.G(lambda e: e.tensor_scalar(kdd[:, pair, :, :], kdd[:, pair, :, :], KEPS, None, ALU.add), t)

            def query_exp(projection):
                res, t_d = head_features(projection, 0)
                pair = projection[0]
                mx, q = qmx.next(), qp.next()
                t_e = []
                for n, (bank, t) in enumerate(res):
                    view = ps[:, bank.at, :].rearrange("p (c m) -> p c m", m=PM)
                    mview = mx.at[:, 4 * n:4 * n + 4, :].rearrange("p c h -> p (c h)")
                    dview = diag[:, 0, pair, 4 * n:4 * n + 4, :].rearrange("p c h -> p (c h)")
                    t1 = self.V(lambda e, m=mview, v=view: e.tensor_reduce(m, v, AX.X, ALU.max), t, mx.free)
                    t1 = self.V(lambda e, m=mview, d=dview: e.scalar_tensor_tensor(m, m, DN, d, ALU.mult, ALU.add), t1, t_d)
                    qv = heads_of(q.at[:, 4 * n:4 * n + 4, :])
                    t1 = self.V(lambda e, m=mview, v=view, qv=qv: e.scalar_tensor_tensor(
                        qv, v, DN, m.unsqueeze(2).broadcast_to([P, 8, PM]), ALU.mult, ALU.subtract), t1, q.free)
                    bank.free = [t1]
                    t_e.append(t1)
                mx.free = [t1]
                t = self.A(lambda e: e.activation(q.at[:, :, :], q.at[:, :, :], ACT.Exp), t_e)
                t_qp = self.G(lambda e: e.tensor_scalar(q.at[:, :, :], q.at[:, :, :], KEPS, None, ALU.add), t)
                queries[pair] = q, t_qp

            def value_projection(pair):
                v = vv.next()
                t_v = []
                for n in range(2):
                    bank = self.banks.next()
                    for k in range(4):
                        c = 4 * n + k
                        t = self.chain(ps[:, bank.at, k * P:(k + 1) * P],
                                       [(self.xnT[:, f, c * P:(c + 1) * P], wv[:, f, pair * P:(pair + 1) * P]) for f in range(FC)],
                                       bank.free, loads["v"], self.xnT_ready, tick=k == 3)
                    t = self.A(lambda e, n=n, b=bank.at: e.activation(
                        v.at[:, 4 * n:4 * n + 4, :, 0:PH], ps[:, b, :].rearrange("p (c h m) -> p c h m", c=4, h=2), ACT.Copy), t, v.free)
                    bank.free = [t]
                    t_v.append(t)
                values[pair] = v, t_v

            def contexts(pair):
                v, t_v = values[pair]
                bank = self.banks.next()
                W = 2 * (PH + 1)
                for b in range(B):
                    t = self.chain(ps[:, bank.at, b * W:(b + 1) * W],
                                   [(kdd[:, pair, c, :], v.at[:, c, :, :].rearrange("p h m -> p (h m)")) for c in range(SC * b, SC * b + SC)],
                                   bank.free, t_kp[pair], t_v, tick=b == B - 1)
                v.free = [t]
                blks = []
                for b in range(B):
                    blk = bd.next()
                    for j in range(2):
                        r = slice(64 * j, 64 * j + 64)
                        o = b * W + j * (PH + 1)
                        t_b = self.V(lambda e, r=r, blk=blk, j=j, o=o: e.tensor_copy(blk.at[r, j, :], ps[r, bank.at, o:o + PH + 1]), t, blk.free)
                    blks.append(blk)
                bank.free = [t_b]
                return blks, t_b

            def turn_queries(pair):
                q, t_qp = queries[pair]
                qT = qpT.next()
                t_qT = self.to_features(q.at, P, NC, [t_qp] * NC, lambda f, n, view, t: self.copy(
                    self.act if n else self.dve, qT.at[:, n * BANK:(n + 1) * BANK], view, t, qT.free))
                q.free = list(t_qT)
                return qT, t_qT

            def output(pair, blks, t_b, qT, t_qT):
                y = queries[pair][0]
                ready = []
                for n in range(NC // 2):
                    bank = self.banks.next()
                    view = ps[:, bank.at, 0:4 * (PH + 1)].rearrange("p (c h m) -> p c h m", c=2, h=2)
                    blk = blks[2 * n // SC]
                    for k in range(2):
                        c = 2 * n + k
                        t = self.chain(view[:, k, :, :].rearrange("p h m -> p (h m)"),
                                       [(qT.at[:, c * P:(c + 1) * P], blk.at[:, :, :].rearrange("p h m -> p (h m)"))],
                                       bank.free, t_b, t_qT, tick=k == 1)
                    blk.free = [t]
                    rd = rden.next()
                    t1 = self.V(lambda e, rd=rd, view=view: e.reciprocal(rd.at[:, :, :], view[:, :, :, PH]), t, rd.free)
                    t1 = self.V(lambda e, rd=rd, view=view, n=n: e.tensor_tensor(
                        y.at[:, 2 * n:2 * n + 2, :].rearrange("p c (h m) -> p c h m", h=2), view[:, :, :, 0:PH],
                        rd.at[:, :, :].unsqueeze(3).broadcast_to([P, 2, 2, PH]), ALU.mult), t1, y.free)
                    bank.free, rd.free = [t1], [t1]
                    ready += [t1, t1]
                qT.free = [t]
                outputs[pair] = y, ready

            t_y = []

            def turn_output(pair):
                y, ready = outputs[pair]
                yT = kdd[:, pair, :, :].rearrange("p c m -> p (c m)")
                t = self.to_features(y.at, P, NC, ready, lambda f, n, view, t: self.copy(
                    self.act if n else self.dve, yT[:, n * BANK:(n + 1) * BANK], view, t))
                y.free = list(t)
                t_y.extend(t)

            ahead = head_projection(wk, 0, loads["k"])
            for pair in range(PAIRS):
                now = ahead
                ahead = head_projection(wk, pair + 1, loads["k"]) if pair + 1 < PAIRS else head_projection(wq, 0, loads["q"])
                t_mx = keys(now)
            value_projection(0)
            for turn in [turn_context] + turns_beside:
                turn()
            t = self.V(lambda e: e.tensor_reduce(gm[:, 0:1], kmax[:, :], AX.X, ALU.max), t_mx)
            bank = self.banks.next()
            t = self.pe.do(lambda e, b=bank.at: e.transpose(ps[0:1, b, 0:P], gm[:, 0:1], self.ident[:, :]), t, bank.free)
            t = self.V(lambda e, b=bank.at: e.tensor_reduce(gm[0:1, 1:2], ps[0:1, b, 0:P], AX.X, ALU.max), t)
            t = self.chain(ps[:, bank.at, 0:1], [(self.ones[0:1, :], gm[0:1, 1:2])], t, self.t_ones)
            t_gm = self.V(lambda e, b=bank.at: e.tensor_scalar(gm[:, 2:3], ps[:, b, 0:1], DN, None, ALU.mult), t)
            bank.free = [t_gm]
            key_exp(0)
            now, ahead = ahead, head_projection(wq, 1, loads["q"])
            query_exp(now)
            for pair in range(PAIRS):
                if pair + 1 < PAIRS:
                    key_exp(pair + 1)
                    now = ahead
                    if pair + 2 < PAIRS:
                        ahead = head_projection(wq, pair + 2, loads["q"])
                    query_exp(now)
                blks, t_b = contexts(pair)
                if pair:
                    turn_output(pair - 1)
                qT, t_qT = turn_queries(pair)
                if pair + 1 < PAIRS:
                    value_projection(pair + 1)
                output(pair, blks, t_b, qT, t_qT)
            turn_output(PAIRS - 1)
            final = self.new_x()
            for c in range(NC):
                bank = self.banks.next()
                t = self.chain(ps[:, bank.at, 0:D], [(kdd[:, p, c, :], wo[:, p, :]) for p in range(PAIRS)], bank.free, t_y, t_wo)
                t = self.V(lambda e, c=c, b=bank.at: e.tensor_tensor(self.x[:, c, :], self.x[:, c, :], ps[:, b, 0:D], ALU.add), t, t_xb)
                bank.free = [t]
                final(c, t)
            self.fence()

    COLUMNS = ["L0_xattn_" + n for n in ("bq", "bk", "bcq", "bck")] + ["L0_ffn_b1"] \
        + ["L1_xattn_a1_" + n for n in ("lnx_g", "lnx_b", "lny_g", "lny_b", "ln3_g", "ln3_b", "li2_b")] \
        + ["L1_xattn_a2_" + n for n in ("lnx_g", "lnx_b", "lny_g", "lny_b", "ln3_g", "ln3_b", "li2_b")]

    def columns(self):
        sizes = [int(np.prod(self.a[n].shape)) // P for n in self.COLUMNS]
        total = sum(sizes)
        rows, cols = self.sb("col_rows", [total, P]), self.sb("cols", [P, total])
        self.col, sources = {}, []
        at = 0
        for n, k in zip(self.COLUMNS, sizes):
            src = self.a[n] if len(self.a[n].shape) == 1 else self.a[n].rearrange("e n -> (e n)")
            sources.append((rows[at:at + k, :], src.rearrange("(k p) -> k p", p=P)))
            self.col[n] = cols[:, at:at + k]
            at += k
        arr = self.arrival("cols")

        def load():
            for dst, src in sources:
                arr.dma(self.sp, dst, src)

        def turn():
            bank = self.banks.next()
            t = self.pe.do(lambda e: e.transpose(self.ps[:, bank.at, 0:total], rows[:, :], self.ident[0:total, 0:total]),
                           (arr.sem, arr.count), bank.free, self.t_ident)
            self.t_col = self.copy(self.act, cols[:, :], self.ps[:, bank.at, 0:total], t)
            bank.free = [self.t_col]
        return load, turn

    PARTS16 = [([(0, 0), (0, 1), (1, 0), (0, 2), (2, 0), (1, 1)], 96)]
    PARTS32 = [([(0, 0), (0, 1), (1, 0), (1, 1)], None), ([(0, 2), (2, 0)], 64)]

    def scratch(self, name, feats, tokens):
        return self.nc.dram_tensor("scratch_" + name, (3, feats, tokens), BF16).ap()

    def parts_out(self, mem, tag, shared=True, n=4):
        self.sent, self.shared = 0, shared
        return Ring([(self.sb(f"{tag}_t{i}", [P, BANK], F32, mem), self.sb(f"{tag}_p{i}", [P, 3, BANK], BF16, mem),
                      self.arrival(f"{tag}_w{i}")) for i in range(n)])

    def send_parts(self, ring, view, bias, t, dram, f, n):
        slot = ring.next()
        rest, parts, arr = slot.at
        if bias is None:
            t = self.A(lambda e: e.activation(parts[:, 0, :], view, ACT.Copy), t, slot.free)
            t_read = self.V(lambda e: e.tensor_tensor(rest[:, :], view, parts[:, 0, :], ALU.subtract), t)
        else:
            t = self.A(lambda e: e.activation(parts[:, 0, :], view, ACT.Identity, bias=bias), t, slot.free)
            t_read = self.V(lambda e: e.scalar_tensor_tensor(rest[:, :], view, bias, parts[:, 0, :], ALU.add, ALU.subtract), t)
        self.flush_parts()
        sent = []

        def second_half():
            t = self.A(lambda e: e.activation(parts[:, 1, :], rest[:, :], ACT.Copy), t_read)
            lane = self.G if self.shared and self.sent % 2 else self.V
            self.sent += 1
            t = lane(lambda e: e.tensor_tensor(parts[:, 2, :], rest[:, :], parts[:, 1, :], ALU.subtract), t)
            t = arr.dma(self.sp, dram[:, f * P:(f + 1) * P, n * BANK:(n + 1) * BANK].rearrange("s p t -> p s t"), parts[:, :, :], t)
            slot.free = [t]
            sent.append(t)
        self.unsent = second_half
        return sent, t_read

    def flush_parts(self):
        if self.unsent:
            half, self.unsent = self.unsent, None
            half()

    def project_parts(self, ring, w, fs, rhs, t_w, t_in, bias, dram, tokens, feats):
        done = {}
        for n in range(tokens // BANK):
            for m in range(feats // P):
                bank = self.banks.next()
                t = self.chain(self.ps[:, bank.at, :], [(w[:, f, m * P:(m + 1) * P], rhs(f, n)) for f in range(fs)],
                               bank.free, t_w, t_in)
                done[m, n], t_read = self.send_parts(ring, self.ps[:, bank.at, :], None if bias is None else bias[:, m:m + 1], t, dram, m, n)
                bank.free = [t_read]
        return done

    def attend(self, tag, jobs, d, scale, mem, kmax, softmax=True, nbuf=3):
        ps, pe = self.ps, self.pe
        spec = self.PARTS16 if d == 16 else self.PARTS32
        sets = []
        for i in range(nbuf):
            qs = [self.sb(f"{tag}_qs{i}{u}", [P, 4, S], BF16, mem) for u in range(len(spec))]
            ks = [self.sb(f"{tag}_ks{i}{u}", [P, 4, kmax], BF16, mem) for u in range(len(spec))]
            nm = self.sb(f"{tag}_nm{i}", [P, 4, 4], F32, mem)
            nt = self.sb(f"{tag}_nt{i}", [P, 4, 4], F32, mem)
            np_ = self.sb(f"{tag}_np{i}", [P, 4, 4, 3], BF16, mem)
            nmT = self.sb(f"{tag}_nmT{i}", [12, S], BF16, mem)
            st = dict(qs=qs, ks=ks, nm=nm, nt=nt, np=np_, nmT=nmT, arr=self.arrival(f"{tag}_l{i}"), arm=self.arrival(f"{tag}_m{i}"),
                      free=[], t_one=None)
            if softmax:
                for u, (pairs, row) in enumerate(spec):
                    if row is not None:
                        st["t_one"] = self.G(lambda e, k=ks[u], row=row: e.memset(k[row:row + 3, :, :], 1.0))
            sets.append(st)
        def settle(job, t_end):
            r = raws.next()
            acc = job["acc"]
            t_raw = self.A(lambda e: e.activation(r.at[:, :], ps[:, acc.at, :], ACT.Copy), t_end, r.free)
            acc.free = [t_raw]
            if not softmax:
                r.free = [job["done"](job, r.at, t_raw, None, None)]
                return
            dn, t_dn = r, t_raw
            if d == 32:
                dn = dens.next()
                t_dn = self.V(lambda e: e.tensor_copy(dn.at[:, :], ps[:, 7, :]), t_end, dn.free)
                acc.free = [t_raw, t_dn]
            yield
            pr = pairs_ring.next()
            for i in range(SC):
                t = self.chain(ps[:, pr.at, 4 * i:4 * i + 4], [(dn.at[:, i * P:(i + 1) * P], pick[:, :])], t_dn, t_pick, pr.free, tick=i == SC - 1)
            rc = rec.next()
            small, wide = rc.at
            t_rc = self.V(lambda e: e.reciprocal(small[:, :], ps[:, pr.at, 0:4 * SC]), t, rc.free)
            pr.free = [t_rc]
            t_rc = self.V(lambda e: e.tensor_copy(wide[:, :, :], small[:, :].unsqueeze(2).broadcast_to([P, 4 * SC, 32])), t_rc)
            if dn is not r:
                dn.free = [t]
            yield
            pb = pairs_ring.next()
            for i in range(SC):
                t = self.chain(ps[:, pb.at, i * P:(i + 1) * P],
                               [(wide[:, 4 * i:4 * i + 4, :].rearrange("p h r -> p (h r)"), self.ident[:, :])], t_rc, pb.free, tick=i == SC - 1)
            rc.free = [t]
            t = job["done"](job, r.at, t_raw, ps[:, pb.at, :], [t, t_raw])
            pb.free, r.free = [t], [t]

        def load(n):
            job, st = jobs[n], sets[n % nbuf]
            arr = st["arr"]
            self.sp.wait(st["free"], job["ready"])
            if n == 0:
                self.pool.wait(job["ready"])
            for u, (pairs, row) in enumerate(spec):
                for i, (qp, kp) in enumerate(pairs):
                    for (dram, first), part, tile, width in ((job["q"], qp, st["qs"][u], S), (job["k"], kp, st["ks"][u], job["keys"])):
                        src = dram[part, job["rows"]:job["rows"] + 4 * d, first:first + width].rearrange("(h i) t -> i h t", h=4)
                        if n == 0 and tile is st["ks"][u]:
                            t_keys = first_keys.dma(self.pool, tile[i * d:(i + 1) * d, :, 0:width], src)
                        else:
                            t = arr.dma(self.sp, tile[i * d:(i + 1) * d, :, 0:width], src)
            st["loaded"] = [t, t_keys] if n == 0 else t

        def pass1(n):
            job, st = jobs[n], sets[n % nbuf]
            pairs = spec[0][0]
            K = len(pairs) * d
            q, k = st["qs"][0], st["ks"][0]
            t_r = None
            for i in range(SC):
                if job["mode"] == "causal":
                    for jj in range(2):
                        pr = pairs_ring.next()
                        N = (i + 1) * P
                        for j in range(2):
                            h = 2 * jj + j
                            pe.do(lambda e, h=h, b=pr.at + j, i=i, N=N: e.matmul(
                                ps[:, b, 0:N], q[0:K, h, i * P:(i + 1) * P], k[0:K, h, 0:N], start=True, stop=False),
                                pr.free, st["loaded"], tick=False)
                            t = pe.do(lambda e, b=pr.at + j, i=i, N=N: e.matmul(
                                ps[:, b, N - P:N], self.identb[:, :], self.mask_qk[:, :], start=False, stop=True),
                                self.t_const, tick=j == 1)
                        t_r = self.V(lambda e, b=pr.at, i=i, jj=jj, N=N: e.tensor_reduce(
                            st["nm"][:, i, 2 * jj:2 * jj + 2], ps[:, b:b + 2, 0:N], AX.X, ALU.max, negate=True), t, st.get("nm_free"))
                        pr.free = [t_r]
                        yield
                elif job["keys"] == S:
                    for jj in range(2):
                        pr = pairs_ring.next()
                        for j in range(2):
                            t = pe.do(lambda e, h=2 * jj + j, b=pr.at + j, i=i: e.matmul(
                                ps[:, b, :], q[0:K, h, i * P:(i + 1) * P], k[0:K, h, 0:S], start=True, stop=True),
                                pr.free, st["loaded"], tick=j == 1)
                        t_r = self.V(lambda e, b=pr.at, i=i, jj=jj: e.tensor_reduce(
                            st["nm"][:, i, 2 * jj:2 * jj + 2], ps[:, b:b + 2, :], AX.X, ALU.max, negate=True), t, st.get("nm_free"))
                        pr.free = [t_r]
                        yield
                else:
                    for h in range(4):
                        pr = pairs_ring.next()
                        for j in range(2):
                            t = pe.do(lambda e, h=h, j=j, b=pr.at + j, i=i: e.matmul(
                                ps[:, b, :], q[0:K, h, i * P:(i + 1) * P], k[0:K, h, j * S:(j + 1) * S], start=True, stop=True),
                                pr.free, st["loaded"], tick=j == 1)
                        t_r = self.V(lambda e, b=pr.at, i=i, h=h: e.tensor_reduce(
                            st["nm"][:, i, h:h + 1], ps[:, b:b + 2, :], AX.XY, ALU.max, negate=True), t, st.get("nm_free"))
                        pr.free = [t_r]
                        yield
            nm, nt, np_, nmT = st["nm"], st["nt"], st["np"], st["nmT"]
            t = self.V(lambda e: e.tensor_copy(np_[:, :, :, 0], nm[:, :, :]), t_r, st.get("np_free"))
            t = self.V(lambda e: e.tensor_tensor(nt[:, :, :], nm[:, :, :], np_[:, :, :, 0], ALU.subtract), t)
            t = self.V(lambda e: e.tensor_copy(np_[:, :, :, 1], nt[:, :, :]), t)
            t = self.V(lambda e: e.tensor_tensor(np_[:, :, :, 2], nt[:, :, :], np_[:, :, :, 1], ALU.subtract), t)
            st["nm_free"] = t
            yield
            pr = pairs_ring.next()
            view = ps[0:12, pr.at, 0:S // 2].bitcast(BF16)
            for i in range(SC):
                t2 = pe.do(lambda e, i=i: e.transpose(view[:, i * P:(i + 1) * P], np_[:, i, :, :].rearrange("p h s -> p (h s)"),
                                                     self.identb[:, :]), t, pr.free, self.t_const, tick=i == SC - 1)
            st["np_free"] = t2
            t = self.V(lambda e: e.tensor_copy(nmT[:, :], view), t2, st.get("nmT_free"))
            pr.free = [t]
            u = len(spec) - 1
            row = spec[u][1]
            for h in range(4):
                t3 = st["arm"].dma(self.sp, st["qs"][u][row:row + 3, h, :], nmT[3 * h:3 * h + 3, :], t)
            st["maxed"] = st["nmT_free"] = t3
            yield

        def pass2(n):
            job, st = jobs[n], sets[n % nbuf]
            acc = job["acc"] = accs.next()
            chunks = job["keys"] // P
            order = list(range(chunks))[::-1] if job["mode"] == "upper" else list(range(chunks))
            late = []

            def values(c, jj, w, wd, t, t_wd, last):
                start = c == order[0]
                lo, hi = (c * P, S) if job["mode"] == "causal" else (0, c * P) if job["mode"] == "upper" else (0, S)
                heads = [(j, 2 * jj + j) for j in range(2)]
                if hi > lo:
                    for j, h in heads:
                        t1 = pe.do(lambda e, j=j, h=h: e.matmul(
                            ps[32 * h:32 * h + 32, acc.at, lo:hi], job["v"](c, h), w.at[:, j, lo:hi], start=start,
                            stop=last and wd is None), t, acc.free, job["v_ready"], tick=j == 1)
                if softmax and d == 32:
                    for j, h in heads:
                        o = 32 * ((h + 2) % 4)
                        t1 = pe.do(lambda e, j=j, o=o: e.matmul(
                            ps[o:o + 32, 7, :], self.ones[:, 0:32], w.at[:, j, :], start=start, stop=last), t, acc.free, tick=j == 1)
                w.free = [t1]
                if wd is not None:
                    for j, h in heads:
                        t1 = pe.do(lambda e, j=j, h=h: e.matmul(
                            ps[32 * h:32 * h + 32, acc.at, c * P:(c + 1) * P], job["v"](c, h), wd.at[:, j, :], start=False, stop=last),
                            t_wd, job["v_ready"], tick=j == 1)
                    wd.free = [t1]
                return t1

            for c in order:
                lo = c * P if job["mode"] == "causal" else 0
                for jj in range(2):
                    pr = pairs_ring.next()
                    for j in range(2):
                        h = 2 * jj + j
                        out = ps[:, pr.at + j, lo:S]
                        pe.wait(pr.free, st["loaded"], st["maxed"] if softmax else None, st["t_one"])
                        for u, (pairs, row) in enumerate(spec):
                            K = len(pairs) * d + (3 if softmax and row is not None else 0)
                            end = u == len(spec) - 1 and job["mode"] != "causal" or (u == len(spec) - 1 and not softmax)
                            t = pe.do(lambda e, u=u, K=K, h=h, c=c, out=out, lo=lo, end=end: e.matmul(
                                out, st["ks"][u][0:K, h, c * P:(c + 1) * P], st["qs"][u][0:K, h, lo:S], start=u == 0, stop=end),
                                tick=end and j == 1)
                        if job["mode"] == "causal" and softmax:
                            t = pe.do(lambda e, b=pr.at + j, lo=lo: e.matmul(
                                ps[:, b, lo:lo + P], self.identb[:, :], self.mask_kq[:, :], start=False, stop=True), tick=j == 1)
                    w = wts.next()
                    if softmax:
                        t = self.A(lambda e, w=w, b=pr.at, lo=lo: e.activation(w.at[:, :, lo:S], ps[:, b:b + 2, lo:S], ACT.Exp, scale=scale),
                                   t, w.free)
                    else:
                        t = self.V(lambda e, w=w, b=pr.at, lo=lo, jj=jj: e.tensor_tensor(
                            w.at[:, :, lo:S], ps[:, b:b + 2, lo:S], job["decay"](jj, S - lo), ALU.mult), t, w.free, job["decay_ready"])
                    pr.free = [t]
                    wd, t_wd = None, None
                    if job["mode"] == "upper":
                        wd = wds.next()
                        t_wd = self.G(lambda e, wd=wd, w=w, c=c: e.affine_select(
                            out=wd.at[:, :, :], in_=w.at[:, :, c * P:(c + 1) * P], compare_op=ALU.is_gt, fill=0.0, base=0,
                            pattern=[[0, 2], [-1, P]], channel_multiplier=1), t, wd.free)
                    late.append((c, jj, w, wd, t, t_wd, c == order[-1]))
                    if len(late) > (1 if d == 32 else 2):
                        for _ in range(1 if d == 32 else 2):
                            values(*late.pop(0))
                    yield
            while late:
                t_end = values(*late.pop(0))
            st["free"] = [t_end]
            job["end"] = t_end

        first_keys = self.arrival(f"{tag}_lk")
        yield
        for n in range(min(nbuf - 1, len(jobs))):
            load(n)
        yield
        pairs_ring = Ring([0, 2, 4])
        for i, s in enumerate(pairs_ring.slots):
            s.free = self.banks.slots[2 * i].free + self.banks.slots[2 * i + 1].free
        accs = Ring([6, 7] if d == 16 else [6])
        for s in accs.slots:
            s.free = self.banks.slots[6].free + self.banks.slots[7].free
        items = lambda m: (2 * SC if jobs[m]["keys"] == S else 4 * SC) + 2
        maxima, given = {}, {}

        lead = 0.6 if d == 16 else 0.35

        def give(m, share):
            if not softmax or m >= len(jobs):
                return
            if m not in maxima:
                maxima[m], given[m] = pass1(m), 0
            while given[m] < items(m) and given[m] < items(m) * share:
                next(maxima[m], None)
                given[m] += 1

        give(0, 1)
        if nbuf > 2:
            give(1, lead)
        yield
        wts = Ring([self.sb(f"{tag}_w{i}", [P, 2, S], F32, mem) for i in range(4 if d == 32 else 5)])
        if jobs[0]["mode"] == "upper":
            wds = Ring([self.sb(f"{tag}_wd{i}", [P, 2, P], F32, mem) for i in range(3)])
        raws = Ring([self.sb(f"{tag}_raw{i}", [P, S], F32, mem) for i in range(2)])
        if softmax:
            off, turn = (16, 0) if d == 16 else (0, 2)
            pick = self.sb(f"{tag}_pick", [P, 4], F32, mem)
            t = self.G(lambda e: e.memset(pick[:, :], 0.0))
            t_pick = self.G(lambda e: e.affine_select(out=pick[:, 0:4 - turn], in_=pick[:, 0:4 - turn], compare_op=ALU.not_equal, fill=1.0,
                                                      base=-off - 32 * turn, pattern=[[-32, 4 - turn]], channel_multiplier=1), t)
            if turn:
                t_pick = self.G(lambda e: e.affine_select(out=pick[:, turn:4], in_=pick[:, turn:4], compare_op=ALU.not_equal, fill=1.0,
                                                          base=-off, pattern=[[-32, turn]], channel_multiplier=1), t_pick)
            rec = Ring([(self.sb(f"{tag}_rec{i}", [P, SC * 4], F32, mem), self.sb(f"{tag}_rex{i}", [P, SC * 4, 32], F32, mem)) for i in range(2)])
            dens = raws if d == 16 else Ring([self.sb(f"{tag}_den{i}", [P, S], F32, mem) for i in range(2)])

        settling = iter(())
        for n, job in enumerate(jobs):
            if n + nbuf - 1 < len(jobs):
                load(n + nbuf - 1)
            steps = 2 * job["keys"] // P
            for k, _ in enumerate(pass2(n)):
                if k >= 1:
                    next(settling, None)
                now = (k + 1) / steps
                if nbuf > 2:
                    give(n + 1, now + lead)
                    give(n + 2, now - (1 - lead))
                else:
                    give(n + 1, (k + 1 - 3) / (0.72 * steps - 3))
            for _ in settling:
                pass
            give(n + 1, 1)
            settling = settle(job, job["end"])
            next(settling, None)
        for _ in settling:
            pass
        for i, s in enumerate(pairs_ring.slots):
            self.banks.slots[2 * i].free = list(s.free)
            self.banks.slots[2 * i + 1].free = list(s.free)
        for i in (6, 7):
            self.banks.slots[i].free = [t for s in accs.slots for t in s.free]

    def context(self, mem):
        ctx = self.sb("ctx", [P, MC, CW], F32, mem)
        arr = self.arrival("ctx")

        def turn():
            self.ctxT_ready = self.to_features(ctx, CW, MC, [(arr.sem, arr.count)] * MC, lambda f, n, view, t: self.copy(
                self.act if n % 2 else self.dve, self.ctxT[:, n * BANK:(n + 1) * BANK], view, t))
        return (lambda: arr.dma(self.sp, ctx[:, :, :], self.a["ctx_512"].rearrange("b (c p) d -> p (b c) d", p=P))), turn

    def cross_attention_weights(self, mem):
        W, tW = {}, {}
        self.xa_weights = W, tW
        for n, rows in (("Wq", FC), ("Wk", FC), ("Wcq", FC), ("Wck", 1), ("Wv", FC), ("Wcv", 1)):
            W[n] = self.sb("xa_" + n, [P, rows, D], F32, mem)

        def load():
            for n, w in W.items():
                tW[n] = self.arrival("xa" + n).dma(self.sp, w[:, :, :], self.a["L0_xattn_" + n].rearrange("(f p) n -> p f n", p=P))
        return load

    def cross_attention(self):
        a, ps = self.a, self.ps
        W, tW = self.xa_weights
        with ExitStack() as mem:
            sb = lambda n, s, dt=F32: self.sb("xa_" + n, s, dt, mem)
            bcol, t_bc = self.col, self.t_col
            brow = sb("brow", [P, 3, D])
            abr = self.arrival("xabr")
            for i, n in enumerate(("bv", "bcv", "bp")):
                t_br = abr.dma(self.sp, brow[:, i, :], a["L0_xattn_" + n].partition_broadcast(P))
            dh = D // H
            wp = sb("wp", [P, 4, D])
            t_wz = self.G(lambda e: e.memset(wp[:, :, :], 0.0))
            awp = self.arrival("xawp")
            for h in range(4):
                t_wp = awp.dma(self.sp, wp[32 * h:32 * h + dh, :, :], a["L0_xattn_Wp"].rearrange("(g h i) n -> h i g n", g=4, h=4)[h], t_wz)
            v = sb("v", [P, NC, H, 32])
            vc = sb("vc", [P, MC, H, 32])
            t_vo = self.G(lambda e: e.memset(v[:, :, :, :], 1.0))
            t_vco = self.G(lambda e: e.memset(vc[:, :, :, :], 1.0))
            self.norm_x()
            dq, dk, dcq, dck = (self.scratch("xa" + n, D, w) for n, w in (("q", T), ("k", T), ("cq", T), ("ck", TM)))
            jobs = []
            attention = self.attend("xa", jobs, dh, dh ** -0.5, mem, MEM)
            next(attention)
            with ExitStack() as tmp:
                ring = self.parts_out(tmp, "xap", n=6)
                xT = lambda f, n: self.xnT[:, f, n * BANK:(n + 1) * BANK]
                cT = lambda f, n: self.ctxT[:, n * BANK:(n + 1) * BANK]
                r_q = self.project_parts(ring, W["Wq"], FC, xT, [tW["Wq"], t_bc], self.xnT_ready, bcol["L0_xattn_bq"], dq, T, D)
                r_k = self.project_parts(ring, W["Wk"], FC, xT, tW["Wk"], self.xnT_ready, bcol["L0_xattn_bk"], dk, T, D)
                t_v, t_vc = [], []
                t_self = {}
                t_y = []

                def done(job, raw, t_raw, rden, t_rden):
                    b, g = job["b"], job["g"]
                    y = yT[:, g, b * S:(b + 1) * S]
                    if not job["cross"]:
                        t_self[b, g] = self.V(lambda e: e.tensor_tensor(y, raw[:, :], rden, ALU.mult), t_rden)
                        return t_self[b, g]
                    q = yc.next()
                    t2 = self.V(lambda e: e.tensor_tensor(q.at[:, :], raw[:, :], rden, ALU.mult), t_rden, q.free)
                    t3 = self.G(lambda e: e.tensor_tensor(y, y, q.at[:, :], ALU.add), t2, t_self[b, g])
                    q.free = [t3]
                    t_y.append(t3)
                    return t2

                def jobs_of(cross):
                    out = []
                    for b in range(B):
                        for g in range(4):
                            rows = g * 4 * dh
                            m = rows // P
                            kn = [b] if not cross else [2 * b, 2 * b + 1]
                            out.append(dict(q=((dcq if cross else dq), b * S), k=((dck, b * MEM) if cross else (dk, b * S)), rows=rows,
                                            keys=MEM if cross else S, mode="full" if cross else "causal", b=b, g=g, cross=cross,
                                            v=(lambda c, h, b=b, g=g: vc[:, b * MC // B + c, 4 * g + h, :]) if cross else
                                              (lambda c, h, b=b, g=g: v[:, b * SC + c, 4 * g + h, :]),
                                            v_ready=t_vc if cross else t_v,
                                            ready=[(r_cq if cross else r_q)[m, b]] + [(r_ck if cross else r_k)[m, n] for n in kn],
                                            done=done))
                    return out
                r_cq = self.project_parts(ring, W["Wcq"], FC, xT, tW["Wcq"], self.xnT_ready, bcol["L0_xattn_bcq"], dcq, T, D)
                r_ck = self.project_parts(ring, W["Wck"], 1, cT, tW["Wck"], self.ctxT_ready, bcol["L0_xattn_bck"], dck, TM, D)
                self.flush_parts()
                jobs += jobs_of(False) + jobs_of(True)
                next(attention)
                for c in range(NC):
                    bank = self.banks.next()
                    t = self.chain(ps[:, bank.at, 0:D], [(self.xnT[:, f, c * P:(c + 1) * P], W["Wv"][:, f, :]) for f in range(FC)],
                                   bank.free, tW["Wv"])
                    t = self.V(lambda e, c=c, b=bank.at: e.tensor_tensor(
                        v[:, c, :, 0:dh], ps[:, b, 0:D].rearrange("p (h i) -> p h i", h=H), brow[:, 0, :].rearrange("p (h i) -> p h i", h=H),
                        ALU.add), t, t_br, t_vo)
                    bank.free = [t]
                    t_v.append(t)
                for c in range(MC):
                    bank = self.banks.next()
                    t = self.chain(ps[:, bank.at, 0:D], [(self.ctxT[:, c * P:(c + 1) * P], W["Wcv"][:, 0, :])], bank.free, tW["Wcv"])
                    t = self.V(lambda e, c=c, b=bank.at: e.tensor_tensor(
                        vc[:, c, :, 0:dh], ps[:, b, 0:D].rearrange("p (h i) -> p h i", h=H), brow[:, 1, :].rearrange("p (h i) -> p h i", h=H),
                        ALU.add), t, t_br, t_vco)
                    bank.free = [t]
                    t_vc.append(t)
                t_xb = None
                for c in range(NC):
                    t_xb = self.G(lambda e, c=c: e.tensor_tensor(self.x[:, c, :], self.x[:, c, :], brow[:, 2, :], ALU.add),
                                  self.xn_ready, t_br)
                next(attention)
                self.fence(*[s.free for s in ring.slots])
            yT = sb("yT", [P, 4, T])
            yc = Ring([sb(f"yc{i}", [P, S]) for i in range(2)])
            for _ in attention:
                pass
            final = self.new_x(alike=True)
            for c in range(NC):
                bank = self.banks.next()
                t = self.chain(ps[:, bank.at, 0:D], [(yT[:, g, c * P:(c + 1) * P], wp[:, g, :]) for g in range(4)], bank.free, t_y, t_wp)
                t = self.V(lambda e, c=c, b=bank.at: e.tensor_tensor(self.x[:, c, :], self.x[:, c, :], ps[:, b, 0:D], ALU.add), t, t_xb)
                bank.free = [t]
                final(c, t)
            self.fence()

    def route(self, mem, tag, w, n_exp, bias_row, t_w):
        ps = self.ps
        lg = self.sb(tag + "_lg", [P, NC, 8], F32, mem)
        st = self.sb(tag + "_st", [P, NC, 2], F32, mem)
        top = self.sb(tag + "_top", [P, NC, 8], F32, mem)
        idx = self.sb(tag + "_idx", [P, NC, 8], U32, mem)
        who = self.sb(tag + "_who", [P, NC, 2], F32, mem)
        t_pad = self.V(lambda e: e.memset(lg[:, :, :], -1.0))
        bank = self.banks.next()
        for c in range(NC):
            t = self.chain(ps[:, bank.at, 8 * c:8 * c + n_exp], [(self.xnT[:, f, c * P:(c + 1) * P], w[:, f, :]) for f in range(FC)],
                           bank.free, self.xnT_ready, t_w, tick=c == NC - 1)
        live = lg[:, :, 0:n_exp]
        view = ps[:, bank.at, 0:8 * NC].rearrange("p (c e) -> p c e", e=8)[:, :, 0:n_exp]
        if bias_row is not None:
            t = self.V(lambda e: e.tensor_tensor(live, view, bias_row.unsqueeze(1).broadcast_to([P, NC, n_exp]), ALU.add), t, t_w, t_pad)
        else:
            t = self.V(lambda e: e.tensor_copy(live, view), t, t_pad)
        bank.free = [t]
        t = self.V(lambda e: e.tensor_reduce(st[:, :, 0], live, AX.X, ALU.max), t)
        bc = lambda i: st[:, :, i].unsqueeze(2).broadcast_to([P, NC, n_exp])
        t = self.V(lambda e: e.tensor_tensor(live, live, bc(0), ALU.subtract), t)
        t = self.A(lambda e: e.activation(live, live, ACT.Exp), t)
        t = self.V(lambda e: e.tensor_reduce(st[:, :, 0], live, AX.X, ALU.add), t)
        t = self.V(lambda e: e.reciprocal(st[:, :, 1], st[:, :, 0]), t)
        t = self.V(lambda e: e.tensor_tensor(live, live, bc(1), ALU.mult), t)
        for c in range(NC):
            t1 = self.V(lambda e, c=c: e.max(top[:, c, :], lg[:, c, :]), t if c == 0 else None)
        for c in range(NC):
            t = self.V(lambda e, c=c: e.max_index(idx[:, c, :], top[:, c, :], lg[:, c, :]), t1 if c == 0 else None)
        t = self.V(lambda e: e.tensor_copy(who[:, :, :], idx[:, :, 0:2]), t)
        return top, who, t

    def moe(self, load_next_weights, turn_next_weights):
        a, ps = self.a, self.ps
        SLOTS = E0 * CAP
        NR = -(-SLOTS // P)
        with ExitStack() as mem:
            sb = lambda n, s, dt=F32: self.sb("mo_" + n, s, dt, mem)
            wr, t_wr = self.wr["L0_ffn_Wr"]
            br = sb("br", [P, E0])
            t_br = self.arrival("mobr").dma(self.sp, br[:, :], a["L0_ffn_br"].partition_broadcast(P))
            b1, t_b1 = self.col["L0_ffn_b1"], self.t_col
            b2 = sb("b2", [1, E0 * D])
            t_b2 = self.arrival("mob2").dma(self.sp, b2[:, :], a["L0_ffn_b2"].rearrange("e d -> (e d)").unsqueeze(0))
            wring = Ring([(sb(f"w1_{i}", [P, FC, HID]), sb(f"w2_{i}", [P, HC, D]), self.arrival(f"mow{i}")) for i in range(3)])
            zero = sb("zero", [P, D])
            t_zero = self.G(lambda e: e.memset(zero[:, :], 0.0))
            xg = self.nc.dram_tensor("scratch_xg", (SLOTS + 2 * T, D), F32).ap()
            yo = self.nc.dram_tensor("scratch_yo", (SLOTS + 1, D), F32).ap()
            zrows = SLOTS // E0 // 2
            az = self.arrival("moz")
            az.dma(self.sp, xg[0:SLOTS, :].rearrange("(p k) d -> p k d", p=zrows), zero[0:zrows, :].unsqueeze(1).broadcast_to([zrows, SLOTS // zrows, D]), t_zero)
            t_z = az.dma(self.sp, yo[SLOTS:SLOTS + 1, :], zero[0:1, :], t_zero)
            weights = {}

            context_operands = self.context_operands(mem)

            def load(e):
                slot = wring.next()
                w1, w2, arr = slot.at
                arr.dma(self.sp, w1[:, :, :], a["L0_ffn_W1"][e].rearrange("(f p) n -> p f n", p=P), slot.free)
                t = arr.dma(self.sp, w2[:, :, :], a["L0_ffn_W2"][e].rearrange("(f p) n -> p f n", p=P))
                weights[e] = (slot, w1, w2, t)
            for e in range(3):
                load(e)
            load_next_weights()
            self.norm_x()
            top, who, t_top = self.route(mem, "mor", wr, E0, br[:, :], [t_wr, t_br])
            next(context_operands)
            iota_e = sb("iota_e", [P, E0])
            t_i = self.G(lambda e: e.iota(iota_e[:, :], pattern=[[1, E0]], base=0, channel_multiplier=0, allow_small_or_imprecise_dtypes=True))
            dump = sb("dump", [P, 2, NC])
            t_i = self.G(lambda e: e.iota(dump[:, :, :], pattern=[[T, 2], [P, NC]], base=SLOTS, channel_multiplier=1, allow_small_or_imprecise_dtypes=True))
            before = sb("before", [P, P])
            t_b = self.G(lambda e: e.memset(before[:, :], 1.0))
            t_b = self.G(lambda e: e.affine_select(out=before[:, :], in_=before[:, :], compare_op=ALU.is_gt, fill=0.0, base=0,
                                                   pattern=[[1, P]], channel_multiplier=-1), t_b)
            chosen = sb("chosen", [P, 2, NC, E0])
            G = sb("G", [P, NC, E0])
            G2 = sb("G2", [P, NC, E0])
            ib = iota_e[:, :].unsqueeze(1).broadcast_to([P, NC, E0])
            for k in range(2):
                t = self.V(lambda e, k=k: e.tensor_tensor(chosen[:, k, :, :], ib, who[:, :, k:k + 1].broadcast_to([P, NC, E0]), ALU.is_equal), t_top, t_i)
            t = self.V(lambda e: e.tensor_tensor(G[:, :, :], chosen[:, 0, :, :], top[:, :, 0:1].broadcast_to([P, NC, E0]), ALU.mult), t)
            t = self.V(lambda e: e.tensor_tensor(G2[:, :, :], chosen[:, 1, :, :], top[:, :, 1:2].broadcast_to([P, NC, E0]), ALU.mult), t)
            t = self.V(lambda e: e.tensor_tensor(G[:, :, :], G[:, :, :], G2[:, :, :], ALU.add), t)
            t = self.V(lambda e: e.tensor_tensor(G2[:, :, :], chosen[:, 0, :, :], chosen[:, 1, :, :], ALU.add), t)
            t_G = self.V(lambda e: e.scalar_tensor_tensor(G[:, :, :], G2[:, :, :], -1.0, G[:, :, :], ALU.add, ALU.add), t)
            K = 7
            digit = sb("digit", [P, K], I32)
            t_i = self.G(lambda e: e.iota(digit[:, :], pattern=[[1, K]], base=1, channel_multiplier=0), t_i)
            level = sb("level", [P, E0], I32)
            cand = sb("cand", [P, K, E0], I32)
            step = sb("step", [P, K], I32)
            hit = sb("hit", [P, K, E0, NC])
            many = sb("many", [P, K, E0])
            found = sb("found", [P, E0])
            found_i = sb("found_i", [P, E0], I32)
            t = self.V(lambda e: e.memset(level[:, :], 0))
            for shift in range(27, -1, -3):
                t1 = self.V(lambda e, shift=shift: e.tensor_scalar(step[:, :], digit[:, :], shift, None, ALU.logical_shift_left), t, t_i)
                t = self.V(lambda e: e.tensor_tensor(cand[:, :, :], level[:, :].unsqueeze(1).broadcast_to([P, K, E0]),
                                                     step[:, :].unsqueeze(2).broadcast_to([P, K, E0]), ALU.bitwise_or), t1)
                t = self.V(lambda e: e.tensor_tensor(hit[:, :, :, :], G[:, :, :].rearrange("p c e -> p e c").unsqueeze(1).broadcast_to([P, K, E0, NC]),
                                                     cand[:, :, :].bitcast(F32).unsqueeze(3).broadcast_to([P, K, E0, NC]), ALU.is_ge), t, t_G)
                t = self.V(lambda e: e.tensor_reduce(many[:, :, :], hit[:, :, :, :], AX.X, ALU.add), t)
                if 3 <= shift <= 24:
                    next(context_operands)
                bank = self.banks.next()
                t = self.chain(ps[:, bank.at, 0:K * E0], [(self.ones[:, :], many[:, :, :].rearrange("p k e -> p (k e)"))], t, bank.free, self.t_ones)
                t = self.V(lambda e, b=bank.at: e.tensor_scalar(many[:, :, :].rearrange("p k e -> p (k e)"), ps[:, b, 0:K * E0], float(CAP), None, ALU.is_ge), t)
                bank.free = [t]
                t = self.V(lambda e: e.tensor_reduce(found[:, :], many[:, :, :].rearrange("p k e -> p e k"), AX.X, ALU.add), t)
                t = self.V(lambda e: e.tensor_copy(found_i[:, :], found[:, :]), t)
                t = self.V(lambda e, shift=shift: e.tensor_scalar(found_i[:, :], found_i[:, :], shift, None, ALU.logical_shift_left), t)
                t = self.V(lambda e: e.tensor_tensor(level[:, :], level[:, :], found_i[:, :], ALU.bitwise_or), t)
            kind = sb("kind", [P, NC, 2, E0])
            lv = level[:, :].bitcast(F32).unsqueeze(1).broadcast_to([P, NC, E0])
            t = self.V(lambda e: e.tensor_tensor(kind[:, :, 0, :], G[:, :, :], lv, ALU.is_gt), t)
            t = self.V(lambda e: e.tensor_tensor(kind[:, :, 1, :], G[:, :, :], lv, ALU.is_equal), t)
            bank = self.banks.next()
            flat = kind[:, :, :, :].rearrange("p c k e -> p (c k e)")
            W = 2 * E0
            self.pe.wait(bank.free, t, t_b)
            for back in range(NC):
                t = self.pe.do(lambda e, back=back, b=bank.at: e.matmul(
                    ps[:, b, back * W:NC * W], (self.ones if back else before)[:, :], flat[:, 0:(NC - back) * W],
                    start=back == 0, stop=back == NC - 1), tick=back == NC - 1)
            t = self.chain(ps[:, bank.at, NC * W:NC * W + E0], [(self.ones[:, :], kind[:, c, 0, :]) for c in range(NC)])
            place = sb("place", [P, NC, 2, E0])
            above = sb("above", [P, E0])
            t1 = self.V(lambda e, b=bank.at: e.tensor_scalar(place[:, :, :, :].rearrange("p c k e -> p (c k e)"), ps[:, b, 0:NC * W],
                                                             -float(CAP), None, ALU.add), t)
            t = self.V(lambda e, b=bank.at: e.tensor_copy(above[:, :], ps[:, b, NC * W:NC * W + E0]), t)
            bank.free = [t]
            t = self.V(lambda e: e.tensor_tensor(place[:, :, 1, :], place[:, :, 1, :], above[:, :].unsqueeze(1).broadcast_to([P, NC, E0]), ALU.add), t, t1)
            t = self.V(lambda e: e.tensor_tensor(place[:, :, :, :], place[:, :, :, :], kind[:, :, :, :], ALU.mult), t)
            rank = sb("rank", [P, NC, E0])
            t_rank = self.V(lambda e: e.scalar_tensor_tensor(rank[:, :, :], place[:, :, 0, :], float(CAP), place[:, :, 1, :], ALU.add, ALU.add), t)
            slot = sb("slot", [P, 2, NC])
            rk = sb("rk", [P, 2, NC])
            ok = sb("ok", [P, 2, NC])
            to = sb("to", [P, 2, NC], U32)
            fro = sb("fro", [P, 2, NC], U32)
            for k in range(2):
                t = self.V(lambda e, k=k: e.tensor_tensor(chosen[:, k, :, :], chosen[:, k, :, :], rank[:, :, :], ALU.mult), t_rank)
                t = self.V(lambda e, k=k: e.tensor_reduce(rk[:, k, :], chosen[:, k, :, :], AX.X, ALU.add), t)
                t = self.V(lambda e, k=k: e.scalar_tensor_tensor(slot[:, k, :], who[:, :, k], float(CAP), rk[:, k, :], ALU.mult, ALU.add), t)
                t = self.V(lambda e, k=k: e.tensor_scalar(ok[:, k, :], rk[:, k, :], float(CAP), None, ALU.is_lt), t)
            t = self.V(lambda e: e.tensor_tensor(rk[:, :, :], slot[:, :, :], dump[:, :, :], ALU.subtract), t)
            t = self.V(lambda e: e.tensor_tensor(rk[:, :, :], rk[:, :, :], ok[:, :, :], ALU.mult), t)
            t_to = self.V(lambda e: e.tensor_tensor(to[:, :, :], rk[:, :, :], dump[:, :, :], ALU.add), t)
            t = self.V(lambda e: e.scalar_tensor_tensor(rk[:, :, :], slot[:, :, :], -float(SLOTS), ok[:, :, :], ALU.add, ALU.mult), t_to)
            t_fro = self.V(lambda e: e.tensor_scalar(fro[:, :, :], rk[:, :, :], float(SLOTS), None, ALU.add), t)
            sc = self.arrival("mosc")
            self.pool.wait(t_to, t_z)
            for c in range(NC):
                for k in range(2):
                    sc.count += 16
                    self.pool.items.append(lambda e, c=c, k=k: e.indirect_dma_start(
                        xg, bass.IndirectOffsetOnAxis(ap=to[:, k, c:c + 1], axis=0), self.xn[:, c, :], None).then_inc(sc.sem, 16))
            t_sc = (sc.sem, sc.count)
            next(context_operands)
            turn_next_weights()
            xs = sb("xs", [P, NR, D])
            xgT = sb("xgT", [P, FC, NR * P])
            ax = self.arrival("moxg")
            full = SLOTS // P
            t = ax.dma(self.pool, xs[:, 0:full, :], xg[0:full * P, :].rearrange("(r p) d -> p r d", p=P), t_sc)
            rest = SLOTS - full * P
            if rest:
                t = ax.dma(self.pool, xs[0:rest, full, :], xg[full * P:SLOTS, :])
            t_g = []
            for f in range(FC):
                for r0 in range(0, NR, 4):
                    bank = self.banks.next()
                    rs = list(range(r0, min(NR, r0 + 4)))
                    for r in rs:
                        m = P if r < full else rest
                        t1 = self.pe.do(lambda e, r=r, m=m, b=bank.at, r0=r0, f=f: e.transpose(
                            ps[:, b, (r - r0) * P:(r - r0) * P + m], xs[0:m, r, f * P:(f + 1) * P], self.ident[0:m, 0:m]),
                            t, bank.free, tick=r == rs[-1])
                    n = (len(rs) - 1) * P + m
                    t1 = self.copy(self.act if f else self.dve, xgT[:, f, r0 * P:r0 * P + n], ps[:, bank.at, 0:n], t1)
                    bank.free = [t1]
                    t_g.append(t1)
            hT = Ring([sb(f"hT{i}", [P, HC, CAP]) for i in range(2)])
            os_ = Ring([(sb(f"o{i}", [P, 2, D]), self.arrival(f"moo{i}")) for i in range(2)])
            t_done = []
            for x in range(E0):
                wslot, w1, w2, t_w = weights[x]
                h = hT.next()
                t_h = []
                for m0 in range(0, HC, 2):
                    bank = self.banks.next()
                    for m in (m0, m0 + 1):
                        t = self.chain(ps[:, bank.at, (m - m0) * 256:(m - m0) * 256 + CAP],
                                       [(w1[:, f, m * P:(m + 1) * P], xgT[:, f, x * CAP:(x + 1) * CAP]) for f in range(FC)],
                                       bank.free, t_w, t_g, tick=m != m0)
                    for m in (m0, m0 + 1):
                        t1 = self.A(lambda e, m=m, m0=m0, b=bank.at, h=h, x=x: e.activation(
                            h.at[:, m, :], ps[:, b, (m - m0) * 256:(m - m0) * 256 + CAP], ACT.Silu,
                            bias=b1[:, x * HC + m:x * HC + m + 1]), t, h.free, t_b1)
                    bank.free = [t1]
                    t_h.append(t1)
                o = os_.next()
                ot, oarr = o.at
                for r, (lo, n) in enumerate(((0, P), (P, CAP - P))):
                    bank = self.banks.next()
                    t = self.chain(ps[0:n, bank.at, 0:D], [(h.at[:, m, lo:lo + n], w2[:, m, :]) for m in range(HC)] +
                                   [(self.ones[0:1, 0:n], b2[0:1, x * D:(x + 1) * D])], bank.free, t_h, t_b2, self.t_ones)
                    t1 = self.V(lambda e, n=n, r=r, b=bank.at, ot=ot: e.tensor_copy(ot[0:n, r, :], ps[0:n, b, 0:D]), t, o.free)
                    bank.free = [t1]
                    t2 = oarr.dma(self.sp, yo[x * CAP + lo:x * CAP + lo + n, :], ot[0:n, r, :], t1)
                h.free, wslot.free = [t], [t]
                o.free = [t2]
                t_done.append(t2)
                if x + 3 < E0:
                    load(x + 3)
            ga = [self.arrival(f"moga{i}") for i in range(8)]
            gb = Ring([(xs[:, i, :], ga[i]) for i in range(8)])
            self.pool.wait(t_done, t_fro)
            final = self.new_x()
            for c in range(NC):
                for k in range(2):
                    g = gb.next()
                    gt, arr = g.at
                    self.pool.wait(g.free)
                    arr.count += 16
                    self.pool.items.append(lambda e, c=c, k=k, gt=gt, arr=arr: e.indirect_dma_start(
                        gt[:, :], None, yo, bass.IndirectOffsetOnAxis(ap=fro[:, k, c:c + 1], axis=0)).then_inc(arr.sem, 16))
                    t = self.V(lambda e, c=c, k=k, gt=gt: e.scalar_tensor_tensor(
                        self.x[:, c, :], gt[:, :], top[:, c, k:k + 1], self.x[:, c, :], ALU.mult, ALU.add),
                        (arr.sem, arr.count), self.dve.last())
                    g.free = [t]
                final(c, t)
            self.fence()

    def retention_weights(self, mem):
        a, ps = self.a, self.ps
        dk = D // H
        sb = lambda n, s: self.sb("rew_" + n, s, F32, mem)
        wT, woT = sb("wT", [P, FC, 3 * D]), sb("woT", [P, 4, D])
        raw, rawo = sb("raw", [P, 3 * FC, D]), sb("rawo", [P, FC, H, 32])
        t_wT, t_wo, tickets = [], [], {}
        self.re_weights = wT, woT, t_wT, t_wo

        def load():
            tickets['qkv'] = self.arrival("rew").dma(self.sp, raw[:, :, :], a["L1_attn_W_qkv"].rearrange("(o p) i -> p o i", p=P))
            t_z = self.G(lambda e: e.memset(rawo[:, :, :, :], 0.0))
            aw = self.arrival("rewo")
            for f in range(FC):
                tickets['o'] = aw.dma(self.sp, rawo[:, f, :, 0:dk], a["L1_attn_W_o"][f * P:(f + 1) * P, :].rearrange("p (h i) -> p h i", h=H), t_z)

        def turn():
            for f in range(FC):
                for o0 in (0, 3):
                    bank = self.banks.next()
                    for o in range(3):
                        t = self.pe.do(lambda e, o=o, o0=o0, f=f, b=bank.at: e.transpose(
                            ps[:, b, o * P:(o + 1) * P], raw[:, o0 + o, f * P:(f + 1) * P], self.ident[:, :]), tickets['qkv'], bank.free, tick=o == 2)
                    t = self.copy(self.act, wT[:, f, o0 * P:(o0 + 3) * P], ps[:, bank.at, 0:3 * P], t)
                    bank.free = [t]
                    t_wT.append(t)
            for g in range(4):
                bank = self.banks.next()
                for f in range(FC):
                    t = self.pe.do(lambda e, f=f, g=g, b=bank.at: e.transpose(
                        ps[:, b, f * P:(f + 1) * P], rawo[:, f, 4 * g:4 * g + 4, :].rearrange("p h i -> p (h i)"), self.ident[:, :]),
                        tickets['o'], bank.free, tick=f == 1)
                t = self.copy(self.act, woT[:, g, :], ps[:, bank.at, 0:D], t)
                bank.free = [t]
                t_wo.append(t)
        return load, turn

    def retention(self):
        a, ps = self.a, self.ps
        dk = D // H
        with ExitStack() as mem:
            sb = lambda n, s, dt=F32: self.sb("re_" + n, s, dt, mem)
            wT, woT, t_wT, t_wo = self.re_weights
            v = sb("v", [P, NC, H, 32])
            jobs = []
            attention = self.attend("re", jobs, dk, 1.0, mem, S, softmax=False)
            next(attention)
            decay = sb("decay", [P, H, S])
            lg = sb("lg", [P, 4, H])
            dq, dkk = self.scratch("req", D, T), self.scratch("rek", D, T)
            t_lg = self.arrival("relg").dma(self.sp, lg[:, 0, :], a["L1_attn_log_gamma"].partition_broadcast(P))
            self.norm_x()
            with ExitStack() as tmp:
                tb = lambda n, s, dt=F32: self.sb("ret_" + n, s, dt, tmp)
                dist = tb("dist", [P, S])
                kt = tb("kt", [P, NC, D])
                kst = tb("kst", [P, 4, NC, H])
                ksq = tb("ksq", [P, NC, D])
                t = self.V(lambda e: e.tensor_scalar(lg[:, 1, :], lg[:, 0, :], -1.0, None, ALU.mult), t_lg)
                t = self.V(lambda e: e.tensor_tensor(lg[:, 1, :], lg[:, 1, :], lg[:, 0, :], ALU.min), t)
                t = self.A(lambda e: e.activation(lg[:, 2, :], lg[:, 1, :], ACT.Exp), t)
                t = self.A(lambda e: e.activation(lg[:, 3, :], lg[:, 2, :], ACT.Ln, bias=1.0), t)
                t = self.V(lambda e: e.tensor_scalar(lg[:, 0, :], lg[:, 0, :], 0.0, None, ALU.min), t)
                t_gamma = self.V(lambda e: e.tensor_tensor(lg[:, 0, :], lg[:, 0, :], lg[:, 3, :], ALU.subtract), t)
                t = self.G(lambda e: e.iota(dist[:, :], pattern=[[1, S]], base=0, channel_multiplier=-1, allow_small_or_imprecise_dtypes=True))
                t_di = self.G(lambda e: e.tensor_scalar(dist[:, :], dist[:, :], 0.0, None, ALU.max), t)
                t_v0 = self.G(lambda e: e.memset(v[:, :, :, :], 0.0))
                t_v, t_k = [], []
                for c in range(NC):
                    bank = self.banks.next()
                    t = self.chain(ps[:, bank.at, :], [(self.xnT[:, f, c * P:(c + 1) * P], wT[:, f, D:3 * D]) for f in range(FC)],
                                   bank.free, t_wT, self.xnT_ready)
                    t1 = self.A(lambda e, c=c, b=bank.at: e.activation(kt[:, c, :], ps[:, b, 0:D], ACT.Copy), t)
                    t2 = self.A(lambda e, c=c, b=bank.at: e.activation(
                        v[:, c, :, 0:dk], ps[:, b, D:2 * D].rearrange("p (h i) -> p h i", h=H), ACT.Copy), t, t_v0)
                    bank.free = [t2]
                    t_k.append(t1)
                    t_v.append(t2)
                    for h in (2 * c, 2 * c + 1):
                        t_dc = self.A(lambda e, h=h: e.activation(decay[:, h, :], dist[:, :], ACT.Exp, scale=lg[:, 0, h:h + 1]), t_di, t_gamma)
                t_dec = [self.G(lambda e: e.affine_select(out=decay[:, :, 0:P], in_=decay[:, :, 0:P], compare_op=ALU.is_ge, fill=0.0, base=0,
                                                          pattern=[[0, H], [1, P]], channel_multiplier=-1), t_dc)]
                t_kn = []
                for b in range(B):
                    half = slice(b * SC, (b + 1) * SC)
                    k4 = kt[:, half, :].rearrange("p c (h i) -> p (c h) i", h=H)
                    q4 = ksq[:, half, :].rearrange("p c (h i) -> p (c h) i", h=H)
                    s4 = lambda i, half=half: kst[:, i, half, :].rearrange("p c h -> p (c h)")
                    wide = lambda i, s4=s4: s4(i).unsqueeze(2).broadcast_to([P, SC * H, dk])
                    t = self.V(lambda e, k4=k4, s4=s4: e.tensor_reduce(s4(0), k4, AX.X, ALU.add), t_k[half])
                    t = self.V(lambda e, s4=s4: e.tensor_scalar(s4(0), s4(0), 1.0 / dk, None, ALU.mult), t)
                    t = self.V(lambda e, k4=k4, wide=wide: e.tensor_tensor(k4, k4, wide(0), ALU.subtract), t)
                    t = self.A(lambda e, k4=k4, q4=q4: e.activation(q4, k4, ACT.Square), t)
                    t = self.V(lambda e, q4=q4, s4=s4: e.tensor_reduce(s4(1), q4, AX.X, ALU.add), t)
                    t = self.V(lambda e, s4=s4: e.tensor_scalar(s4(1), s4(1), 1.0 / dk, LN_EPS, ALU.mult, ALU.add), t)
                    t = self.A(lambda e, s4=s4: e.activation(s4(2), s4(1), ACT.Sqrt), t)
                    t = self.V(lambda e, s4=s4: e.reciprocal(s4(3), s4(2)), t)
                    t = self.V(lambda e, k4=k4, wide=wide: e.tensor_tensor(k4, k4, wide(3), ALU.mult), t)
                    t_kn += [t] * SC
                ring = self.parts_out(tmp, "rep", n=8)
                r_q = self.project_parts(ring, wT, FC, lambda f, n: self.xnT[:, f, n * BANK:(n + 1) * BANK], t_wT, None, None, dq, T, D)
                r_k = {}

                def send(f, n, view, t):
                    r_k[f, n], t_read = self.send_parts(ring, view, None, t, dkk, f, n)
                    return t_read
                self.to_features(kt, D, NC, t_kn, send)
                self.flush_parts()
                t_y = []

                def done(job, raw, t_raw, rden, t_rden):
                    b, g = job["b"], job["g"]
                    t_y.append(self.G(lambda e: e.tensor_copy(yT[:, g, b * S:(b + 1) * S], raw[:, :]), t_raw))
                    return t_y[-1]

                for b in range(B):
                    for g in range(4):
                        rows = g * 4 * dk
                        jobs.append(dict(q=(dq, b * S), k=(dkk, b * S), rows=rows, keys=S, mode="causal", b=b, g=g,
                                         v=lambda c, h, b=b, g=g: v[:, b * SC + c, 4 * g + h, :], v_ready=t_v[-1],
                                         decay=lambda jj, n, g=g: decay[:, 4 * g + 2 * jj:4 * g + 2 * jj + 2, 0:n], decay_ready=t_dec,
                                         ready=[r_q[rows // P, b], r_k[rows // P, b]], done=done))
                next(attention)
                next(attention)
                self.fence(*[s.free for s in ring.slots])

            yT = sb("yT", [P, 4, T])
            for _ in attention:
                pass
            final = self.new_x(turn=False)
            gb = self.da_rows
            push, first_norm, _ = self.norm_as_it_comes(self.xn, self.xn, gb[:, 0, :], gb[:, 1, :], self.t_da_rows)
            for c in range(NC):
                bank = self.banks.next()
                t = self.chain(ps[:, bank.at, 0:D], [(yT[:, g, c * P:(c + 1) * P], woT[:, g, :]) for g in range(4)], bank.free, t_y, t_wo)
                t = self.V(lambda e, c=c, b=bank.at: e.tensor_tensor(self.x[:, c, :], self.x[:, c, :], ps[:, b, 0:D], ALU.add), t)
                bank.free = [t]
                final(c, t)
                if c % 4 == 3:
                    for k in range(c - 3, c + 1):
                        push(k, self.normed[0][k])
            self.normed = first_norm, None
            self.fence()

    def affine_copy(self, gain, shift, t_gb, dst):
        def emit(f, n, view, t):
            return self.A(lambda e: e.activation(dst[:, f, n * BANK:(n + 1) * BANK], view, ACT.Identity,
                                                 bias=shift[:, f:f + 1], scale=gain[:, f:f + 1]), t, t_gb)
        return emit

    def context_operands(self, mem):
        a, ps = self.a, self.ps
        HD = H * 32
        names = ["L1_xattn_a2_lny_g", "L1_xattn_a2_lny_b"]
        vecs, t_c = self.col, self.t_col
        ctx = self.sb("co_ctx", [P, MC, CW], F32, mem)
        t_ctx = self.arrival("coctx").dma(self.sp, ctx[:, :, :], a["ctx_512"].rearrange("b (c p) d -> p (b c) d", p=P))
        w = {}
        for n in ("wk", "wv"):
            tile = self.sb("co_" + n, [P, HD], F32, mem)
            w[n] = tile, self.arrival("co" + n).dma(self.sp, tile[:, :].rearrange("p (h d) -> p h d", h=H),
                                                    a["L1_xattn_a2_" + n].rearrange("h p d -> p h d"))
        ring = self.parts_out(mem, "co", shared=False, n=4)
        stage = Ring([(self.sb(f"co_v{i}", [P, HD], F32, mem), self.arrival(f"cov{i}")) for i in range(2)])
        self.ctx_k, self.ctx_v = self.scratch("a2k", HD, TM), self.nc.dram_tensor("scratch_a2v", (TM, HD), F32).ap()

        def steps():
            done = self.normalize(ctx, ctx, MC, [t_ctx] * MC)
            t_T = self.to_features(ctx, CW, MC, done, self.affine_copy(*(vecs[n] for n in names), t_c, self.ctxT[:, :].unsqueeze(1)))
            yield
            self.ctx_v_ready = []
            for c in range(MC):
                if c and c % 2 == 0:
                    yield
                bank, slot = self.banks.next(), stage.next()
                v, arr = slot.at
                t = self.chain(ps[:, bank.at, :], [(self.ctxT[:, c * P:(c + 1) * P], w["wv"][0][:, :])], bank.free, w["wv"][1], t_T)
                t = self.copy(self.act, v[:, :], ps[:, bank.at, :], t, slot.free)
                bank.free = [t]
                t = arr.dma(self.sp, self.ctx_v[c * P:(c + 1) * P, :], v[:, :], t)
                slot.free = [t]
                self.ctx_v_ready.append(t)
            yield
            self.ctx_k_ready = self.project_parts(ring, w["wk"][0][:, :].unsqueeze(1), 1, lambda f, n: self.ctxT[:, n * BANK:(n + 1) * BANK],
                                                  w["wk"][1], t_T, None, self.ctx_k, TM, HD)
            self.flush_parts()
            yield
        return steps()

    def mha(self, pre, xb, xb_ready, cross, next_norm=None):
        a, ps = self.a, self.ps
        A = "L1_xattn_" + pre + "_"
        dh = 32
        HD = H * dh
        ty = TM if cross else T
        ny = ty // P
        with ExitStack() as mem:
            sb = lambda n, s, dt=F32: self.sb(pre + n, s, dt, mem)
            vecs, t_c = self.col, self.t_col
            rows = sb("rows", [P, 2, D])
            ar = self.arrival(pre + "rows")
            for i, n in enumerate(("li1_b", "li3_b")):
                t_rows = ar.dma(self.sp, rows[:, i, :], a[A + n].partition_broadcast(P))
            li1 = sb("li1", [P, HD // P, D])
            t_li1 = self.arrival(pre + "li1").dma(self.sp, li1[:, :, :], a[A + "li1_w"].rearrange("(f p) n -> p f n", p=P))
            core = self.ctxT[:, :].rearrange("p (c d) -> p c d", c=NC)
            y = sb("y", [P, NC, D])

            affine = lambda g, b, dst: self.affine_copy(vecs[A + g], vecs[A + b], t_c, dst)
            with ExitStack() as att:
                ab = lambda n, s, dt=F32: self.sb(pre + n, s, dt, att)
                v = ab("v", [P, ny, HD])
                jobs = []
                attention = self.attend(pre, jobs, dh, dh ** -0.5, att, ty // B, nbuf=3)
                next(attention)
                dq, dk = self.scratch(pre + "q", HD, T), self.ctx_k if cross else self.scratch(pre + "k", HD, ty)
                with ExitStack() as tmp:
                    tb = lambda n, s, dt=F32: self.sb(pre + n, s, dt, tmp)
                    w, tw = {}, {}
                    for n in ("wq",) if cross else ("wq", "wk", "wv"):
                        w[n] = tb(n, [P, FC, HD])
                        arr = self.arrival(pre + n)
                        for f in range(FC):
                            tw[n] = arr.dma(self.sp, w[n][:, f, :].rearrange("p (h d) -> p h d", h=H),
                                            a[A + n][:, f * P:(f + 1) * P, :].rearrange("h p d -> p h d"))
                    ring = self.parts_out(tmp, pre + "p", n=6)
                    done = self.normalize(xb, core, NC, xb_ready)
                    xcols = lambda f, n: self.xnT[:, f, n * BANK:(n + 1) * BANK]
                    if cross:
                        t_x = self.to_features(core, D, NC, done, affine("lnx_g", "lnx_b", self.xnT))
                        r_k = self.ctx_k_ready
                        arr = self.arrival(pre + "v")
                        t_v = [arr.dma(self.sp, v[:, c:c + 4, :], self.ctx_v[c * P:(c + 4) * P, :].rearrange("(c p) n -> p c n", p=P), self.ctx_v_ready)
                               for c in range(0, MC, 4)]
                    else:
                        yT = tb("ynT", [P, FC, T])

                        def both(f, n, view, t):
                            affine("lnx_g", "lnx_b", self.xnT)(f, n, view, t)
                            return affine("lny_g", "lny_b", yT)(f, n, view, t)
                        t_x = self.to_features(core, D, NC, done, both)
                        r_k = self.project_parts(ring, w["wk"], FC, lambda f, n: yT[:, f, n * BANK:(n + 1) * BANK], tw["wk"], t_x, None, dk, T, HD)
                        t_v = []
                    r_q = self.project_parts(ring, w["wq"], FC, xcols, tw["wq"], t_x, None, dq, T, HD)
                    self.flush_parts()
                    t_o = []

                    def settled(job, raw, t_raw, rden, t_rden):
                        b, g = job["b"], job["g"]
                        t_o.append(self.V(lambda e: e.tensor_tensor(oT[:, g, b * S:(b + 1) * S], raw[:, :], rden, ALU.mult), t_rden))
                        return t_o[-1]
                    for b in range(B):
                        for g in range(4):
                            kn = [2 * b, 2 * b + 1] if cross else [b]
                            jobs.append(dict(q=(dq, b * S), k=(dk, b * (ty // B)), rows=g * P, keys=ty // B, mode="full" if cross else "upper",
                                             b=b, g=g, v=lambda c, h, b=b, g=g: v[:, b * (ny // B) + c, (4 * g + h) * dh:(4 * g + h + 1) * dh],
                                             v_ready=t_v, ready=[r_q[g, b]] + [r_k[g, n] for n in kn], done=settled))
                    next(attention)
                    for c in range(0 if cross else NC):
                        bank = self.banks.next()
                        t = self.chain(ps[:, bank.at, :], [(yT[:, f, c * P:(c + 1) * P], w["wv"][:, f, :]) for f in range(FC)], bank.free, tw["wv"], t_x)
                        t = self.copy(self.act, v[:, c, :], ps[:, bank.at, :], t)
                        bank.free = [t]
                        t_v.append(t)
                    for c in range(NC):
                        t_yb = self.G(lambda e, c=c: e.tensor_tensor(y[:, c, :], xb[:, c, :], rows[:, 0, :], ALU.add), xb_ready[c], t_rows)
                    next(attention)
                    self.fence(*[s.free for s in ring.slots])
                oT = ab("oT", [P, 4, T])
                for _ in attention:
                    pass
                push, done, t_m = self.norm_as_it_comes(y, core, emit=affine("ln3_g", "ln3_b", self.xnT))
                for c in range(NC):
                    bank = self.banks.next()
                    t = self.chain(ps[:, bank.at, 0:D], [(oT[:, g, c * P:(c + 1) * P], li1[:, g, :]) for g in range(4)], bank.free, t_o, t_li1)
                    t = self.V(lambda e, c=c, b=bank.at: e.tensor_tensor(y[:, c, :], y[:, c, :], ps[:, b, 0:D], ALU.add), t, t_yb)
                    bank.free = [t]
                    push(c, t)
                self.fence()
            li2, li3 = sb("li2", [P, FC, HID]), sb("li3", [P, HC, D])
            t_li2 = self.arrival(pre + "li2").dma(self.sp, li2[:, :, :], a[A + "li2_w"].rearrange("(f p) n -> p f n", p=P))
            t_li3 = self.arrival(pre + "li3").dma(self.sp, li3[:, :, :], a[A + "li3_w"].rearrange("(f p) n -> p f n", p=P))
            hT = sb("hT", [P, HC, T])
            for c in range(NC):
                t_1 = self.G(lambda e, c=c: e.tensor_tensor(y[:, c, :], y[:, c, :], xb[:, c, :], ALU.add), done[c])
                t_1 = self.G(lambda e, c=c: e.tensor_tensor(y[:, c, :], y[:, c, :], rows[:, 1, :], ALU.add), t_1)
                if cross:
                    t_1 = self.G(lambda e, c=c: e.tensor_tensor(y[:, c, :], y[:, c, :], self.x[:, c, :], ALU.add), t_1)
            t_h = []
            for n in range(T // BANK):
                for m in range(HC):
                    bank = self.banks.next()
                    t = self.chain(ps[:, bank.at, :], [(li2[:, f, m * P:(m + 1) * P], self.xnT[:, f, n * BANK:(n + 1) * BANK]) for f in range(FC)],
                                   bank.free, t_li2, t_m)
                    t = self.A(lambda e, m=m, n=n, b=bank.at: e.activation(hT[:, m, n * BANK:(n + 1) * BANK], ps[:, b, :], ACT.Gelu,
                                                                          bias=vecs[A + "li2_b"][:, m:m + 1]), t, t_c)
                    bank.free = [t]
                t_h.append(t)
            if cross:
                new, final, out = self.x, self.new_x(), None
            else:
                new = xb
                final, out, _ = self.norm_as_it_comes(xb, xb, *next_norm)
            for c in range(NC):
                bank = self.banks.next()
                t = self.chain(ps[:, bank.at, 0:D], [(hT[:, m, c * P:(c + 1) * P], li3[:, m, :]) for m in range(HC)], bank.free, t_h[c // SC], t_li3)
                t = self.V(lambda e, c=c, b=bank.at: e.tensor_tensor(new[:, c, :], y[:, c, :], ps[:, b, 0:D], ALU.add), t, t_1)
                bank.free = [t]
                final(c, t)
            self.fence()
        return out

    def double_attention(self):
        gb, t_gb, xb = self.da_rows, self.t_da_rows, self.xn
        done = self.normed[0]
        done = self.mha("a1", xb, done, False, (gb[:, 2, :], gb[:, 3, :], t_gb))
        self.mha("a2", xb, done, True)
        self.fence()

    def swiglu(self):
        a, ps = self.a, self.ps
        NT = NC + E1 - 1
        with ExitStack() as mem:
            sb = lambda n, s, dt=F32: self.sb("sw_" + n, s, dt, mem)
            wr, t_wr = self.wr["L1_ffn_w_router"]
            zero = sb("zero", [P, D])
            t_zero = self.G(lambda e: e.memset(zero[:, :], 0.0))
            xg = self.nc.dram_tensor("scratch_swx", (NT * P, D), F32).ap()
            yo = self.nc.dram_tensor("scratch_swy", (NT * P, D), F32).ap()
            t_z = self.arrival("swz").dma(self.sp, xg.rearrange("(i p) d -> p i d", p=P),
                                          zero[:, :].unsqueeze(1).broadcast_to([P, NT, D]), t_zero)
            wv = sb("wv", [P, E1, FC, 2 * HID])
            wp = sb("wp", [P, E1, HC, D])
            t_w = []
            for x in range(E1):
                t_w.append(self.arrival(f"sww{x}").dma(self.sp, wv[:, x, :, :], a["L1_ffn_w_v"][x].rearrange("(f p) n -> p f n", p=P)))
            iota_e = sb("iota_e", [P, E1])
            t_i = self.G(lambda e: e.iota(iota_e[:, :], pattern=[[1, E1]], base=0, channel_multiplier=0, allow_small_or_imprecise_dtypes=True))
            full = sb("full", [P, NC])
            t_i = self.G(lambda e: e.iota(full[:, :], pattern=[[P, NC]], base=0, channel_multiplier=0, allow_small_or_imprecise_dtypes=True))
            tile_no = sb("tile_no", [1, NT])
            t_i = self.G(lambda e: e.iota(tile_no[:, :], pattern=[[1, NT]], base=0, channel_multiplier=0, allow_small_or_imprecise_dtypes=True))
            before = sb("before", [P, P])
            t_b = self.G(lambda e: e.memset(before[:, :], 1.0))
            t_b = self.G(lambda e: e.affine_select(out=before[:, :], in_=before[:, :], compare_op=ALU.is_gt, fill=0.0, base=0,
                                                   pattern=[[1, P]], channel_multiplier=-1), t_b)
            self.norm_x()
            top, who, t = self.route(mem, "swr", wr, E1, None, t_wr)
            pick = sb("pick", [P, NC, E1])
            t_pick = self.V(lambda e: e.tensor_tensor(pick[:, :, :], iota_e[:, :].unsqueeze(1).broadcast_to([P, NC, E1]),
                                                      who[:, :, 0:1].broadcast_to([P, NC, E1]), ALU.is_equal), t, t_i)
            bank = self.banks.next()
            flat = pick[:, :, :].rearrange("p c e -> p (c e)")
            self.pe.wait(bank.free, t_pick, t_b, self.t_ones)
            for back in range(NC):
                self.pe.do(lambda e, back=back, b=bank.at: e.matmul(
                    ps[:, b, back * E1:NC * E1], (self.ones if back else before)[:, :], flat[:, 0:(NC - back) * E1],
                    start=back == 0, stop=back == NC - 1), tick=False)
            t = self.chain(ps[:, bank.at, NC * E1:(NC + 1) * E1], [(self.ones[:, :], pick[:, c, :]) for c in range(NC)])
            place = sb("place", [P, NC + 1, E1])
            t = self.V(lambda e, b=bank.at: e.tensor_copy(place[:, :, :].rearrange("p c e -> p (c e)"), ps[:, b, 0:(NC + 1) * E1]), t)
            bank.free = [t]
            some = sb("some", [P, E1, NC])
            ends = sb("ends", [P, 2, E1])
            t = self.V(lambda e: e.tensor_tensor(some[:, :, :], full[:, :].unsqueeze(1).broadcast_to([P, E1, NC]),
                                                 place[:, NC, :].unsqueeze(2).broadcast_to([P, E1, NC]), ALU.is_lt), t, t_i)
            t = self.V(lambda e: e.tensor_reduce(ends[:, 0, :], some[:, :, :], AX.X, ALU.add), t)
            t = self.V(lambda e: e.tensor_copy(ends[:, 1, :], ends[:, 0, :]), t)
            for x in range(1, E1):
                t = self.V(lambda e, x=x: e.tensor_tensor(ends[:, 1, x:x + 1], ends[:, 1, x:x + 1], ends[:, 1, x - 1:x], ALU.add), t)
            t_ends = t
            slot = sb("slot", [P, NC])
            to = sb("to", [P, NC], U32)
            t = self.V(lambda e: e.tensor_tensor(ends[:, 0, :], ends[:, 1, :], ends[:, 0, :], ALU.subtract), t_ends)
            t = self.V(lambda e: e.scalar_tensor_tensor(place[:, 0:NC, :], ends[:, 0, :].unsqueeze(1).broadcast_to([P, NC, E1]), float(P),
                                                        place[:, 0:NC, :], ALU.mult, ALU.add), t)
            t = self.V(lambda e: e.tensor_tensor(place[:, 0:NC, :], place[:, 0:NC, :], pick[:, :, :], ALU.mult), t)
            t = self.V(lambda e: e.tensor_reduce(slot[:, :], place[:, 0:NC, :], AX.X, ALU.add), t)
            t_to = self.V(lambda e: e.tensor_copy(to[:, :], slot[:, :]), t)
            past = sb("past", [1, NT, E1 - 1])
            owner = sb("owner", [1, NT])
            owner_i = sb("owner_i", [1, NT], I32)
            t = self.V(lambda e: e.tensor_tensor(past[:, :, :], tile_no[:, :].unsqueeze(2).broadcast_to([1, NT, E1 - 1]),
                                                 ends[0:1, 1, 0:E1 - 1].unsqueeze(1).broadcast_to([1, NT, E1 - 1]), ALU.is_ge), t_ends)
            t = self.V(lambda e: e.tensor_reduce(owner[:, :], past[:, :, :], AX.X, ALU.add), t)
            t_owner = self.V(lambda e: e.tensor_copy(owner_i[:, :], owner[:, :]), t)
            sc = self.arrival("swsc")
            self.pool.wait(t_to, t_z, self.xn_ready)
            for c in range(NC):
                sc.count += 16
                self.pool.items.append(lambda e, c=c: e.indirect_dma_start(
                    xg, bass.IndirectOffsetOnAxis(ap=to[:, c:c + 1], axis=0), self.xn[:, c, :], None).then_inc(sc.sem, 16))
            t_sc = (sc.sem, sc.count)
            xs = sb("xs", [P, NT, D])
            xgT = sb("xgT", [P, NT, D])
            t_xs = []
            for i in range(NT):
                if i % 3 == 0:
                    n = min(3, NT - i)
                    t = self.arrival(f"swxs{i}").dma(self.sp, xs[:, i:i + n, :], xg[i * P:(i + n) * P, :].rearrange("(r p) d -> p r d", p=P), t_sc)
                t_xs.append(t)
            t_wp = [self.arrival(f"swp{x}").dma(self.sp, wp[:, x, :, :], a["L1_ffn_w_proj"][x].rearrange("(f p) n -> p f n", p=P)) for x in range(E1)]
            hs = Ring([sb(f"h{i}", [P, HID]) for i in range(2)])
            hTs = Ring([sb(f"hT{i}", [P, HID]) for i in range(2)])
            gates = Ring([sb(f"gt{i}", [P, BANK]) for i in range(2)])
            os_ = Ring([(sb(f"o{i}", [P, D]), self.arrival(f"swo{i}")) for i in range(2)])
            expert = {}
            t_T, t_h, t_done = {}, {}, []

            def turn(i):
                bank = self.banks.next()
                for f in range(FC):
                    t = self.pe.do(lambda e, f=f, i=i, b=bank.at: e.transpose(
                        ps[:, b, f * P:(f + 1) * P], xs[:, i, f * P:(f + 1) * P], self.ident[:, :]), t_xs[i], bank.free, tick=f == FC - 1)
                t_T[i] = self.copy(self.act, xgT[:, i, :], ps[:, bank.at, 0:D], t)
                bank.free = [t_T[i]]

            def up(i):
                self.pe.wait(t_owner)
                self.pe.items.append(lambda e: expert.update({i: e.value_load(owner_i[0:1, i:i + 1], min_val=0, max_val=E1 - 1)}))
                h = hs.next()
                for n in range(HID // BANK):
                    gate, val = self.banks.next(), self.banks.next()
                    for bank, off in ((gate, n * BANK), (val, HID + n * BANK)):
                        self.pe.wait(bank.free, t_w, t_T[i])
                        for f in range(FC):
                            t = self.pe.do(lambda e, f=f, off=off, b=bank.at: e.matmul(
                                ps[:, b, :], xgT[:, i, f * P:(f + 1) * P],
                                wv[:, bass.ds(expert[i], 1), f, off:off + BANK].rearrange("p o n -> p (o n)"), start=f == 0, stop=f == FC - 1),
                                tick=f == FC - 1)
                        if bank is gate:
                            g = gates.next()
                            t_g = self.A(lambda e, g=g, b=bank.at: e.activation(g.at[:, :], ps[:, b, :], ACT.Silu), t, g.free)
                            gate.free = [t_g]
                    t1 = self.V(lambda e, g=g, n=n, b=val.at: e.tensor_tensor(
                        h.at[:, n * BANK:(n + 1) * BANK], g.at[:, :], ps[:, b, :], ALU.mult), t, t_g, h.free)
                    val.free, g.free = [t1], [t1]
                    t_h[i, n] = t1
                t_h[i] = h

            def down(i):
                h, hT = t_h[i], hTs.next()
                t_hT = []
                for n in range(HID // BANK):
                    bank = self.banks.next()
                    for k in range(4):
                        t = self.pe.do(lambda e, k=k, n=n, b=bank.at: e.transpose(
                            ps[:, b, k * P:(k + 1) * P], h.at[:, (4 * n + k) * P:(4 * n + k + 1) * P], self.ident[:, :]),
                            t_h[i, n], bank.free, tick=k == 3)
                    t1 = self.copy(self.act if n else self.dve, hT.at[:, n * BANK:(n + 1) * BANK], ps[:, bank.at, :], t, hT.free)
                    bank.free = [t1]
                    t_hT.append(t1)
                h.free = [t]
                return hT, t_hT

            def project(i, hT, t_hT):
                bank = self.banks.next()
                self.pe.wait(bank.free, t_wp)
                for m in range(HC):
                    t = self.pe.do(lambda e, m=m, b=bank.at: e.matmul(
                        ps[:, b, 0:D], hT.at[:, m * P:(m + 1) * P],
                        wp[:, bass.ds(expert[i], 1), m, :].rearrange("p o n -> p (o n)"), start=m == 0, stop=m == HC - 1),
                        t_hT[m // 4], tick=m == HC - 1)
                hT.free = [t]
                o = os_.next()
                ot, oarr = o.at
                t1 = self.V(lambda e, b=bank.at, ot=ot: e.tensor_copy(ot[:, :], ps[:, b, 0:D]), t, o.free)
                bank.free = [t1]
                t2 = oarr.dma(self.sp, yo[i * P:(i + 1) * P, :], ot[:, :], t1)
                o.free = [t2]
                t_done.append(t2)

            turn(0)
            turned = None
            for i in range(NT):
                if i + 1 < NT:
                    turn(i + 1)
                if i:
                    turned = down(i - 1)
                up(i)
                if i:
                    project(i - 1, *turned)
            project(NT - 1, *down(NT - 1))
            gb = Ring([(sb(f"g{i}", [P, D]), self.arrival(f"swga{i}")) for i in range(NC)])
            self.pool.wait(t_done)
            ready = []
            for c in range(NC):
                gt, arr = gb.next().at
                arr.count += 16
                self.pool.items.append(lambda e, c=c, gt=gt, arr=arr: e.indirect_dma_start(
                    gt[:, :], None, yo, bass.IndirectOffsetOnAxis(ap=to[:, c:c + 1], axis=0)).then_inc(arr.sem, 16))
                ready.append(self.V(lambda e, c=c, gt=gt: e.tensor_tensor(self.x[:, c, :], self.x[:, c, :], gt[:, :], ALU.add),
                                    (arr.sem, arr.count), self.x_ready[c]))
            self.x_ready = ready


def build(nc, names, aps, out):
    with ExitStack() as ctx:
        p = Program(nc, ctx, dict(zip(names, aps)), out)
        block = ctx.enter_context(nc.Block())

        @block.sync
        def _(e):
            for f in p.sp.items:
                f(e)

        @block.tensor
        def _(e):
            for f in p.pe.items:
                f(e)

        @block.scalar
        def _(e):
            for f in p.act.items:
                f(e)

        @block.vector
        def _(e):
            for f in p.dve.items:
                f(e)

        @block.gpsimd
        def _(e):
            for f in p.pool.items:
                f(e)


NAMES = ["x", "ctx_512"] + ["L0_attn_" + n for n in ("Wq", "Wk", "Wv", "Wo", "bo", "P")] \
    + ["L0_xattn_" + n for n in ("Wk", "bk", "Wq", "bq", "Wv", "bv", "Wck", "bck", "Wcq", "bcq", "Wcv", "bcv", "Wp", "bp")] \
    + ["L0_ffn_" + n for n in ("Wr", "br", "W1", "b1", "W2", "b2")] \
    + ["L1_attn_" + n for n in ("W_qkv", "W_o", "log_gamma")] \
    + ["L1_xattn_" + n for n in ("ln1_g", "ln1_b", "ln2_g", "ln2_b")] \
    + [f"L1_xattn_{a}_{n}" for a in ("a1", "a2") for n in (
        "wq", "wk", "wv", "li1_w", "li1_b", "lnx_g", "lnx_b", "lny_g", "lny_b", "ln3_g", "ln3_b",
        "li2_w", "li2_b", "li3_w", "li3_b")] \
    + ["L1_ffn_" + n for n in ("w_router", "w_v", "w_proj")]

def kernel(**inputs):
    import concourse.bacc as bacc
    from concourse.bass_utils import run_bass_kernel_spmd as run

    nc = bacc.Bacc("TRN2", target_bir_lowering=False, num_devices=1)
    arrays, aps = {}, []
    for name in NAMES:
        v = np.ascontiguousarray(inputs[name])
        arrays["in_" + name] = v
        aps.append(nc.dram_tensor("in_" + name, v.shape, mybir.dt.from_np(v.dtype), kind="ExternalInput").ap())
    out = nc.dram_tensor("out_0", (B, S, D), F32, kind="ExternalOutput").ap()
    build(nc, NAMES, aps, out)
    r = run(nc, [arrays], core_ids=[0])
    return np.asarray(r.results[0]["out_0"])
```
